# Optimizing a Trainium2 kernel written in Bass

```python
import numpy as np
import jax
import jax.numpy as jnp

def _softmax(x, axis=-1):
    return jax.nn.softmax(x, axis=axis)

def _gelu(x):
    return jax.nn.gelu(x, approximate=True)

def _silu(x):
    return jax.nn.silu(x)

def _sigmoid(x):
    return jax.nn.sigmoid(x)

def _layernorm(x, axis=-1, eps=1e-05):
    m = jnp.mean(x, axis=axis, keepdims=True)
    v = jnp.var(x, axis=axis, keepdims=True)
    return (x - m) / jnp.sqrt(v + eps)

def _scatter_add(tgt, idx, src, axis=0):
    return tgt.at[idx].add(src)

def _segment_sum(src, seg, n):
    return jax.ops.segment_sum(src, seg, n)
kernel_name = 'mk_gnn_preln_d4_gnn_r16_37f8c3'

def setup_inputs(seed: int=0):
    np.random.seed(seed)
    _w = jnp.asarray

    def _rec_inputs():
        import jax
        import jax.numpy as jnp
        _gk = jax.random.key(seed)
        x = -0.0002928 + 1 * jax.random.normal(jax.random.fold_in(_gk, 1), (3125, 64), jnp.float32)
        _s = jax.random.randint(jax.random.fold_in(_gk, 2), (50000,), 0, 3125, jnp.int32)
        _d = jax.random.randint(jax.random.fold_in(_gk, 3), (50000,), 0, 3125, jnp.int32)
        _loop = jnp.arange(3125, dtype=jnp.int32)
        src = jnp.concatenate([_s, _d, _loop])
        dst = jnp.concatenate([_d, _s, _loop])
        _o = jnp.argsort(dst, stable=True)
        src = src[_o]
        dst = dst[_o]
        edge_attr_32 = 0.000189758 + 1.00013 * jax.random.normal(jax.random.fold_in(_gk, 12), (103125, 32), jnp.float32)
        edge_attr_64 = -8.16379e-05 + 0.999858 * jax.random.normal(jax.random.fold_in(_gk, 13), (103125, 64), jnp.float32)
        edge_weight = jax.random.uniform(jax.random.fold_in(_gk, 15), (103125,), jnp.float32, 0.0, 0.999999)
        edge_weight_n2 = jax.random.uniform(jax.random.fold_in(_gk, 16), (103125,), jnp.float32, 0.0, 0.999999)
        return (x, src, dst, edge_attr_32, edge_attr_64, edge_weight, edge_weight_n2)
    x, src, dst, edge_attr_32, edge_attr_64, edge_weight, edge_weight_n2 = _rec_inputs()

    def _L0_gnn_setup():
        import jax, jax.numpy as jnp
        import numpy as np
        N, E, D_IN, D_OUT = (4096, 65536, 64, 64)
        EPS = 1e-08
        key = jax.random.key(seed)
        ks = jax.random.split(key, 8)
        h = jax.random.normal(ks[0], (N, D_IN), dtype=jnp.float32)
        edge_index = jax.random.randint(ks[1], (2, E), 0, N, dtype=jnp.int64 if jax.config.jax_enable_x64 else jnp.int32)
        adj_v = jax.random.uniform(ks[2], (E,), dtype=jnp.float32)
        deg_v = jax.random.uniform(ks[3], (E,), dtype=jnp.float32)
        W = jax.random.normal(ks[4], (D_IN, D_OUT), dtype=jnp.float32) / np.sqrt(D_IN)
        b = jax.random.normal(ks[5], (D_OUT,), dtype=jnp.float32) * 0.01
        deg_coeff = jnp.array([0.5, 0.0], dtype=jnp.float32)
        coeff_param = jnp.zeros((3,), dtype=jnp.float32)
        scale_param = 2.0 * jnp.ones((1,), dtype=jnp.float32)
        return {'h': h, 'edge_index': edge_index, 'adj_v': adj_v, 'deg_v': deg_v, 'W': W, 'b': b, 'deg_coeff': deg_coeff, 'coeff_param': coeff_param, 'scale_param': scale_param}
    _L0_gnn_all = _L0_gnn_setup()
    _L0_gnn_in = {k: v for k, v in _L0_gnn_all.items() if k in ('W', 'b', 'deg_coeff', 'coeff_param', 'scale_param')}
    del _L0_gnn_all

    def _L1_gnn_setup():
        import jax, jax.numpy as jnp
        import numpy as np
        N, E, D, ED = (6250, 100000, 64, 32)
        LN_EPS = 1e-05
        NEG_SLOPE = 0.2
        key = jax.random.key(seed)
        ks = jax.random.split(key, 12)
        return {'x': jax.random.normal(ks[0], (N, D), jnp.float32), 'edge_index': jax.random.randint(ks[1], (2, E), 0, N, dtype=jnp.int64), 'edge_attr': jax.random.normal(ks[2], (E, ED), jnp.float32), 'We': jax.random.normal(ks[3], (ED, D), jnp.float32) / np.sqrt(ED), 'be': jnp.zeros((D,), jnp.float32), 'W1': jax.random.normal(ks[4], (D, D), jnp.float32) / np.sqrt(D), 'b1': jnp.zeros((D,), jnp.float32), 'W2': jax.random.normal(ks[5], (D, D), jnp.float32) / np.sqrt(D), 'b2': jnp.zeros((D,), jnp.float32), 'eps_gin': jnp.zeros((), jnp.float32), 'gamma': jnp.ones((D,), jnp.float32), 'beta': jnp.zeros((D,), jnp.float32)}
    _L1_gnn_all = _L1_gnn_setup()
    _L1_gnn_in = {k: v for k, v in _L1_gnn_all.items() if k in ('We', 'be', 'W1', 'b1', 'W2', 'b2', 'eps_gin', 'gamma', 'beta')}
    del _L1_gnn_all

    def _L2_gnn_setup():
        import jax, jax.numpy as jnp
        import numpy as np
        N_NODES = 6250
        N_EDGES = 100000
        D_NODE = 64
        D_EDGE = 64
        D_MSG = 64
        D_OUT = 64
        NEG_SLOPE = 0.01
        LN_EPS = 1e-05

        def _layer_norm(x, w, b):
            mu = jnp.mean(x, axis=-1, keepdims=True)
            var = jnp.mean(jnp.square(x - mu), axis=-1, keepdims=True)
            return (x - mu) * jax.lax.rsqrt(var + LN_EPS) * w + b

        def _mlp(x, ln_w, ln_b, W, b):
            h = _layer_norm(x, ln_w, ln_b)
            h = h @ W.T + b
            return jax.nn.leaky_relu(h, NEG_SLOPE)
        key = jax.random.key(seed)
        ks = jax.random.split(key, 12)
        half = D_MSG // 2
        inp = {'node_z': jax.random.normal(ks[0], (N_NODES, D_NODE), jnp.float32), 'edge_z': jax.random.normal(ks[1], (N_EDGES, D_EDGE), jnp.float32), 'src': jax.random.randint(ks[2], (N_EDGES,), 0, N_NODES, jnp.int32), 'dst': jax.random.randint(ks[3], (N_EDGES,), 0, N_NODES, jnp.int32), 'node_ln_w': jnp.ones((D_NODE,), jnp.float32), 'node_ln_b': jnp.zeros((D_NODE,), jnp.float32), 'node_W': jax.random.normal(ks[4], (half, D_NODE), jnp.float32) / np.sqrt(D_NODE), 'node_b': jnp.zeros((half,), jnp.float32), 'edge_ln_w': jnp.ones((D_EDGE,), jnp.float32), 'edge_ln_b': jnp.zeros((D_EDGE,), jnp.float32), 'edge_W': jax.random.normal(ks[5], (half, D_EDGE), jnp.float32) / np.sqrt(D_EDGE), 'edge_b': jnp.zeros((half,), jnp.float32), 'red_ln_w': jnp.ones((D_MSG,), jnp.float32), 'red_ln_b': jnp.zeros((D_MSG,), jnp.float32), 'red_W': jax.random.normal(ks[6], (D_OUT, D_MSG), jnp.float32) / np.sqrt(D_MSG), 'red_b': jnp.zeros((D_OUT,), jnp.float32)}
        return inp
    _L2_gnn_all = _L2_gnn_setup()
    _L2_gnn_in = {k: v for k, v in _L2_gnn_all.items() if k in ('node_ln_w', 'node_ln_b', 'node_W', 'node_b', 'edge_ln_w', 'edge_ln_b', 'edge_W', 'edge_b', 'red_ln_w', 'red_ln_b', 'red_W', 'red_b')}
    del _L2_gnn_all

    def _L3_gnn_setup():
        import jax, jax.numpy as jnp
        import numpy as np
        N = 3125
        E = 50000
        H = 6
        F_IN = 64
        F_OUT = 64
        NEG_SLOPE = 0.2
        key = jax.random.key(seed)
        k1, k2, k3, k4, k5 = jax.random.split(key, 5)
        x = jax.random.normal(k1, (N, F_IN), jnp.float32)
        edge_idx = jax.random.randint(k2, (2, E), 0, N, dtype=jnp.int64)
        scale = 1.0 / np.sqrt(F_IN)
        W_l = jax.random.normal(k3, (F_IN, H * F_OUT), jnp.float32) * scale
        W_r = jax.random.normal(k4, (F_IN, H * F_OUT), jnp.float32) * scale
        att = jax.random.normal(k5, (H, F_OUT), jnp.float32) * scale
        bias = jnp.zeros((F_OUT,), jnp.float32)
        return {'x': x, 'edge_idx': edge_idx, 'W_l': W_l, 'W_r': W_r, 'att': att, 'bias': bias}
    _L3_gnn_all = _L3_gnn_setup()
    _L3_gnn_in = {k: v for k, v in _L3_gnn_all.items() if k in ('W_l', 'W_r', 'att', 'bias')}
    del _L3_gnn_all
    return {'x': x, 'src': src, 'dst': dst, 'edge_attr_32': edge_attr_32, 'edge_attr_64': edge_attr_64, 'edge_weight': edge_weight, 'edge_weight_n2': edge_weight_n2, 'L0_gnn_W': _L0_gnn_in['W'], 'L0_gnn_b': _L0_gnn_in['b'], 'L0_gnn_deg_coeff': _L0_gnn_in['deg_coeff'], 'L0_gnn_coeff_param': _L0_gnn_in['coeff_param'], 'L0_gnn_scale_param': _L0_gnn_in['scale_param'], 'L1_gnn_We': _L1_gnn_in['We'], 'L1_gnn_be': _L1_gnn_in['be'], 'L1_gnn_W1': _L1_gnn_in['W1'], 'L1_gnn_b1': _L1_gnn_in['b1'], 'L1_gnn_W2': _L1_gnn_in['W2'], 'L1_gnn_b2': _L1_gnn_in['b2'], 'L1_gnn_eps_gin': _L1_gnn_in['eps_gin'], 'L1_gnn_gamma': _L1_gnn_in['gamma'], 'L1_gnn_beta': _L1_gnn_in['beta'], 'L2_gnn_node_ln_w': _L2_gnn_in['node_ln_w'], 'L2_gnn_node_ln_b': _L2_gnn_in['node_ln_b'], 'L2_gnn_node_W': _L2_gnn_in['node_W'], 'L2_gnn_node_b': _L2_gnn_in['node_b'], 'L2_gnn_edge_ln_w': _L2_gnn_in['edge_ln_w'], 'L2_gnn_edge_ln_b': _L2_gnn_in['edge_ln_b'], 'L2_gnn_edge_W': _L2_gnn_in['edge_W'], 'L2_gnn_edge_b': _L2_gnn_in['edge_b'], 'L2_gnn_red_ln_w': _L2_gnn_in['red_ln_w'], 'L2_gnn_red_ln_b': _L2_gnn_in['red_ln_b'], 'L2_gnn_red_W': _L2_gnn_in['red_W'], 'L2_gnn_red_b': _L2_gnn_in['red_b'], 'L3_gnn_W_l': _L3_gnn_in['W_l'], 'L3_gnn_W_r': _L3_gnn_in['W_r'], 'L3_gnn_att': _L3_gnn_in['att'], 'L3_gnn_bias': _L3_gnn_in['bias']}

def reference(x, src, dst, edge_attr_32, edge_attr_64, edge_weight, edge_weight_n2, L0_gnn_W, L0_gnn_b, L0_gnn_deg_coeff, L0_gnn_coeff_param, L0_gnn_scale_param, L1_gnn_We, L1_gnn_be, L1_gnn_W1, L1_gnn_b1, L1_gnn_W2, L1_gnn_b2, L1_gnn_eps_gin, L1_gnn_gamma, L1_gnn_beta, L2_gnn_node_ln_w, L2_gnn_node_ln_b, L2_gnn_node_W, L2_gnn_node_b, L2_gnn_edge_ln_w, L2_gnn_edge_ln_b, L2_gnn_edge_W, L2_gnn_edge_b, L2_gnn_red_ln_w, L2_gnn_red_ln_b, L2_gnn_red_W, L2_gnn_red_b, L3_gnn_W_l, L3_gnn_W_r, L3_gnn_att, L3_gnn_bias):
    import jax
    import jax.numpy as jnp

    def _L0_gnn_ref(h, edge_index, adj_v, deg_v, W, b, deg_coeff, coeff_param, scale_param):
        import jax, jax.numpy as jnp
        import numpy as np
        N, E, D_IN, D_OUT = (4096, 65536, 64, 64)
        EPS = 1e-08
        n_nodes = h.shape[0]
        Wh = h @ W + b
        row, col = (edge_index[0], edge_index[1])
        sc = jax.nn.softplus(deg_coeff[0] * deg_v + deg_coeff[1])
        Wr = Wh[row]
        Wc = Wh[col]
        dot = jnp.sum(Wr * Wc, axis=-1)
        nr = jnp.sqrt(jnp.sum(Wr * Wr, axis=-1))
        nc = jnp.sqrt(jnp.sum(Wc * Wc, axis=-1))
        sim = dot / jnp.maximum(nr * nc, EPS)
        sim_pos = jax.nn.relu(sim)
        sim_neg = -jax.nn.relu(-sim)
        no_diag = (row != col).astype(Wh.dtype)
        base = adj_v * sc * no_diag
        prop_pos = jax.ops.segment_sum((base * sim_pos)[:, None] * Wc, row, num_segments=n_nodes)
        prop_neg = jax.ops.segment_sum((base * sim_neg)[:, None] * Wc, row, num_segments=n_nodes)
        coeff = jax.nn.softmax(coeff_param)
        scale = jax.nn.softplus(scale_param)
        return scale * (coeff[0] * prop_pos + coeff[1] * prop_neg + coeff[2] * Wh)

    def _L1_gnn_ref(x, edge_index, edge_attr, We, be, W1, b1, W2, b2, eps_gin, gamma, beta):
        import jax, jax.numpy as jnp
        import numpy as np
        N, E, D, ED = (6250, 100000, 64, 32)
        LN_EPS = 1e-05
        NEG_SLOPE = 0.2
        src, dst = (edge_index[0], edge_index[1])
        msg = jax.nn.relu(x[src] + edge_attr @ We + be)
        aggr = jax.ops.segment_sum(msg, dst, num_segments=x.shape[0])
        h = (1.0 + eps_gin) * x + aggr
        h = jax.nn.relu(h @ W1 + b1) @ W2 + b2
        h = jnp.where(h >= 0, h, NEG_SLOPE * h)
        mu = jnp.mean(h, axis=-1, keepdims=True)
        var = jnp.mean((h - mu) ** 2, axis=-1, keepdims=True)
        return (h - mu) / jnp.sqrt(var + LN_EPS) * gamma + beta

    def _L2_gnn_ref(node_z, edge_z, src, dst, node_ln_w, node_ln_b, node_W, node_b, edge_ln_w, edge_ln_b, edge_W, edge_b, red_ln_w, red_ln_b, red_W, red_b):
        import jax, jax.numpy as jnp
        import numpy as np
        N_NODES = 6250
        N_EDGES = 100000
        D_NODE = 64
        D_EDGE = 64
        D_MSG = 64
        D_OUT = 64
        NEG_SLOPE = 0.01
        LN_EPS = 1e-05

        def _layer_norm(x, w, b):
            mu = jnp.mean(x, axis=-1, keepdims=True)
            var = jnp.mean(jnp.square(x - mu), axis=-1, keepdims=True)
            return (x - mu) * jax.lax.rsqrt(var + LN_EPS) * w + b

        def _mlp(x, ln_w, ln_b, W, b):
            h = _layer_norm(x, ln_w, ln_b)
            h = h @ W.T + b
            return jax.nn.leaky_relu(h, NEG_SLOPE)
        n_nodes = node_z.shape[0]
        half = node_W.shape[0]
        hn = _mlp(node_z, node_ln_w, node_ln_b, node_W, node_b)
        he = _mlp(edge_z, edge_ln_w, edge_ln_b, edge_W, edge_b)
        msg = jnp.concatenate([hn[src], he], axis=-1)
        emb_edge = _mlp(msg, red_ln_w, red_ln_b, red_W, red_b)
        local = jnp.concatenate([hn, jnp.zeros((n_nodes, half), hn.dtype)], axis=-1)
        emb_local = _mlp(local, red_ln_w, red_ln_b, red_W, red_b)
        msg_sum = jax.ops.segment_sum(emb_edge, dst, num_segments=n_nodes) + emb_local
        deg = jax.ops.segment_sum(jnp.ones((dst.shape[0],), hn.dtype), dst, num_segments=n_nodes)
        z = msg_sum / (deg + 1.0)[:, None]
        return z

    def _L3_gnn_ref(x, edge_idx, W_l, W_r, att, bias):
        import jax, jax.numpy as jnp
        import numpy as np
        N = 3125
        E = 50000
        H = 6
        F_IN = 64
        F_OUT = 64
        NEG_SLOPE = 0.2
        n = x.shape[0]
        loops = jnp.arange(n, dtype=edge_idx.dtype)
        src = jnp.concatenate([edge_idx[0], loops])
        dst = jnp.concatenate([edge_idx[1], loops])
        gl = (x @ W_l).reshape(n, H, F_OUT)
        gr = (x @ W_r).reshape(n, H, F_OUT)
        s = jax.nn.leaky_relu(gl[src] + gr[dst], NEG_SLOPE)
        e = jnp.einsum('ehf,hf->eh', s, att)
        m = jax.ops.segment_max(e, dst, num_segments=n)
        p = jnp.exp(e - m[dst])
        denom = jax.ops.segment_sum(p, dst, num_segments=n)
        alpha = p / (denom[dst] + 1e-16)
        msg = alpha[:, :, None] * gl[src]
        out = jax.ops.segment_sum(msg, dst, num_segments=n)
        out = out.mean(axis=1) + bias
        return jax.nn.selu(out)
    edge_index = jnp.stack([src, dst])
    h = jnp.maximum(_layernorm(x, axis=-1), 0.0)
    x = x + _L0_gnn_ref(h, edge_index, edge_weight, edge_weight_n2, L0_gnn_W, L0_gnn_b, L0_gnn_deg_coeff, L0_gnn_coeff_param, L0_gnn_scale_param)
    h = jnp.maximum(_layernorm(x, axis=-1), 0.0)
    x = x + _L1_gnn_ref(h, edge_index, edge_attr_32, L1_gnn_We, L1_gnn_be, L1_gnn_W1, L1_gnn_b1, L1_gnn_W2, L1_gnn_b2, L1_gnn_eps_gin, L1_gnn_gamma, L1_gnn_beta)
    h = jnp.maximum(_layernorm(x, axis=-1), 0.0)
    x = x + _L2_gnn_ref(h, edge_attr_64, src, dst, L2_gnn_node_ln_w, L2_gnn_node_ln_b, L2_gnn_node_W, L2_gnn_node_b, L2_gnn_edge_ln_w, L2_gnn_edge_ln_b, L2_gnn_edge_W, L2_gnn_edge_b, L2_gnn_red_ln_w, L2_gnn_red_ln_b, L2_gnn_red_W, L2_gnn_red_b)
    h = jnp.maximum(_layernorm(x, axis=-1), 0.0)
    x = x + _L3_gnn_ref(h, edge_index, L3_gnn_W_l, L3_gnn_W_r, L3_gnn_att, L3_gnn_bias)
    return x

_drawn_inputs = setup_inputs


def setup_inputs(seed=0):
    import zlib

    import numpy as np

    out = dict(_drawn_inputs(seed))
    spreads = {'L0_gnn_coeff_param': (0.0, 0.1),
     'L1_gnn_be': (0.0, 0.1),
     'L1_gnn_b1': (0.0, 2.0),
     'L1_gnn_b2': (0.0, 2.0),
     'L1_gnn_gamma': (1.0, 0.2),
     'L1_gnn_beta': (0.0, 0.1),
     'L2_gnn_node_ln_w': (1.0, 0.6),
     'L2_gnn_node_ln_b': (0.0, 0.552),
     'L2_gnn_node_b': (0.0, 0.476),
     'L2_gnn_edge_ln_w': (1.0, 0.6),
     'L2_gnn_edge_ln_b': (0.0, 0.51),
     'L2_gnn_edge_b': (0.0, 0.663),
     'L2_gnn_red_ln_w': (1.0, 0.569),
     'L2_gnn_red_ln_b': (0.0, 0.351),
     'L2_gnn_red_b': (0.0, 0.289),
     'L3_gnn_bias': (0.0, 0.1)}
    factors = {'edge_weight_n2': 3.02, 'L0_gnn_b': 2.829, 'L3_gnn_W_r': 8.0, 'L3_gnn_att': 8.0}
    for name, (base, spread) in spreads.items():
        noise = np.random.default_rng([zlib.crc32(name.encode()), seed]).standard_normal(out[name].shape)
        drawn = base * np.exp(spread * noise) if base else spread * noise
        out[name] = jnp.asarray(drawn.astype(out[name].dtype))
    for name, factor in factors.items():
        out[name] = (out[name] * factor).astype(out[name].dtype)
    return out
```

```python
import numpy as np
from contextlib import ExitStack, contextmanager
import concourse.bass as bass
from concourse import mybir

F32 = mybir.dt.float32
I32 = mybir.dt.int32
ALU = mybir.AluOpType
ACT = mybir.ActivationFunctionType
AX = mybir.AxisListType.X

P = 128
N = 3125
E = 103125
D = 64
B = 8
ROWS = B * P
BATCHES = -(-E // (2 * ROWS)) * 2
TILES = BATCHES * B
PAIRS = BATCHES // 2
NB = -(-(N + P) // P)
NPAD = NB * P
TABLES = B
SROWS = NPAD + P
H = 6
HP = H // 2
HALF = D // 2
WH = D + 1
FAR = -1.0e30


class Ctx:

    def __init__(self, nc, phase=""):
        self.nc, self.phase = nc, phase
        self.stack = ExitStack()
        self.used = []

    def sb(self, name, shape, dtype=F32):
        return self.stack.enter_context(self.nc.sbuf_tensor(self.phase + name, shape, dtype))

    def ps(self, name, shape, dtype=F32):
        return self.stack.enter_context(self.nc.psum_tensor(self.phase + name, shape, dtype))

    def sem(self, name):
        self.used.append(self.nc.alloc_semaphore(self.phase + name))
        return self.used[-1]

    def sems(self, *names):
        return [self.sem(n) for n in names]

    def __enter__(self):
        self.stack.__enter__()
        return self

    def __exit__(self, *a):
        if self.used and not a[0]:
            self.nc.clear_and_free_semaphores(self.used)
            self.nc.all_engine_barrier()
        return self.stack.__exit__(*a)


class Kept:
    pass


class Chain:

    def __init__(self, engine, sem):
        self.engine, self.sem, self.count = engine, sem, 0

    def __call__(self, ins):
        self.count += 1
        ins.then_inc(self.sem, 1)
        self.engine.wait_ge(self.sem, self.count)


def pairs(engine, body):
    body(0, False)
    with engine.Fori(1, PAIRS - 1) as t:
        body(t, False)
    body(PAIRS - 1, True)


def wait_past(engine, sem, value):
    if not isinstance(value, int) or value > 0:
        engine.wait_ge(sem, value)


def over(ap, n):
    return ap.unsqueeze(2).to_broadcast([ap.shape[0], ap.shape[1], n])


def rows_over(ap, n):
    return ap.unsqueeze(1).to_broadcast([ap.shape[0], n, ap.shape[1]])


def tiles3(ap, a=B):
    return ap.rearrange("p (a b) -> p a b", a=a)


def setup(nc, k, ins):
    with Ctx(nc, "setup_") as c:
        loaded, chain_s, pool_s, act_s, cleared, zero_ready, z_ready, soft_ready, done = c.sems(
            "params_loaded", "dve_step", "pool_step", "act_step", "tables_cleared", "zeros_ready",
            "softplus_arg_ready", "softplus_parts_ready", "spare")
        zeros = c.sb("zeros", [P, SROWS // P * D])
        w2 = c.sb("deg_v", [P, TILES])
        w1 = c.sb("adj_v", [P, TILES])
        dst_f = c.sb("dst_f", [P, TILES])
        base_i = c.sb("base_i", [P, TILES], I32)
        za, zb, zc = c.sb("za", [P, TILES]), c.sb("zb", [P, TILES]), c.sb("zc", [P, TILES])
        small = c.sb("small", [P, 16])
        tmp = c.sb("tmp", [P, H * D])
        loads = [
            (k.x[:, :, :], ins["x"].rearrange("(b p) d -> p b d", p=P)),
            (k.src_i[:, :], ins["src_t"]), (k.dst_i[:, :], ins["dst_t"]),
            (w1[:, :], ins["w_t"]), (w2[:, :], ins["w2_t"]),
            (base_i[:, :], ins["dst_t"][0:1, :].to_broadcast([P, TILES])),
            (k.W0[0:D, :], ins["W0"]), (k.W0[D:D + 1, :], ins["b0"]),
            (k.deg_coeff[:, :], ins["deg_coeff"].partition_broadcast(P)),
            (k.coeff[:, :], ins["coeff_param"].partition_broadcast(P)),
            (k.scale[:, :], ins["scale_param"].partition_broadcast(P)),
            (k.eps_gin[:, :], ins["eps_gin"].partition_broadcast(P)),
            (k.We[:, :], ins["We"]), (k.be[:, :], ins["be"].partition_broadcast(P)),
            (k.W1[:, :], ins["W1"]), (k.b1[:, :], ins["b1"]),
            (k.W2[0:D, :], ins["W2"]), (k.W2[D:D + 1, :], ins["b2"]),
            (k.gamma[:, :], ins["gamma"].partition_broadcast(P)),
            (k.beta[:, :], ins["beta"].partition_broadcast(P)),
            (k.nlw[:, :], ins["nlw"].partition_broadcast(P)),
            (k.nlb[:, :], ins["nlb"].partition_broadcast(P)),
            (k.nW[0:D, :], ins["nWT"]), (k.nW[D:D + 1, :], ins["nb"]),
            (k.elw[:, :], ins["elw"]), (k.elb[:, :], ins["elb"]),
            (k.eW[:, :], ins["eWT"]), (k.eb[:, :], ins["eb"].partition_broadcast(P)),
            (k.rlw[:, :], ins["rlw"]), (k.rlb[:, :], ins["rlb"]),
            (k.rlw_row[:, :], ins["rlw_r"].partition_broadcast(P)),
            (k.rlb_row[:, :], ins["rlb_r"].partition_broadcast(P)),
            (k.rW[0:D, :], ins["rWT"]), (k.rW[D:D + 1, :], ins["rb"]),
            (k.rb[:, :], ins["rb_v"].partition_broadcast(P)),
            (k.Wlr[0:D, :], ins["Wl"]), (k.Wlr[D:P, :], ins["Wr"]),
            (k.att_row[:, :], ins["att_r"].partition_broadcast(P)),
            (k.att_col[:, :], ins["att_c"]),
            (k.bias3[:, :], ins["bias"].partition_broadcast(P)),
        ]
        for j in range(HP):
            for o in range(2):
                loads.append((k.Wl_h[o * D:(o + 1) * D, j, :],
                              ins["Wl"][:, (2 * j + o) * D:(2 * j + o + 1) * D]))
        with nc.Block() as block:
            @block.sync
            def _(sp):
                for dst, src in loads:
                    sp.dma_start(dst, src).then_inc(loaded, 16)
                sp.wait_ge(zero_ready, 1)
                for i in range(TABLES):
                    sp.dma_start(k.scatter_sums[i].rearrange("(p r) d -> p (r d)", p=P),
                                 zeros[:, :]).then_inc(cleared, 16)
                sp.wait_ge(cleared, 16 * TABLES)
                sp.wait_ge(loaded, 16 * len(loads))

            @block.gpsimd
            def _(pool):
                step = Chain(pool, pool_s)
                exact = dict(allow_small_or_imprecise_dtypes=True)
                pool.iota(k.row0[:, :], pattern=[[1, P]], base=0, channel_multiplier=0, **exact)
                pool.iota(k.row1[:, :], pattern=[[1, P]], base=1, channel_multiplier=0, **exact)
                pool.iota(k.col0[:, :], pattern=[[0, 1]], base=0, channel_multiplier=1, **exact)
                pool.iota(k.col1[:, :], pattern=[[0, 1]], base=1, channel_multiplier=1, **exact)
                step(pool.iota(k.spare_row[:, :], pattern=[[0, 1]], base=NPAD, channel_multiplier=1,
                               **exact))

            @block.scalar
            def _(act):
                act.wait_ge(z_ready, 1)
                act.activation(zb[:, :], za[:, :], ACT.Abs).then_inc(act_s, 1)
                act.activation(small[:, 1:2], small[:, 0:1], ACT.Abs).then_inc(act_s, 1)
                act.wait_ge(act_s, 2)
                act.activation(zc[:, :], zb[:, :], ACT.Exp, scale=-1.0).then_inc(act_s, 1)
                act.activation(small[:, 2:3], small[:, 1:2], ACT.Exp, scale=-1.0).then_inc(act_s, 1)
                act.activation(k.coeff_e[:, :], k.coeff_d[:, :], ACT.Exp).then_inc(act_s, 1)
                act.wait_ge(act_s, 5)
                act.activation(zb[:, :], zc[:, :], ACT.Ln, bias=1.0).then_inc(soft_ready, 1)
                act.activation(small[:, 3:4], small[:, 2:3], ACT.Ln, bias=1.0).then_inc(soft_ready, 1)

            @block.vector
            def _(dve):
                step = Chain(dve, chain_s)
                dve.memset(zeros[:, :], 0.0).then_inc(zero_ready, 1)
                dve.memset(k.eps[:, :], 1e-5)
                dve.memset(k.zero_i[:, :], 0)
                dve.memset(k.zero_o[:, :], 0)
                dve.memset(k.zero_o2[:, :], 0)
                dve.memset(k.hT[D:D + 1, :], 1.0)
                step(dve.memset(k.coeff_s[:, :], 0.0))
                dve.wait_ge(loaded, 16 * len(loads))
                dve.wait_ge(pool_s, 1)
                step(dve.tensor_copy(k.src_f[:, :], k.src_i[:, :]))
                step(dve.tensor_copy(dst_f[:, :], k.dst_i[:, :]))
                step(dve.tensor_copy(zc[:, :], base_i[:, :]))
                step(dve.tensor_tensor(k.dst_rel[:, :], dst_f[:, :], zc[:, :], ALU.subtract))
                step(dve.tensor_scalar(k.win_node[:, :], zc[:, :], k.col0[:, :], None, ALU.add))
                step(dve.tensor_scalar(k.src_sp[:, :], k.src_f[:, :], k.spare_row[:, :], None,
                                       ALU.subtract))
                step(dve.tensor_tensor(k.ident[:, :], k.row0[:, :],
                                       k.col0[:, :].to_broadcast([P, P]), ALU.is_equal))
                step(dve.tensor_scalar(k.center[:, :], k.ident[0:D, 0:D], -1.0 / D, None, ALU.add))
                step(dve.tensor_copy(small[:, 0:1], k.scale[:, :]))
                step(dve.tensor_reduce(small[:, 4:5], k.coeff[:, :], AX, ALU.max))
                step(dve.tensor_scalar(k.coeff_d[:, :], k.coeff[:, :], small[:, 4:5], None,
                                       ALU.subtract))
                dve.tensor_scalar(za[:, :], w2[:, :], k.deg_coeff[:, 0:1], k.deg_coeff[:, 1:2],
                                  ALU.mult, ALU.add).then_inc(z_ready, 1)
                step(dve.tensor_tensor(dst_f[:, :], k.src_f[:, :], dst_f[:, :], ALU.not_equal))
                step(dve.tensor_tensor(w1[:, :], w1[:, :], dst_f[:, :], ALU.mult))
                dve.wait_ge(soft_ready, 2)
                step(dve.scalar_tensor_tensor(zb[:, :], za[:, :], 0.0, zb[:, :], ALU.max, ALU.add))
                step(dve.tensor_tensor(k.weight[:, :], w1[:, :], zb[:, :], ALU.mult))
                step(dve.scalar_tensor_tensor(small[:, 5:6], small[:, 0:1], 0.0, small[:, 3:4],
                                              ALU.max, ALU.add))
                step(dve.tensor_reduce(small[:, 6:7], k.coeff_e[:, :], AX, ALU.add))
                step(dve.reciprocal(small[:, 7:8], small[:, 6:7]))
                step(dve.tensor_tensor(small[:, 8:9], small[:, 5:6], small[:, 7:8], ALU.mult))
                step(dve.tensor_scalar(k.coeff_s[:, :], k.coeff_e[:, :], small[:, 8:9], None,
                                       ALU.mult))
                step(dve.tensor_scalar(k.eWw[:, :], k.eW[:, :], k.elw[:, :], None, ALU.mult))
                step(dve.tensor_scalar(k.rWw[:, :], k.rW[0:D, :], k.rlw[:, :], None, ALU.mult))
                step(dve.tensor_copy(k.elb_col[:, :], k.elb[:, 0:1].to_broadcast([D, P])))
                step(dve.tensor_copy(k.rlb_col[:, :], k.rlb[:, 0:1].to_broadcast([D, P])))
                step(dve.tensor_tensor(tmp[:, :], k.Wlr[:, :], k.att_row[:, :], ALU.mult))
                step(dve.tensor_reduce(k.Watt[:, :], tiles3(tmp[:, :], H), AX, ALU.add))
                step(dve.tensor_scalar(k.Watt[:, :], k.Watt[:, :], 0.2, None, ALU.mult))
                step(dve.memset(k.att_blk[:, :, :], 0.0))
                for j in range(HP):
                    for o in range(2):
                        step(dve.tensor_scalar(k.att_blk[o * D:(o + 1) * D, j, 2 * j + o:2 * j + o + 1],
                                               k.att_col[o * D:(o + 1) * D, j:j + 1], 0.8, None,
                                               ALU.mult))

        with nc.psum_tensor("fold", [P, 512], F32) as fold, nc.Block() as block:
            @block.tensor
            def _(pe):
                pe.matmul(fold[0:D, 0:HALF], k.center[:, :], k.eWw[:, :], start=True, stop=True)
                pe.matmul(fold[0:D, 64:64 + D], k.center[:, :], k.rWw[:, :], start=True, stop=True)
                pe.matmul(fold[:, 128:128 + HALF], k.elb_col[:, :], k.eW[:, :],
                          start=True, stop=True)
                pe.matmul(fold[:, 192:192 + D], k.rlb_col[:, :], k.rW[0:D, :],
                          start=True, stop=True).then_inc(done, 1)

            @block.vector
            def _(dve):
                dve.wait_ge(done, 1)
                dve.tensor_copy(k.eR[:, 0:HALF], fold[0:D, 0:HALF])
                dve.tensor_copy(k.eR[:, HALF:HALF + D], k.center[:, :])
                dve.tensor_copy(k.rR[:, 0:D], fold[0:D, 64:64 + D])
                dve.tensor_copy(k.rR[:, D:2 * D], k.center[:, :])
                dve.tensor_tensor(k.ec[:, :], fold[:, 128:128 + HALF], k.eb[:, :], ALU.add)
                dve.tensor_tensor(k.rc[:, :], fold[:, 192:192 + D], k.rb[:, :], ALU.add)


class Norm:

    def __init__(self, c, k):
        self.k = k
        self.var_ready, self.std_ready = c.sems("variance_ready", "std_ready")
        self.stat = c.sb("stat", [P, 4, NB])
        self.n_dve = self.n_act = 0

    def dve(self, dve, step, out, in_, tmp):
        s, k = self.stat, self.k
        self.n_dve += 1
        step(dve.tensor_reduce(s[:, 0, :], in_, AX, ALU.add))
        step(dve.tensor_scalar(s[:, 0, :], s[:, 0, :], 1.0 / D, None, ALU.mult))
        step(dve.tensor_tensor(out, in_, over(s[:, 0, :], D), ALU.subtract))
        step(dve.tensor_tensor(tmp, out, out, ALU.mult))
        dve.tensor_reduce(s[:, 1, :], tmp, AX, ALU.add).then_inc(self.var_ready, 1)
        dve.wait_ge(self.std_ready, self.n_dve)
        step(dve.reciprocal(s[:, 3, :], s[:, 2, :]))
        step(dve.tensor_tensor(out, out, over(s[:, 3, :], D), ALU.mult))

    def act(self, act):
        self.n_act += 1
        act.wait_ge(self.var_ready, self.n_act)
        act.activation(self.stat[:, 2, :], self.stat[:, 1, :], ACT.Sqrt, bias=self.k.eps[:, :],
                       scale=1.0 / D).then_inc(self.std_ready, 1)


def transposed(pe, k, ps, src, rows=P):
    for b in range(NB):
        last = pe.transpose(ps[0:D, b * P:(b + 1) * P], src[:, b, :], k.ident[:, :])
    return last


def node0(nc, k):
    with Ctx(nc, "node0_") as c:
        step_s, h_ready, hT_ready, hTs_ready, wh_ready, nsq_ready, nrm_ready, row_ready, stored = c.sems(
            "dve_step", "h_ready", "hT_in_psum", "hT_ready", "wh_in_psum", "norm_square_ready",
            "norm_ready", "rows_ready", "table_stored")
        norm = Norm(c, k)
        nsq = c.sb("nsq", [P, NB])
        ps = c.ps("node_ps", [P, 4096])
        with nc.Block() as block:
            @block.scalar
            def _(act):
                norm.act(act)
                act.wait_ge(nsq_ready, 1)
                act.activation(k.wh[:, :, D], nsq[:, :], ACT.Sqrt).then_inc(nrm_ready, 1)

            @block.vector
            def _(dve):
                step = Chain(dve, step_s)
                norm.dve(dve, step, k.h[:, :, :], k.x[:, :, :], k.t1[:, :, :])
                dve.tensor_scalar(k.h[:, :, :], k.h[:, :, :], 0.0, None, ALU.max).then_inc(h_ready, 1)
                dve.wait_ge(hT_ready, 1)
                dve.tensor_copy(k.hT[0:D, :], ps[0:D, 0:NPAD]).then_inc(hTs_ready, 1)
                dve.wait_ge(wh_ready, 1)
                step(dve.tensor_copy(k.wh[:, :, 0:D], tiles3(ps[:, 0:NB * D], NB)))
                step(dve.tensor_tensor(k.t1[:, :, :], k.wh[:, :, 0:D], k.wh[:, :, 0:D], ALU.mult))
                dve.tensor_reduce(nsq[:, :], k.t1[:, :, :], AX, ALU.add).then_inc(nsq_ready, 1)

            @block.tensor
            def _(pe):
                pe.wait_ge(h_ready, 1)
                transposed(pe, k, ps, k.h).then_inc(hT_ready, 1)
                pe.wait_ge(hTs_ready, 1)
                for b in range(NB):
                    last = pe.matmul(ps[:, b * D:(b + 1) * D], k.hT[:, b * P:(b + 1) * P],
                                     k.W0[:, :], start=True, stop=True)
                last.then_inc(wh_ready, 1)

            @block.sync
            def _(sp):
                sp.wait_ge(nrm_ready, 1)
                sp.dma_start(k.t_wh.rearrange("(b p) d -> p b d", p=P), k.wh[:, :, :]).then_inc(stored, 16)
                sp.wait_ge(stored, 16)


def node1(nc, k):
    with Ctx(nc, "node1_") as c:
        step_s, hb_ready, stored = c.sems("dve_step", "hb_ready", "table_stored")
        got = [c.sem(f"partial_loaded{i}") for i in range(TABLES)]
        norm = Norm(c, k)
        part = [c.sb(f"partial{i}", [P, NB, D]) for i in range(4)]
        with nc.Block() as block:
            @block.sync
            def _(sp):
                for i in range(TABLES):
                    if i >= 4:
                        sp.wait_ge(step_s, i - 2)
                    sp.dma_start(part[i % 4][:, :, :],
                                 k.scatter_sums[i][0:NPAD, :].rearrange("(b p) d -> p b d", p=P)
                                 ).then_inc(got[i], 16)
                sp.wait_ge(hb_ready, 1)
                sp.dma_start(k.t_h.rearrange("(b p) d -> p b d", p=P), k.t1[:, :, :]).then_inc(stored, 16)
                sp.wait_ge(stored, 16)

            @block.scalar
            def _(act):
                norm.act(act)

            @block.vector
            def _(dve):
                step = Chain(dve, step_s)
                step(dve.tensor_scalar(k.t1[:, :, :], k.wh[:, :, 0:D], k.coeff_s[:, 2:3], None, ALU.mult))
                for i in range(TABLES):
                    dve.wait_ge(got[i], 16)
                    step(dve.tensor_tensor(k.t1[:, :, :], k.t1[:, :, :], part[i % 4][:, :, :], ALU.add))
                step(dve.tensor_tensor(k.x[:, :, :], k.x[:, :, :], k.t1[:, :, :], ALU.add))
                norm.dve(dve, step, k.h[:, :, :], k.x[:, :, :], k.t1[:, :, :])
                step(dve.tensor_scalar(k.h[:, :, :], k.h[:, :, :], 0.0, None, ALU.max))
                dve.tensor_tensor(k.t1[:, :, :], k.h[:, :, :], rows_over(k.be[:, :], NB),
                                  ALU.add).then_inc(hb_ready, 1)
                dve.memset(k.accT[0:D + 1, 0:NPAD], 0.0)


def node2(nc, k):
    with Ctx(nc, "node2_") as c:
        (step_s, hT_ready, gin_ready, m1_ready, r_ready, m2_ready, h_ready, zT_ready, zTs_ready,
         n_ready, l_ready, lT_ready, lTs_ready, e_ready, hn_ready, stored) = c.sems(
            "dve_step", "hT_in_psum", "gin_ready", "mlp1_in_psum", "mlp1_ready", "mlp2_in_psum",
            "node_norm_ready", "zT_in_psum", "zT_ready", "hn_in_psum", "local_norm_ready",
            "localT_in_psum", "localT_ready", "local_in_psum", "hn_ready", "table_stored")
        norm = Norm(c, k)
        ps = c.ps("node_ps", [P, 4096])
        chunks = [(o, min(512, NPAD - o)) for o in range(0, NPAD, 512)]
        with nc.Block() as block:
            @block.tensor
            def _(pe):
                transposed(pe, k, ps, k.h).then_inc(hT_ready, 1)
                pe.wait_ge(gin_ready, 1)
                for o, w in chunks:
                    last = pe.matmul(ps[0:D, o:o + w], k.W1[:, :], k.accT[0:D, o:o + w],
                                     start=True, stop=True)
                last.then_inc(m1_ready, 1)
                pe.wait_ge(r_ready, 1)
                for b in range(NB):
                    last = pe.matmul(ps[:, b * D:(b + 1) * D], k.hT[:, b * P:(b + 1) * P],
                                     k.W2[:, :], start=True, stop=True)
                last.then_inc(m2_ready, 1)
                pe.wait_ge(h_ready, 1)
                transposed(pe, k, ps, k.t2).then_inc(zT_ready, 1)
                pe.wait_ge(zTs_ready, 1)
                for b in range(NB):
                    last = pe.matmul(ps[:, b * D:b * D + HALF], k.hT[:, b * P:(b + 1) * P],
                                     k.nW[:, :], start=True, stop=True)
                last.then_inc(n_ready, 1)
                pe.wait_ge(l_ready, 1)
                transposed(pe, k, ps, k.t2).then_inc(lT_ready, 1)
                pe.wait_ge(lTs_ready, 1)
                for b in range(NB):
                    last = pe.matmul(ps[:, b * D:(b + 1) * D], k.hT[:, b * P:(b + 1) * P],
                                     k.rW[:, :], start=True, stop=True)
                last.then_inc(e_ready, 1)

            @block.scalar
            def _(act):
                act.wait_ge(m1_ready, 1)
                act.activation(k.hT[0:D, :], ps[0:D, 0:NPAD], ACT.Relu, bias=k.b1[:, :]).then_inc(r_ready, 1)
                for _ in range(4):
                    norm.act(act)

            @block.vector
            def _(dve):
                step = Chain(dve, step_s)
                step(dve.tensor_scalar(k.eps1[:, :], k.eps_gin[:, :], 1.0, None, ALU.add))
                dve.wait_ge(hT_ready, 1)
                dve.scalar_tensor_tensor(k.accT[0:D, 0:NPAD], ps[0:D, 0:NPAD], k.eps1[0:D, :],
                                         k.accT[0:D, 0:NPAD], ALU.mult, ALU.add).then_inc(gin_ready, 1)
                dve.wait_ge(m2_ready, 1)
                m2 = tiles3(ps[:, 0:NB * D], NB)
                step(dve.tensor_copy(k.t1[:, :, :], m2))
                step(dve.scalar_tensor_tensor(k.t1[:, :, :], k.t1[:, :, :], 0.2, k.t1[:, :, :],
                                              ALU.mult, ALU.max))
                norm.dve(dve, step, k.t2[:, :, :], k.t1[:, :, :], k.h[:, :, :])
                step(dve.tensor_tensor(k.t2[:, :, :], k.t2[:, :, :], rows_over(k.gamma[:, :], NB), ALU.mult))
                step(dve.tensor_tensor(k.t2[:, :, :], k.t2[:, :, :], rows_over(k.beta[:, :], NB), ALU.add))
                step(dve.tensor_tensor(k.x[:, :, :], k.x[:, :, :], k.t2[:, :, :], ALU.add))
                norm.dve(dve, step, k.h[:, :, :], k.x[:, :, :], k.t1[:, :, :])
                step(dve.tensor_scalar(k.h[:, :, :], k.h[:, :, :], 0.0, None, ALU.max))
                norm.dve(dve, step, k.t2[:, :, :], k.h[:, :, :], k.t1[:, :, :])
                step(dve.tensor_tensor(k.t2[:, :, :], k.t2[:, :, :], rows_over(k.nlw[:, :], NB), ALU.mult))
                dve.tensor_tensor(k.t2[:, :, :], k.t2[:, :, :], rows_over(k.nlb[:, :], NB),
                                  ALU.add).then_inc(h_ready, 1)
                dve.wait_ge(zT_ready, 1)
                dve.tensor_copy(k.hT[0:D, :], ps[0:D, 0:NPAD]).then_inc(zTs_ready, 1)
                dve.wait_ge(n_ready, 1)
                step(dve.memset(k.wh[:, :, HALF:D], 0.0))
                step(dve.tensor_copy(k.wh[:, :, 0:HALF], m2[:, :, 0:HALF]))
                dve.scalar_tensor_tensor(k.wh[:, :, 0:HALF], k.wh[:, :, 0:HALF], 0.01,
                                         k.wh[:, :, 0:HALF], ALU.mult, ALU.max).then_inc(hn_ready, 1)
                dve.wait_ge(hn_ready, 1)
                norm.dve(dve, step, k.t2[:, :, :], k.wh[:, :, 0:D], k.t1[:, :, :])
                step(dve.tensor_tensor(k.t2[:, :, :], k.t2[:, :, :], rows_over(k.rlw_row[:, :], NB), ALU.mult))
                dve.tensor_tensor(k.t2[:, :, :], k.t2[:, :, :], rows_over(k.rlb_row[:, :], NB),
                                  ALU.add).then_inc(l_ready, 1)
                dve.wait_ge(lT_ready, 1)
                dve.tensor_copy(k.hT[0:D, :], ps[0:D, 0:NPAD]).then_inc(lTs_ready, 1)
                dve.memset(k.accT[0:D + 1, 0:NPAD], 0.0)
                dve.wait_ge(e_ready, 1)
                step(dve.tensor_copy(k.t1[:, :, :], m2))
                step(dve.scalar_tensor_tensor(k.local[:, :, :], k.t1[:, :, :], 0.01, k.t1[:, :, :],
                                              ALU.mult, ALU.max))

            @block.sync
            def _(sp):
                sp.wait_ge(hn_ready, 1)
                sp.dma_start(k.t_hn.rearrange("(b p) d -> p b d", p=P),
                             k.wh[:, :, 0:HALF]).then_inc(stored, 16)
                sp.wait_ge(stored, 16)


def node3(nc, k):
    with Ctx(nc, "node3_") as c:
        step_s, a_ready, h_ready, stored = c.sems("dve_step", "sums_in_psum", "h_ready", "table_stored")
        norm = Norm(c, k)
        deg = c.sb("deg", [P, 2, NB])
        ps = c.ps("node_ps", [P, 8, 512])
        PER = 7
        with nc.Block() as block:
            @block.tensor
            def _(pe):
                for b in range(NB):
                    o = b % PER * (D + 1)
                    last = pe.matmul(ps[:, b // PER, o:o + D + 1], k.accT[0:D + 1, b * P:(b + 1) * P],
                                     k.ident[0:D + 1, 0:D + 1], start=True, stop=True)
                last.then_inc(a_ready, 1)

            @block.scalar
            def _(act):
                norm.act(act)

            @block.vector
            def _(dve):
                step = Chain(dve, step_s)
                dve.wait_ge(a_ready, 1)
                for g in range(-(-NB // PER)):
                    b0, b1 = g * PER, min(NB, (g + 1) * PER)
                    v = tiles3(ps[:, g, 0:(b1 - b0) * (D + 1)], b1 - b0)
                    step(dve.tensor_tensor(k.t1[:, b0:b1, :], v[:, :, 0:D], k.local[:, b0:b1, :], ALU.add))
                    step(dve.tensor_scalar(deg[:, 0, b0:b1], v[:, :, D], 1.0, None, ALU.add))
                step(dve.reciprocal(deg[:, 1, :], deg[:, 0, :]))
                step(dve.tensor_tensor(k.t1[:, :, :], k.t1[:, :, :], over(deg[:, 1, :], D), ALU.mult))
                step(dve.tensor_tensor(k.x[:, :, :], k.x[:, :, :], k.t1[:, :, :], ALU.add))
                norm.dve(dve, step, k.h[:, :, :], k.x[:, :, :], k.t1[:, :, :])
                dve.tensor_scalar(k.h[:, :, :], k.h[:, :, :], 0.0, None, ALU.max).then_inc(h_ready, 1)

            @block.sync
            def _(sp):
                sp.wait_ge(h_ready, 1)
                sp.dma_start(k.t_h3.rearrange("(b p) d -> p b d", p=P), k.h[:, :, :]).then_inc(stored, 16)
                sp.wait_ge(stored, 16)


def node4(nc, k, out):
    L = 1.0507009873554805
    A = 1.6732632423543772
    with Ctx(nc, "node4_") as c:
        step_s, o_ready, m_ready, e_ready, x_ready, stored = c.sems(
            "dve_step", "heads_in_psum", "negative_part_ready", "exp_ready", "x_ready", "out_stored")
        ps = c.ps("node_ps", [P, 2048])
        with nc.Block() as block:
            @block.tensor
            def _(pe):
                for b in range(NB):
                    for j in range(HP):
                        last = pe.matmul(ps[:, b * D:(b + 1) * D], k.accT[:, j * NPAD + b * P:j * NPAD + (b + 1) * P],
                                         k.Wl_h[:, j, :], start=(j == 0), stop=(j == HP - 1))
                last.then_inc(o_ready, 1)

            @block.scalar
            def _(act):
                act.wait_ge(m_ready, 1)
                act.activation(k.t2[:, :, :], k.h[:, :, :], ACT.Exp).then_inc(e_ready, 1)

            @block.vector
            def _(dve):
                step = Chain(dve, step_s)
                dve.wait_ge(o_ready, 1)
                step(dve.tensor_tensor(k.t1[:, :, :], tiles3(ps[:, 0:NB * D], NB),
                                       rows_over(k.bias3[:, :], NB), ALU.add))
                dve.tensor_scalar(k.h[:, :, :], k.t1[:, :, :], 0.0, None, ALU.min).then_inc(m_ready, 1)
                step(dve.tensor_scalar(k.t1[:, :, :], k.t1[:, :, :], 0.0, L, ALU.max, ALU.mult))
                step(dve.tensor_tensor(k.x[:, :, :], k.x[:, :, :], k.t1[:, :, :], ALU.add))
                dve.wait_ge(e_ready, 1)
                step(dve.tensor_scalar(k.t2[:, :, :], k.t2[:, :, :], -1.0, L * A, ALU.add, ALU.mult))
                dve.tensor_tensor(k.x[:, :, :], k.x[:, :, :], k.t2[:, :, :], ALU.add).then_inc(x_ready, 1)

            @block.sync
            def _(sp):
                full = N // P
                sp.wait_ge(x_ready, 1)
                sp.dma_start(out[0:full * P, :].rearrange("(b p) d -> p b d", p=P),
                             k.x[:, 0:full, :]).then_inc(stored, 16)
                sp.dma_start(out[full * P:N, :], k.x[0:N - full * P, full, :]).then_inc(stored, 16)
                sp.wait_ge(stored, 32)


class Gather:

    def __init__(self, c, k, table, width, slot):
        self.k, self.table, self.width, self.slot = k, table, width, slot
        self.idx = [c.sb(f"gather_idx{h}", [P, B], I32) for h in (0, 1)]
        self.go = c.sem("gather_go")
        self.gate = c.sem("pool_gate")
        self.gathered = [c.sem(f"gathered{h}") for h in (0, 1)]

    def order(self, dve, t, h):
        dve.tensor_copy(self.idx[h][:, :], self.k.src_i[:, bass.ds(t * 2 * B + h * B, B)]).then_inc(self.go, 1)

    def gather(self, nc, pool, n, h, first=False):
        pool.wait_ge(self.go, n)
        if not first:
            pool.wait_ge(self.gate, n - 1)
        nc.gpsimd.tensor_tensor(self.k.zero_o[:, :], self.k.zero_i[:, :], self.k.zero_i[:, :],
                                ALU.add).then_inc(self.gate, 1)
        for j in range(B):
            nc.gpsimd.indirect_dma_start(
                self.slot(h, j), None, self.table[:, :],
                bass.IndirectOffsetOnAxis(ap=self.idx[h][:, j:j + 1], axis=0)).then_inc(self.gathered[h], 16)

    def loop(self, nc, pool):
        self.gather(nc, pool, 1, 0, True)
        self.gather(nc, pool, 2, 1)

        def body(t, last):
            if not last:
                self.gather(nc, pool, 2 * t + 3, 0)
                self.gather(nc, pool, 2 * t + 4, 1)
        pairs(pool, body)


def onehot(dve, k, out, t, h):
    return dve.tensor_tensor(out, over(k.dst_rel[:, bass.ds(t * 2 * B + h * B, B)], P),
                             rows_over(k.row0[:, :], B), ALU.is_equal)


def edge0(nc, k):
    with Ctx(nc, "edge0_") as c:
        g = [c.sb(f"src_rows{h}", [P, B, WH]) for h in (0, 1)]
        win = [c.sb(f"window{h}", [P, B, WH]) for h in (0, 1)]
        drow = [c.sb(f"dst_row{h}", [P, ROWS], I32) for h in (0, 1)]
        srow = [c.sb(f"src_row{h}", [P, ROWS], I32) for h in (0, 1)]
        oht = [c.sb(f"onehot_t{h}", [P, ROWS]) for h in (0, 1)]
        same = [c.sb(f"same_src{h}", [P, ROWS]) for h in (0, 1)]
        vw = [c.sb(f"weighted{h}", [P, B, D]) for h in (0, 1)]
        val = [c.sb(f"sums{h}", [P, B, D]) for h in (0, 1)]
        sidx = [c.sb(f"scatter_idx{h}", [P, B], I32) for h in (0, 1)]
        rank = c.sb("rank", [P, ROWS])
        prod = c.sb("prod", [P, B, D])
        s = c.sb("small", [P, 16, B])
        wc = [c.ps(f"dst_rows_ps{h}", [P, B, P]) for h in (0, 1)]
        dup = [c.ps(f"sums_ps{h}", [P, B, D]) for h in (0, 1)]
        ga = Gather(c, k, k.t_wh, WH, lambda h, j: g[h][:, j, :])
        rows_ready = [c.sem(f"rows_loaded{h}") for h in (0, 1)]
        win_ready = [c.sem(f"window_loaded{h}") for h in (0, 1)]
        scattered = [c.sem(f"scattered{h}") for h in (0, 1)]
        (oht_ready, same_ready, vw_ready, wc_ready, dup_ready, val_ready, sidx_ready, gate2) = c.sems(
            "onehot_ready", "same_ready", "weighted_ready", "dst_rows_in_psum", "sums_in_psum",
            "sums_ready", "scatter_idx_ready", "pool_gate2")
        (rank_done, last_done, stands_done, moved_done, prod_done, norms_done, dot_done, floor_done,
         recip_done, sim_done, parts_done, signed_done, weight_done) = c.sems(
            "rank_done", "last_done", "stands_done", "moved_done", "prod_done", "norms_done",
            "dot_done", "floor_done", "recip_done", "sim_done", "parts_done", "signed_done",
            "weight_done")
        with nc.Block() as block:
            @block.sync
            def _(sp):
                def body(t, last):
                    for h in (0, 1):
                        n = 2 * t + h + 1
                        sp.wait_ge(same_ready, n)
                        sp.dma_start(drow[h][:, :], k.dst_row[bass.ds(2 * t + h, 1), :].to_broadcast([P, ROWS])
                                     ).then_inc(rows_ready[h], 16)
                        sp.dma_start(srow[h][:, :], k.src_row[bass.ds(2 * t + h, 1), :].to_broadcast([P, ROWS])
                                     ).then_inc(rows_ready[h], 16)
                        sp.wait_ge(wc_ready, n)
                        for j in range(B):
                            base = sp.value_load(k.dst_i[0:1, bass.ds(t * 2 * B + h * B + j, 1)],
                                                 min_val=0, max_val=N)
                            sp.dma_start(win[h][:, j, :], k.t_wh[bass.ds(base, P), :]
                                         ).then_inc(win_ready[h], 16)
                pairs(sp, body)

            @block.gpsimd
            def _(pool):
                def scatter(n, h, t):
                    pool.wait_ge(val_ready, n + 2)
                    pool.wait_ge(sidx_ready, n)
                    wait_past(pool, scattered[1 - h], B * 16 * (t + h))
                    pool.wait_ge(gate2, n)
                    nc.gpsimd.tensor_tensor(k.zero_o2[:, :], k.zero_i[:, :], k.zero_i[:, :],
                                            ALU.add).then_inc(gate2, 1)
                    for j in range(B):
                        nc.gpsimd.indirect_dma_start(
                            k.scatter_sums[j], bass.IndirectOffsetOnAxis(ap=sidx[h][:, j:j + 1], axis=0),
                            val[h][:, j, :], None, compute_op=ALU.add).then_inc(scattered[h], 16)

                pool.sem_inc(gate2, 1)
                ga.gather(nc, pool, 1, 0, True)

                def body(t, last):
                    ga.gather(nc, pool, 2 * t + 2, 1)
                    scatter(2 * t + 1, 0, t)
                    if not last:
                        ga.gather(nc, pool, 2 * t + 3, 0)
                    scatter(2 * t + 2, 1, t)
                pairs(pool, body)
                for h in (0, 1):
                    pool.wait_ge(scattered[h], B * 16 * PAIRS)

            @block.tensor
            def _(pe):
                pe.sem_inc(wc_ready, 2)
                pe.sem_inc(dup_ready, 2)

                def body(t, last):
                    for h in (0, 1):
                        n = 2 * t + h + 1
                        pe.wait_ge(win_ready[h], B * 16 * (t + 1))
                        pe.wait_ge(oht_ready, n)
                        for j in range(B):
                            last_mm = pe.matmul(wc[h][:, j, 0:WH], oht[h][:, j * P:(j + 1) * P],
                                                win[h][:, j, :], start=True, stop=True)
                        last_mm.then_inc(wc_ready, 1)
                        pe.wait_ge(vw_ready, n)
                        pe.wait_ge(val_ready, n)
                        for j in range(B):
                            mm = pe.matmul(dup[h][:, j, :], same[h][:, j * P:(j + 1) * P],
                                           vw[h][:, j, :], start=True, stop=True)
                        mm.then_inc(dup_ready, 1)
                pairs(pe, body)

            @block.scalar
            def _(act):
                act.sem_inc(val_ready, 2)

                def body(t, last):
                    for h in (0, 1):
                        n = 2 * t + h + 1
                        act.wait_ge(dup_ready, n + 2)
                        wait_past(act, scattered[h], B * 16 * t)
                        act.activation(val[h][:, :, :], dup[h][:, :, :], ACT.Copy).then_inc(val_ready, 1)
                pairs(act, body)

            @block.vector
            def _(dve):
                ga.order(dve, 0, 0)
                ga.order(dve, 0, 1)
                dve.sem_inc(same_ready, 2)

                def body(t, last):
                    for h in (0, 1):
                        n = 2 * t + h + 1
                        cols = bass.ds(t * 2 * B + h * B, B)
                        dve.wait_ge(rows_ready[h], 32 * (t + 1))
                        dve.tensor_tensor(tiles3(oht[h][:, :]), tiles3(drow[h][:, :]),
                                          over(k.win_node[:, cols], P), ALU.is_equal).then_inc(oht_ready, 1)
                        dve.wait_ge(dup_ready, n)
                        dve.tensor_tensor(tiles3(same[h][:, :]), tiles3(srow[h][:, :]),
                                          over(k.src_f[:, cols], P), ALU.is_equal).then_inc(same_ready, 1)
                        dve.wait_ge(same_ready, n + 2)
                        dve.tensor_tensor(tiles3(rank[:, :]), tiles3(same[h][:, :]),
                                          rows_over(k.row1[:, :], B), ALU.mult).then_inc(rank_done, 1)
                        dve.wait_ge(rank_done, n)
                        dve.tensor_reduce(s[:, 0, :], tiles3(rank[:, :]), AX, ALU.max).then_inc(last_done, 1)
                        dve.wait_ge(last_done, n)
                        dve.tensor_scalar(s[:, 1, :], s[:, 0, :], k.col1[:, :], None,
                                          ALU.is_equal).then_inc(stands_done, 1)
                        dve.wait_ge(stands_done, n)
                        dve.tensor_tensor(s[:, 2, :], s[:, 1, :], k.src_sp[:, cols],
                                          ALU.mult).then_inc(moved_done, 1)
                        dve.wait_ge(moved_done, n)
                        wait_past(dve, scattered[h], B * 16 * t)
                        dve.tensor_scalar(sidx[h][:, :], s[:, 2, :], k.spare_row[:, :], None,
                                          ALU.add).then_inc(sidx_ready, 1)
                        dve.wait_ge(ga.gathered[h], B * 16 * (t + 1))
                        dve.wait_ge(wc_ready, n + 2)
                        dve.tensor_tensor(prod[:, :, :], g[h][:, :, 0:D], wc[h][:, :, 0:D],
                                          ALU.mult).then_inc(prod_done, 1)
                        dve.tensor_tensor(s[:, 3, :], g[h][:, :, D], wc[h][:, :, D],
                                          ALU.mult).then_inc(norms_done, 1)
                        dve.wait_ge(norms_done, n)
                        if not last:
                            ga.order(dve, t + 1, h)
                        dve.tensor_reduce(s[:, 4, :], prod[:, :, :], AX, ALU.add).then_inc(dot_done, 1)
                        dve.tensor_scalar(s[:, 5, :], s[:, 3, :], 1e-8, None, ALU.max).then_inc(floor_done, 1)
                        dve.wait_ge(floor_done, n)
                        dve.reciprocal(s[:, 6, :], s[:, 5, :]).then_inc(recip_done, 1)
                        dve.wait_ge(recip_done, n)
                        dve.tensor_tensor(s[:, 7, :], s[:, 4, :], s[:, 6, :], ALU.mult).then_inc(sim_done, 1)
                        dve.wait_ge(sim_done, n)
                        dve.tensor_scalar(s[:, 8, :], s[:, 7, :], 0.0, k.coeff_s[:, 0:1], ALU.max, ALU.mult)
                        dve.tensor_scalar(s[:, 9, :], s[:, 7, :], 0.0, k.coeff_s[:, 1:2], ALU.min,
                                          ALU.mult).then_inc(parts_done, 1)
                        dve.wait_ge(parts_done, n)
                        dve.tensor_tensor(s[:, 10, :], s[:, 8, :], s[:, 9, :], ALU.add).then_inc(signed_done, 1)
                        dve.wait_ge(signed_done, n)
                        dve.tensor_tensor(s[:, 11, :], s[:, 10, :], k.weight[:, cols],
                                          ALU.mult).then_inc(weight_done, 1)
                        dve.wait_ge(weight_done, n)
                        dve.tensor_tensor(vw[h][:, :, :], wc[h][:, :, 0:D], over(s[:, 11, :], D),
                                          ALU.mult).then_inc(vw_ready, 1)
                pairs(dve, body)


def accumulate(dve, k, ps, rows, t, h, n, added):
    for j in range(B):
        base = dve.value_load(k.dst_i[0:1, bass.ds(t * 2 * B + h * B + j, 1)], min_val=0, max_val=N)
        dve.wait_ge(added[j - 1], n if j else n + 1)
        acc = k.accT[0:rows, bass.ds(base, P)]
        dve.tensor_tensor(acc, acc, ps[0:rows, j, :], ALU.add).then_inc(added[j], 1)


def edge1(nc, k):
    with Ctx(nc, "edge1_") as c:
        g = [c.sb(f"src_rows{h}", [P, B, D]) for h in (0, 1)]
        ea = [c.sb(f"edge_attr{h}", [32, ROWS]) for h in (0, 1)]
        oh = [c.sb(f"onehot{h}", [P, B, P]) for h in (0, 1)]
        msg = [c.sb(f"msg{h}", [P, B, D]) for h in (0, 1)]
        m = [c.ps(f"msg_ps{h}", [P, B, D]) for h in (0, 1)]
        sp_ = [c.ps(f"sums_ps{h}", [D, B, P]) for h in (0, 1)]
        ga = Gather(c, k, k.t_h, D, lambda h, j: g[h][:, j, :])
        ea_ready = [c.sem(f"edge_attr_loaded{h}") for h in (0, 1)]
        oh_ready, m_ready, msg_ready, sums_ready = c.sems(
            "onehot_ready", "msg_in_psum", "msg_ready", "sums_in_psum")
        added = [c.sem(f"added{j}") for j in range(B)]
        with nc.Block() as block:
            @block.sync
            def _(sp):
                sp.dma_start(ea[0][:, :], k.ea32[0]).then_inc(ea_ready[0], 16)
                sp.dma_start(ea[1][:, :], k.ea32[1]).then_inc(ea_ready[1], 16)

                def body(t, last):
                    if not last:
                        for h in (0, 1):
                            sp.wait_ge(m_ready, 2 * t + h + 1)
                            sp.dma_start(ea[h][:, :], k.ea32[bass.ds(2 * t + 2 + h, 1)].rearrange("a f e -> (a f) e")
                                         ).then_inc(ea_ready[h], 16)
                pairs(sp, body)

            @block.gpsimd
            def _(pool):
                ga.loop(nc, pool)

            @block.tensor
            def _(pe):
                def messages(n, h, tt):
                    pe.wait_ge(msg_ready, n)
                    pe.wait_ge(ea_ready[h], 16 * tt)
                    pe.wait_ge(ga.gathered[h], B * 16 * tt)
                    pe.matmul(m[h][:, :, :], k.ident[:, :], g[h][:, :, :], start=True, stop=False)
                    for j in range(B):
                        mm = pe.matmul(m[h][:, j, :], ea[h][:, j * P:(j + 1) * P], k.We[:, :],
                                       start=False, stop=(j == B - 1))
                    mm.then_inc(m_ready, 1)

                pe.sem_inc(sums_ready, 2)
                messages(1, 0, 1)

                def body(t, last):
                    for h in (0, 1):
                        n = 2 * t + h + 1
                        if not (last and h):
                            messages(n + 1, 1 - h, t + 1 + h)
                        pe.wait_ge(added[B - 1], n)
                        pe.wait_ge(oh_ready, n)
                        pe.wait_ge(msg_ready, n + 2)
                        for j in range(B):
                            mm = pe.matmul(sp_[h][:, j, :], msg[h][:, j, :], oh[h][:, j, :],
                                           start=True, stop=True)
                        mm.then_inc(sums_ready, 1)
                pairs(pe, body)

            @block.scalar
            def _(act):
                act.sem_inc(msg_ready, 2)

                def body(t, last):
                    for h in (0, 1):
                        n = 2 * t + h + 1
                        act.wait_ge(m_ready, n)
                        act.wait_ge(sums_ready, n)
                        act.activation(msg[h][:, :, :], m[h][:, :, :], ACT.Relu).then_inc(msg_ready, 1)
                pairs(act, body)

            @block.vector
            def _(dve):
                ga.order(dve, 0, 0)
                ga.order(dve, 0, 1)
                dve.sem_inc(added[B - 1], 2)
                onehot(dve, k, oh[0][:, :, :], 0, 0).then_inc(oh_ready, 1)

                def body(t, last):
                    for h in (0, 1):
                        n = 2 * t + h + 1
                        if not (last and h):
                            onehot(dve, k, oh[1 - h][:, :, :], t + h, 1 - h).then_inc(oh_ready, 1)
                        if not last:
                            dve.wait_ge(m_ready, n)
                            ga.order(dve, t + 1, h)
                        dve.wait_ge(sums_ready, n + 2)
                        accumulate(dve, k, sp_[h], D, t, h, n, added)
                pairs(dve, body)


def edge2(nc, k):
    with Ctx(nc, "edge2_") as c:
        cat = [c.sb(f"cat{h}", [P, B, D]) for h in (0, 1)]
        ea = [c.sb(f"edge_attr{h}", [D, ROWS]) for h in (0, 1)]
        oh = [c.sb(f"onehot{h}", [P, B, P]) for h in (0, 1)]
        msg = [c.sb(f"msg{h}", [P, B, D + 1]) for h in (0, 1)]
        catT = c.sb("cat_t", [D, ROWS])
        junk = c.sb("squares", [P, 2, B, D])
        st = c.sb("stat", [P, 6, B])
        he = c.sb("he_pre", [P, B, HALF])
        he2 = c.sb("he_pre2", [P, B, HALF])
        u, u2 = c.sb("u", [P, B, D]), c.sb("u2", [P, B, D])
        hep = c.ps("he_ps", [P, B, P])
        catTp = c.ps("cat_t_ps", [D, ROWS])
        rp = c.ps("msg_ps", [P, B, P])
        sums = c.ps("sums_ps", [D + 1, B, P])
        ga = Gather(c, k, k.t_hn, HALF, lambda h, j: cat[h][:, j, 0:HALF])
        ea_ready = [c.sem(f"edge_attr_loaded{h}") for h in (0, 1)]
        (hep_ready, sq1, std1_ready, inv1, he_sc, he_b, cat_ready, catTp_ready, catT_ready, rp_ready,
         sq2, std2_ready, inv2, u_sc, u_b, oh_ready, msg_ready, sums_ready, ones_ready) = c.sems(
            "he_in_psum", "squares1_done", "std1_ready", "inverse1_done", "he_scaled", "he_shifted",
            "cat_ready", "cat_t_in_psum", "cat_t_ready", "msg_in_psum", "squares2_done", "std2_ready",
            "inverse2_done", "msg_scaled", "msg_shifted", "onehot_ready", "msg_ready", "sums_in_psum",
            "ones_ready")
        added = [c.sem(f"added{j}") for j in range(B)]

        def sweep(engine, body):
            body(0, True, False)
            with engine.Fori(1, PAIRS - 1) as t:
                body(t, False, False)
            body(PAIRS - 1, False, True)

        with nc.Block() as block:
            @block.sync
            def _(sp):
                sp.dma_start(ea[0][:, :], k.ea64[0]).then_inc(ea_ready[0], 16)
                sp.dma_start(ea[1][:, :], k.ea64[1]).then_inc(ea_ready[1], 16)

                def body(t, last):
                    if not last:
                        for h in (0, 1):
                            sp.wait_ge(hep_ready, 2 * t + h + 1)
                            sp.dma_start(ea[h][:, :], k.ea64[bass.ds(2 * t + 2 + h, 1)].rearrange("a f e -> (a f) e")
                                         ).then_inc(ea_ready[h], 16)
                pairs(sp, body)

            @block.gpsimd
            def _(pool):
                ga.loop(nc, pool)

            @block.tensor
            def _(pe):
                def edge_part(h, tt):
                    pe.wait_ge(ea_ready[h], 16 * tt)
                    for j in range(B):
                        mm = pe.matmul(hep[:, j, 0:HALF + D], ea[h][:, j * P:(j + 1) * P], k.eR[:, :],
                                       start=True, stop=True)
                    mm.then_inc(hep_ready, 1)

                def sum_up(n, h):
                    pe.wait_ge(msg_ready, n)
                    for j in range(B):
                        mm = pe.matmul(sums[:, j, :], msg[h][:, j, :], oh[h][:, j, :], start=True, stop=True)
                    mm.then_inc(sums_ready, 1)

                edge_part(0, 1)
                pe.wait_ge(ones_ready, 1)

                def body(t, first, last):
                    for h in (0, 1):
                        n = 2 * t + h + 1
                        pe.wait_ge(ga.gathered[h], B * 16 * (t + 1))
                        pe.wait_ge(cat_ready, n)
                        for j in range(B):
                            if j == 0:
                                mm = pe.matmul(catTp[:, 0:P], cat[h][:, 0, :], k.ident[:, :],
                                               start=True, stop=True)
                            else:
                                mm = pe.transpose(catTp[:, j * P:(j + 1) * P], cat[h][:, j, :], k.ident[:, :])
                        mm.then_inc(catTp_ready, 1)
                        if not (last and h):
                            edge_part(1 - h, t + 1 + h)
                        pe.wait_ge(catT_ready, n)
                        if not (first and h == 0):
                            pe.wait_ge(msg_ready, n - 1)
                        for j in range(B):
                            mm = pe.matmul(rp[:, j, :], catT[:, j * P:(j + 1) * P], k.rR[:, :],
                                           start=True, stop=True)
                        mm.then_inc(rp_ready, 1)
                        if not (first and h == 0):
                            if not (first and h == 1):
                                pe.wait_ge(added[B - 1], n)
                            sum_up(n - 1, 1 - h)
                sweep(pe, body)
                pe.wait_ge(added[B - 1], BATCHES + 1)
                sum_up(BATCHES, 1)

            @block.scalar
            def _(act):
                def root(ps, q, n, sq, ready):
                    for j in range(B):
                        a = act.activation(junk[:, q, j, :], ps[:, j, :], ACT.Square,
                                           accum_out=st[:, 3 * q, j:j + 1])
                    a.then_inc(sq, 1)
                    act.wait_ge(sq, n)
                    act.activation(st[:, 3 * q + 1, :], st[:, 3 * q, :], ACT.Sqrt, bias=k.eps[:, :],
                                   scale=1.0 / D).then_inc(ready, 1)

                act.wait_ge(hep_ready, 1)
                root(hep[:, :, HALF:HALF + D], 0, 1, sq1, std1_ready)

                def body(t, first, last):
                    for h in (0, 1):
                        n = 2 * t + h + 1
                        act.wait_ge(catTp_ready, n)
                        act.activation(catT[:, :], catTp[:, :], ACT.Copy).then_inc(catT_ready, 1)
                        if not (last and h):
                            act.wait_ge(hep_ready, n + 1)
                            root(hep[:, :, HALF:HALF + D], 0, n + 1, sq1, std1_ready)
                        act.wait_ge(rp_ready, n)
                        root(rp[:, :, D:2 * D], 1, n, sq2, std2_ready)
                sweep(act, body)

            @block.vector
            def _(dve):
                ga.order(dve, 0, 0)
                ga.order(dve, 0, 1)
                dve.sem_inc(added[B - 1], 2)
                dve.memset(msg[0][:, :, D], 1.0)
                dve.memset(msg[1][:, :, D], 1.0).then_inc(ones_ready, 1)

                def edge_row(n, h):
                    dve.wait_ge(std1_ready, n)
                    dve.reciprocal(st[:, 2, :], st[:, 1, :]).then_inc(inv1, 1)
                    dve.wait_ge(inv1, n)
                    dve.tensor_tensor(he[:, :, :], hep[:, :, 0:HALF], over(st[:, 2, :], HALF),
                                      ALU.mult).then_inc(he_sc, 1)
                    dve.wait_ge(he_sc, n)
                    dve.tensor_tensor(he2[:, :, :], he[:, :, :], rows_over(k.ec[:, :], B),
                                      ALU.add).then_inc(he_b, 1)
                    dve.wait_ge(he_b, n)
                    dve.scalar_tensor_tensor(cat[h][:, :, HALF:D], he2[:, :, :], 0.01, he2[:, :, :],
                                             ALU.mult, ALU.max).then_inc(cat_ready, 1)

                def message(n, h, t):
                    onehot(dve, k, oh[h][:, :, :], t, h).then_inc(oh_ready, 1)
                    dve.wait_ge(std2_ready, n)
                    dve.reciprocal(st[:, 5, :], st[:, 4, :]).then_inc(inv2, 1)
                    dve.wait_ge(inv2, n)
                    dve.tensor_tensor(u[:, :, :], rp[:, :, 0:D], over(st[:, 5, :], D),
                                      ALU.mult).then_inc(u_sc, 1)
                    dve.wait_ge(u_sc, n)
                    dve.tensor_tensor(u2[:, :, :], u[:, :, :], rows_over(k.rc[:, :], B),
                                      ALU.add).then_inc(u_b, 1)
                    dve.wait_ge(u_b, n)
                    dve.scalar_tensor_tensor(msg[h][:, :, 0:D], u2[:, :, :], 0.01, u2[:, :, :],
                                             ALU.mult, ALU.max).then_inc(msg_ready, 1)

                def add(n, h, t):
                    dve.wait_ge(sums_ready, n)
                    accumulate(dve, k, sums, D + 1, t, h, n, added)

                def body(t, first, last):
                    for h in (0, 1):
                        n = 2 * t + h + 1
                        edge_row(n, h)
                        if not first:
                            add(n - 2, h, t - 1)
                        if not (first and h == 0):
                            message(n - 1, 1 - h, t - 1 + h)
                        if not last:
                            dve.wait_ge(catTp_ready, n)
                            ga.order(dve, t + 1, h)
                sweep(dve, body)
                add(BATCHES - 1, 0, PAIRS - 1)
                message(BATCHES, 1, PAIRS - 1)
                add(BATCHES, 1, PAIRS - 1)


def edge3a(nc, k):
    with Ctx(nc, "edge3a_") as c:
        hc = [c.sb(f"both_ends{h}", [P, B, 2 * D]) for h in (0, 1)]
        win = [c.sb(f"window{h}", [P, B, D]) for h in (0, 1)]
        drow = [c.sb(f"dst_row{h}", [P, ROWS], I32) for h in (0, 1)]
        oht = [c.sb(f"onehot_t{h}", [P, ROWS]) for h in (0, 1)]
        hcT = [c.sb(f"both_ends_t{h}", [P, ROWS]) for h in (0, 1)]
        rl = [c.sb(f"relu{h}", [P, HP, ROWS]) for h in (0, 1)]
        scs = c.sb("scores", [P, H, B])
        scT = [c.sb(f"scores_t{h}", [H * B, P]) for h in (0, 1)]
        hdp = c.ps("dst_rows_ps", [P, B, D])
        hcTp = c.ps("both_ends_t_ps", [P, ROWS])
        zp = [c.ps(f"z_ps{j}", [P, 512]) for j in range(HP)]
        scp = c.ps("scores_ps", [P, H, B])
        scTp = c.ps("scores_t_ps", [H * B, P])
        ga = Gather(c, k, k.t_h3, D, lambda h, j: hc[h][:, j, 0:D])
        rows_ready = [c.sem(f"rows_loaded{h}") for h in (0, 1)]
        win_ready = [c.sem(f"window_loaded{h}") for h in (0, 1)]
        kept = [c.sem(f"rows_kept{h}") for h in (0, 1)]
        stored = [c.sem(f"scores_stored{h}") for h in (0, 1)]
        z_ready = [c.sem(f"z_in_psum{j}") for j in range(HP)]
        relu_done = [c.sem(f"relu_done{j}") for j in range(HP)]
        oht_ready, hd_ready, hc_ready, hcTp_ready, hcT_ready, sc_ready, scs_ready, scTp_ready, scT_ready = c.sems(
            "onehot_ready", "dst_rows_in_psum", "both_ends_ready", "both_ends_t_in_psum",
            "both_ends_t_ready", "scores_in_psum", "scores_ready", "scores_t_in_psum", "scores_t_ready")
        with nc.Block() as block:
            @block.sync
            def _(sp):
                def load(t, h):
                    n = 2 * t + h + 1
                    sp.wait_ge(oht_ready, n)
                    sp.dma_start(drow[h][:, :], k.dst_row[bass.ds(2 * t + h, 1), :].to_broadcast([P, ROWS])
                                 ).then_inc(rows_ready[h], 16)
                    sp.wait_ge(hd_ready, n)
                    for j in range(B):
                        base = sp.value_load(k.dst_i[0:1, bass.ds(t * 2 * B + h * B + j, 1)],
                                             min_val=0, max_val=N)
                        sp.dma_start(win[h][:, j, :], k.t_h3[bass.ds(base, P), :]
                                     ).then_inc(win_ready[h], 16)

                load(0, 0)

                def body(t, last):
                    for h in (0, 1):
                        if not (last and h):
                            load(t + h, 1 - h)
                        sp.wait_ge(ga.gathered[h], B * 16 * (t + 1))
                        sp.dma_start(k.kept[bass.ds(2 * t + h, 1)].rearrange("a p (b d) -> (a p) b d", b=B),
                                     hc[h][:, :, 0:D]).then_inc(kept[h], 16)
                pairs(sp, body)
                for h in (0, 1):
                    sp.wait_ge(kept[h], 16 * PAIRS)

            @block.gpsimd
            def _(pool):
                ga.loop(nc, pool)

            @block.tensor
            def _(pe):
                pe.sem_inc(hd_ready, 2)

                def ends(n, h, tt):
                    pe.wait_ge(win_ready[h], B * 16 * tt)
                    pe.wait_ge(oht_ready, n + 2)
                    for j in range(B):
                        mm = pe.matmul(hdp[:, j, :], oht[h][:, j * P:(j + 1) * P], win[h][:, j, :],
                                       start=True, stop=True)
                    mm.then_inc(hd_ready, 1)

                def turn(n, h):
                    pe.wait_ge(hc_ready, n)
                    for j in range(B):
                        mm = pe.transpose(hcTp[:, j * P:(j + 1) * P], hc[h][:, j, :], k.ident[:, :])
                    mm.then_inc(hcTp_ready, 1)

                def scores(n, h):
                    pe.wait_ge(hcT_ready, n)
                    for q in range(2):
                        for j in range(HP):
                            pe.wait_ge(relu_done[j], 2 * n - 1 + q)
                            pe.matmul(zp[j][:, :], k.Wlr[:, j * P:(j + 1) * P],
                                      hcT[h][:, q * 512:(q + 1) * 512], start=True,
                                      stop=True).then_inc(z_ready[j], 1)
                        if q == 0:
                            yield

                def dots(n, h):
                    pe.wait_ge(relu_done[HP - 1], 2 * n + 1)
                    for i in range(B):
                        cols = slice(i * P, (i + 1) * P)
                        pe.matmul(scp[:, :, i], hcT[h][:, cols], k.Watt[:, :], start=True, stop=False)
                        for j in range(HP):
                            mm = pe.matmul(scp[:, :, i], rl[h][:, j, cols], k.att_blk[:, j, :],
                                           start=False, stop=(j == HP - 1))
                    mm.then_inc(sc_ready, 1)

                def turn_scores(n):
                    pe.wait_ge(scT_ready, n)
                    pe.wait_ge(scs_ready, n)
                    pe.matmul(scTp[:, :], scs[:, :, :].rearrange("p h b -> p (h b)"), k.ident[:, :],
                              start=True, stop=True).then_inc(scTp_ready, 1)

                ends(1, 0, 1)
                turn(1, 0)

                def body(t, first, last):
                    for h in (0, 1):
                        n = 2 * t + h + 1
                        more = not (last and h)
                        if more:
                            ends(n + 1, 1 - h, t + 1 + h)
                        z = scores(n, h)
                        next(z)
                        if more:
                            turn(n + 1, 1 - h)
                        for _ in z:
                            pass
                        if not (first and h == 0):
                            turn_scores(n - 1)
                        dots(n, h)
                body(0, True, False)
                with pe.Fori(1, PAIRS - 1) as t:
                    body(t, False, False)
                body(PAIRS - 1, False, True)
                turn_scores(BATCHES)

            @block.scalar
            def _(act):
                for j in range(HP):
                    act.sem_inc(relu_done[j], 1)

                def store(n, h, at):
                    act.wait_ge(scT_ready, n + 1)
                    act.dma_start(k.scores_d[bass.ds(at, 1)].rearrange("a q e -> (a q) e"),
                                  scT[h][:, :]).then_inc(stored[h], 16)

                def body(t, first, last):
                    for h in (0, 1):
                        n = 2 * t + h + 1
                        for q in range(2):
                            for j in range(HP):
                                act.wait_ge(z_ready[j], 2 * n - 1 + q)
                                act.activation(rl[h][:, j, q * 512:(q + 1) * 512], zp[j][:, :],
                                               ACT.Relu).then_inc(relu_done[j], 1)
                        if not (first and h == 0):
                            store(n - 1, 1 - h, 2 * t + h - 1)
                body(0, True, False)
                with act.Fori(1, PAIRS - 1) as t:
                    body(t, False, False)
                body(PAIRS - 1, False, True)
                store(BATCHES, 1, BATCHES - 1)
                for h in (0, 1):
                    act.wait_ge(stored[h], 16 * PAIRS)

            @block.vector
            def _(dve):
                ga.order(dve, 0, 0)
                ga.order(dve, 0, 1)
                dve.sem_inc(oht_ready, 2)
                dve.sem_inc(scT_ready, 1)

                def onehot_t(h, t):
                    dve.wait_ge(rows_ready[h], 16 * (t + 1))
                    dve.tensor_tensor(tiles3(oht[h][:, :]), tiles3(drow[h][:, :]),
                                      over(k.win_node[:, bass.ds(t * 2 * B + h * B, B)], P),
                                      ALU.is_equal).then_inc(oht_ready, 1)

                def ends(n, h, t, more):
                    dve.wait_ge(hd_ready, n + 2)
                    dve.wait_ge(ga.gathered[h], B * 16 * (t + 1))
                    dve.tensor_copy(hc[h][:, :, D:2 * D], hdp[:, :, :]).then_inc(hc_ready, 1)
                    if more:
                        onehot_t(1 - h, t + h)
                    dve.wait_ge(hcTp_ready, n)
                    dve.tensor_copy(hcT[h][:, :], hcTp[:, :]).then_inc(hcT_ready, 1)

                def turned(n, h, t):
                    dve.wait_ge(scTp_ready, n)
                    dve.tensor_copy(scT[h][:, :], scTp[:, :]).then_inc(scT_ready, 1)

                onehot_t(0, 0)
                ends(1, 0, 0, True)

                def body(t, first, last):
                    for h in (0, 1):
                        n = 2 * t + h + 1
                        if not (last and h):
                            ends(n + 1, 1 - h, t + h, not (last and h == 0))
                        if not last:
                            dve.wait_ge(kept[h], 16 * (t + 1))
                            ga.order(dve, t + 1, h)
                        if not (first and h == 0):
                            if not first and not (isinstance(t, int) and t - 1 + h == 0):
                                dve.wait_ge(stored[1 - h], 16 * (t - 1 + h))
                            turned(n - 1, 1 - h, t)
                        dve.wait_ge(sc_ready, n)
                        dve.tensor_copy(scs[:, :, :], scp[:, :, :]).then_inc(scs_ready, 1)
                body(0, True, False)
                body(1, False, False)
                with dve.Fori(2, PAIRS - 1) as t:
                    body(t, False, False)
                body(PAIRS - 1, False, True)
                dve.wait_ge(stored[1], 16 * (PAIRS - 1))
                turned(BATCHES, 1, 0)


def softmax(nc, k):
    Q = BATCHES
    sc = k.accT[0:Q, 0:H * ROWS].rearrange("p (h e) -> p h e", h=H)
    with Ctx(nc, "softmax_") as c:
        mx = c.sb("running", [Q, H, ROWS])
        ids = c.sb("dst_seq", [Q, ROWS + 2], I32)
        start = c.sb("starts", [Q, ROWS])
        end = c.sb("ends", [Q, ROWS])
        keep = c.sb("keeps", [Q, ROWS])
        src = c.sb("src", [Q, ROWS], I32)
        loop = c.sb("loop", [Q, 1, ROWS])
        times = c.sb("times", [Q, 1, ROWS])
        edge = c.sb("edge", [Q, 2, H])
        edgeT = c.sb("edge_t", [H, 2, Q])
        carryT = c.sb("carry_t", [H, Q + 2])
        carry = c.sb("carry", [Q, H])
        loaded, step_s, edge_ready, edgeT_ready, carryT_ready, carry_ready, m_ready, p_ready, a_ready, stored = c.sems(
            "loaded", "dve_step", "edge_ready", "edge_t_ready", "carry_t_ready", "carry_ready",
            "shifted_ready", "exp_ready", "alpha_ready", "alpha_stored")
        ps = c.ps("carry_ps", [P, 512])
        with nc.Block() as block:
            @block.sync
            def _(sp):
                sp.dma_start(sc, k.scores_d.rearrange("q (h b) e -> q h (b e)", h=H)).then_inc(loaded, 16)
                sp.dma_start(ids[:, 0:ROWS], k.dst_seq[0:Q * ROWS].rearrange("(q e) -> q e", q=Q)
                             ).then_inc(loaded, 16)
                sp.dma_start(ids[:, ROWS:ROWS + 2],
                             k.dst_seq[ROWS:ROWS + Q * ROWS].rearrange("(q e) -> q e", q=Q)[:, 0:2]
                             ).then_inc(loaded, 16)
                sp.dma_start(src[:, :], k.src_row[:, :]).then_inc(loaded, 16)
                sp.wait_ge(a_ready, 1)
                sp.dma_start(k.scores_d.rearrange("q (h b) e -> q h (b e)", h=H), mx[:, :, :]
                             ).then_inc(stored, 16)
                sp.wait_ge(stored, 16)

            @block.tensor
            def _(pe):
                for i, (a, o) in enumerate([(1, 0), (H, 0), (H, 2), (H, 0), (H, 2)]):
                    pe.wait_ge(edge_ready, i + 1)
                    pe.transpose(ps[0:a, 0:Q], edge[:, 0, 0:a], k.ident[0:Q, 0:Q])
                    pe.transpose(ps[0:a, P:P + Q], edge[:, 1, 0:a], k.ident[0:Q, 0:Q]
                                 ).then_inc(edgeT_ready, 1)
                    pe.wait_ge(carryT_ready, i + 1)
                    pe.transpose(ps[0:Q, 256:256 + a], carryT[0:a, o:o + Q], k.ident[0:a, 0:a]
                                 ).then_inc(carry_ready, 1)

            @block.scalar
            def _(act):
                act.wait_ge(m_ready, 1)
                act.activation(sc, mx[:, :, :], ACT.Exp).then_inc(p_ready, 1)

            @block.vector
            def _(dve):
                step = Chain(dve, step_s)
                passes = [0]

                def scan(out, data, flags, op0, op1, nothing, back, heads=H):
                    passes[0] += 1
                    way = slice(None, None, -1) if back else slice(None)

                    def run(initial):
                        for h in range(heads):
                            last = dve.tensor_tensor_scan(out[:, h, way], flags[:, way], data[:, h, way],
                                                          initial(h), op0, op1)
                        step(last)
                    run(lambda h: nothing)
                    step(dve.tensor_copy(edge[:, 0, 0:heads], out[:, :, 0 if back else ROWS - 1]))
                    step(dve.tensor_reduce(carry[:, 0:1], flags[:, :], AX, ALU.min))
                    dve.tensor_copy(edge[:, 1, 0:heads], carry[:, 0:1].to_broadcast([Q, heads])).then_inc(edge_ready, 1)
                    dve.wait_ge(edgeT_ready, passes[0])
                    step(dve.tensor_copy(edgeT[0:heads, 0, :], ps[0:heads, 0:Q]))
                    step(dve.tensor_copy(edgeT[0:heads, 1, :], ps[0:heads, P:P + Q]))
                    step(dve.memset(carryT[:, :], nothing))
                    dve.tensor_tensor_scan(carryT[0:heads, 1:Q + 1][:, way], edgeT[0:heads, 1, way], edgeT[0:heads, 0, way],
                                           nothing, op0, op1).then_inc(carryT_ready, 1)
                    dve.wait_ge(carry_ready, passes[0])
                    step(dve.tensor_copy(carry[:, 0:heads], ps[0:Q, 256:256 + heads]))
                    run(lambda h: carry[:, h:h + 1])

                dve.wait_ge(loaded, 64)
                step(dve.tensor_tensor(keep[:, :], ids[:, 1:ROWS + 1], ids[:, 0:ROWS], ALU.is_equal))
                step(dve.tensor_tensor(start[:, :], ids[:, 1:ROWS + 1], ids[:, 0:ROWS], ALU.not_equal))
                step(dve.tensor_scalar(start[:, :], start[:, :], FAR, None, ALU.mult))
                step(dve.tensor_tensor(end[:, :], ids[:, 1:ROWS + 1], ids[:, 2:ROWS + 2], ALU.not_equal))
                step(dve.tensor_scalar(end[:, :], end[:, :], FAR, None, ALU.mult))
                step(dve.tensor_tensor(loop[:, 0, :], ids[:, 1:ROWS + 1], src[:, :], ALU.is_equal))
                scan(times, loop, keep, ALU.mult, ALU.add, 0.0, False, 1)
                step(dve.tensor_scalar(times[:, :, :], times[:, :, :], 1.0, None, ALU.is_equal))
                step(dve.tensor_tensor(times[:, :, :], times[:, :, :], loop[:, :, :], ALU.mult))
                step(dve.tensor_scalar(times[:, :, :], times[:, :, :], 1.0, None, ALU.add))
                scan(mx, sc, start, ALU.add, ALU.max, FAR, False)
                scan(mx, mx, end, ALU.add, ALU.max, FAR, True)
                dve.tensor_tensor(mx[:, :, :], sc, mx[:, :, :], ALU.subtract).then_inc(m_ready, 1)
                dve.wait_ge(p_ready, 1)
                step(dve.tensor_tensor(sc, sc, times[:, :, :].to_broadcast([Q, H, ROWS]), ALU.mult))
                scan(mx, sc, keep, ALU.mult, ALU.add, 0.0, False)
                scan(mx, mx, end, ALU.add, ALU.max, FAR, True)
                step(dve.tensor_scalar(mx[:, :, :], mx[:, :, :], 1e-16, float(H), ALU.add, ALU.mult))
                step(dve.reciprocal(mx[:, :, :], mx[:, :, :]))
                dve.tensor_tensor(mx[:, :, :], mx[:, :, :], sc, ALU.mult).then_inc(a_ready, 1)


def edge3b(nc, k):
    DVE_T, POOL_T, ACT_T = range(0, 2), range(2, 5), range(5, 8)
    with Ctx(nc, "edge3b_") as c:
        raw = [c.sb(f"alpha_t{h}", [H * B, P]) for h in (0, 1)]
        al = [c.sb(f"alpha{h}", [P, H, B]) for h in (0, 1)]
        st = [c.sb(f"src_rows{h}", [P, B, D]) for h in (0, 1)]
        hp = [c.sb(f"weighted{h}", [P, B, H, D]) for h in (0, 1)]
        oh = [c.sb(f"onehot{h}", [P, B, P]) for h in (0, 1)]
        alp = [c.ps(f"alpha_ps{h}", [P, H * B]) for h in (0, 1)]
        sums = [c.ps(f"sums_ps{i}", [P, HP, P]) for i in range(4)]
        raw_ready = [c.sem(f"alpha_loaded{h}") for h in (0, 1)]
        st_ready = [c.sem(f"rows_loaded{h}") for h in (0, 1)]
        alp_ready, al_ready, hp_dve, hp_pool, hp_act, oh_ready = c.sems(
            "alpha_in_psum", "alpha_ready", "weighted_by_vector", "weighted_by_gpsimd",
            "weighted_by_scalar", "onehot_ready")
        summed = [c.sem(f"sums_in_psum{j}") for j in range(B)]
        added = [c.sem(f"added{j}") for j in range(B)]
        starts = [0, 0, 0, 0, 1, 1, 1, 2]

        def weigh(engine, h, tiles):
            a, b = tiles[0], tiles[-1] + 1
            rows = st[h][:, a:b, :].unsqueeze(2).to_broadcast([P, b - a, H, D])
            weights = al[h][:, :, a:b].rearrange("p h b -> p b h").unsqueeze(3).to_broadcast([P, b - a, H, D])
            return engine.tensor_tensor(hp[h][:, a:b, :, :], rows, weights, ALU.mult)

        with nc.Block() as block:
            @block.sync
            def _(sp):
                def body(t, last):
                    for h in (0, 1):
                        n = 2 * t + h + 1
                        at = bass.ds(2 * t + h, 1)
                        sp.wait_ge(alp_ready, n)
                        sp.dma_start(raw[h][:, :], k.scores_d[at].rearrange("a q e -> (a q) e")
                                     ).then_inc(raw_ready[h], 16)
                        for used in (hp_dve, hp_pool, hp_act):
                            sp.wait_ge(used, n)
                        sp.dma_start(st[h][:, :, :], k.kept[at].rearrange("a p (b d) -> (a p) b d", b=B)
                                     ).then_inc(st_ready[h], 16)
                pairs(sp, body)

            @block.gpsimd
            def _(pool):
                pool.sem_inc(hp_pool, 2)

                def body(t, last):
                    for h in (0, 1):
                        n = 2 * t + h + 1
                        pool.wait_ge(st_ready[h], 16 * (t + 1))
                        pool.wait_ge(summed[B - 1], n)
                        pool.wait_ge(al_ready, n)
                        weigh(nc.gpsimd, h, POOL_T).then_inc(hp_pool, 1)
                pairs(pool, body)

            @block.scalar
            def _(act):
                act.sem_inc(hp_act, 2)

                def body(t, last):
                    for h in (0, 1):
                        n = 2 * t + h + 1
                        act.wait_ge(st_ready[h], 16 * (t + 1))
                        act.wait_ge(summed[B - 1], n)
                        act.wait_ge(al_ready, n)
                        for j in ACT_T:
                            for a in range(H):
                                w = act.activation(hp[h][:, j, a, :], st[h][:, j, :], ACT.Copy,
                                                   scale=al[h][:, a, j:j + 1])
                        w.then_inc(hp_act, 1)
                pairs(act, body)

            @block.tensor
            def _(pe):
                pe.sem_inc(alp_ready, 2)
                pe.sem_inc(summed[B - 1], 2)

                def alphas(h, tt):
                    pe.wait_ge(raw_ready[h], 16 * tt)
                    pe.matmul(alp[h][:, :], raw[h][:, :], k.ident[0:H * B, 0:H * B], start=True,
                              stop=True).then_inc(alp_ready, 1)

                alphas(0, 1)

                def body(t, last):
                    for h in (0, 1):
                        n = 2 * t + h + 1
                        if not (last and h):
                            alphas(1 - h, t + 1 + h)
                        pe.wait_ge(oh_ready, n)
                        pe.wait_ge(hp_dve, n + 2)
                        for j in range(B):
                            if j == POOL_T[0]:
                                pe.wait_ge(hp_pool, n + 2)
                            if j == ACT_T[0]:
                                pe.wait_ge(hp_act, n + 2)
                            o = (j + 4) % B
                            pe.wait_ge(added[o], n + starts[o] - (j < 4))
                            for i in range(HP):
                                mm = pe.matmul(sums[j % 4][:, i, :],
                                               hp[h][:, j, 2 * i:2 * i + 2, :].rearrange("p a d -> p (a d)"),
                                               oh[h][:, j, :], start=True, stop=True)
                            mm.then_inc(summed[j], 1)
                pairs(pe, body)

            @block.vector
            def _(dve):
                dve.memset(k.accT[:, :], 0.0)
                for j in range(B):
                    if starts[j]:
                        dve.sem_inc(added[j], starts[j])
                dve.sem_inc(hp_dve, 2)
                acc3 = k.accT[:, :].rearrange("p (a w) -> p a w", a=HP)

                def prepare(n, h, t):
                    dve.wait_ge(alp_ready, n + 2)
                    dve.wait_ge(hp_pool, n)
                    dve.wait_ge(hp_act, n)
                    dve.tensor_copy(al[h][:, :, :].rearrange("p h b -> p (h b)"), alp[h][:, :]).then_inc(al_ready, 1)
                    onehot(dve, k, oh[h][:, :, :], t, h).then_inc(oh_ready, 1)
                    dve.wait_ge(st_ready[h], 16 * (t + 1))
                    dve.wait_ge(al_ready, n)
                    weigh(dve, h, DVE_T).then_inc(hp_dve, 1)

                prepare(1, 0, 0)

                def body(t, last):
                    for h in (0, 1):
                        n = 2 * t + h + 1
                        if not (last and h):
                            prepare(n + 1, 1 - h, t + h)
                        for j in range(B):
                            base = dve.value_load(k.dst_i[0:1, bass.ds(t * 2 * B + h * B + j, 1)],
                                                  min_val=0, max_val=N)
                            dve.wait_ge(summed[j], n + 2 if j == B - 1 else n)
                            dve.wait_ge(added[j - 1], n + starts[j - 1] if j else n + 1)
                            acc = acc3[:, :, bass.ds(base, P)]
                            dve.tensor_tensor(acc, acc, sums[j % 4][:, :, :], ALU.add).then_inc(added[j], 1)
                pairs(dve, body)


def build(nc, ins, out, stop=99):
    k = Kept()
    dram = lambda name, shape: nc.dram_tensor(name, shape, F32).ap()
    k.t_wh = dram("table_wh", (NPAD, WH))
    k.t_h = dram("table_h", (NPAD, D))
    k.t_hn = dram("table_hn", (NPAD, HALF))
    k.t_h3 = dram("table_h3", (NPAD, D))
    k.kept = dram("kept_rows", (BATCHES, P, B * D))
    k.scores_d = dram("scores_by_batch", (BATCHES, H * B, P))
    k.scatter_sums = [dram(f"scatter_sums{i}", (SROWS, D)) for i in range(TABLES)]
    k.dst_row, k.src_row, k.ea32, k.ea64, k.dst_seq = (
        ins["dst_row"], ins["src_row"], ins["ea32"], ins["ea64"], ins["dst_seq"])
    with Ctx(nc) as c:
        k.x = c.sb("x", [P, NB, D])
        k.h = c.sb("h", [P, NB, D])
        k.t1 = c.sb("t1", [P, NB, D])
        k.wh = c.sb("wh", [P, NB, WH])
        k.local = c.sb("local", [P, NB, D])
        k.accT = c.sb("accT", [P, HP * NPAD])
        k.src_i = c.sb("src_i", [P, TILES], I32)
        k.dst_i = c.sb("dst_i", [P, TILES], I32)
        k.src_f = c.sb("src_f", [P, TILES])
        k.dst_rel = c.sb("dst_rel", [P, TILES])
        k.win_node = c.sb("win_node", [P, TILES])
        k.src_sp = c.sb("src_sp", [P, TILES])
        k.weight = c.sb("weight", [P, TILES])
        k.ident = c.sb("ident", [P, P])
        k.row0 = c.sb("row0", [P, P])
        k.row1 = c.sb("row1", [P, P])
        k.col0 = c.sb("col0", [P, 1])
        k.col1 = c.sb("col1", [P, 1])
        k.spare_row = c.sb("spare_row", [P, 1])
        k.eps = c.sb("eps", [P, 1])
        k.zero_i = c.sb("zero_i", [P, 1], I32)
        k.zero_o = c.sb("zero_o", [P, 1], I32)
        k.zero_o2 = c.sb("zero_o2", [P, 1], I32)
        k.center = c.sb("center", [D, D])
        k.W0 = c.sb("W0", [D + 1, D])
        k.deg_coeff = c.sb("deg_coeff", [P, 2])
        k.coeff = c.sb("coeff", [P, 3])
        k.coeff_d = c.sb("coeff_d", [P, 3])
        k.coeff_e = c.sb("coeff_e", [P, 3])
        k.coeff_s = c.sb("coeff_s", [P, 3])
        k.scale = c.sb("scale", [P, 1])
        k.eps_gin = c.sb("eps_gin", [P, 1])
        k.eps1 = c.sb("eps1", [P, 1])
        k.We = c.sb("We", [32, D])
        k.be = c.sb("be", [P, D])
        k.W1 = c.sb("W1", [D, D])
        k.b1 = c.sb("b1", [D, 1])
        k.W2 = c.sb("W2", [D + 1, D])
        k.gamma = c.sb("gamma", [P, D])
        k.beta = c.sb("beta", [P, D])
        k.nlw = c.sb("nlw", [P, D])
        k.nlb = c.sb("nlb", [P, D])
        k.nW = c.sb("nW", [D + 1, HALF])
        k.elw = c.sb("elw", [D, 1])
        k.elb = c.sb("elb", [D, 1])
        k.eW = c.sb("eW", [D, HALF])
        k.eb = c.sb("eb", [P, HALF])
        k.rlw = c.sb("rlw", [D, 1])
        k.rlb = c.sb("rlb", [D, 1])
        k.rlw_row = c.sb("rlw_row", [P, D])
        k.rlb_row = c.sb("rlb_row", [P, D])
        k.rW = c.sb("rW", [D + 1, D])
        k.rb = c.sb("rb", [P, D])
        k.Wlr = c.sb("Wlr", [P, H * D])
        k.att_row = c.sb("att_row", [P, H * D])
        k.att_col = c.sb("att_col", [P, HP])
        k.bias3 = c.sb("bias3", [P, D])
        k.Wl_h = c.sb("Wl_h", [P, HP, D])
        k.Watt = c.sb("Watt", [P, H])
        k.att_blk = c.sb("att_blk", [P, HP, H])
        k.eWw = c.sb("eWw", [D, HALF])
        k.rWw = c.sb("rWw", [D, D])
        k.eR = c.sb("eR", [D, HALF + D])
        k.rR = c.sb("rR", [D, 2 * D])
        k.ec = c.sb("ec", [P, HALF])
        k.rc = c.sb("rc", [P, D])
        k.elb_col = c.sb("elb_col", [D, P])
        k.rlb_col = c.sb("rlb_col", [D, P])
        k.hT = k.accT[0:D + 1, NPAD:2 * NPAD]
        k.t2 = k.accT[:, 2 * NPAD:2 * NPAD + NB * D].rearrange("p (b d) -> p b d", b=NB)
        setup(nc, k, ins)
        node0(nc, k)
        edge0(nc, k)
        node1(nc, k)
        if stop > 1:
            edge1(nc, k)
            node2(nc, k)
        if stop > 2:
            edge2(nc, k)
            node3(nc, k)
        if stop > 3:
            edge3a(nc, k)
            softmax(nc, k)
            edge3b(nc, k)
            node4(nc, k, out)


def kernel(x, src, dst, edge_attr_32, edge_attr_64, edge_weight, edge_weight_n2, L0_gnn_W, L0_gnn_b,
           L0_gnn_deg_coeff, L0_gnn_coeff_param, L0_gnn_scale_param, L1_gnn_We, L1_gnn_be, L1_gnn_W1,
           L1_gnn_b1, L1_gnn_W2, L1_gnn_b2, L1_gnn_eps_gin, L1_gnn_gamma, L1_gnn_beta,
           L2_gnn_node_ln_w, L2_gnn_node_ln_b, L2_gnn_node_W, L2_gnn_node_b, L2_gnn_edge_ln_w,
           L2_gnn_edge_ln_b, L2_gnn_edge_W, L2_gnn_edge_b, L2_gnn_red_ln_w, L2_gnn_red_ln_b,
           L2_gnn_red_W, L2_gnn_red_b, L3_gnn_W_l, L3_gnn_W_r, L3_gnn_att, L3_gnn_bias):
    import concourse.bacc as _bacc
    from concourse.bass_utils import run_bass_kernel_spmd as _run

    def padded(a, rows, fill=0):
        a = np.asarray(a)
        out = np.full((rows,) + a.shape[1:], fill, a.dtype)
        out[:a.shape[0]] = a
        return out

    def by_tile(a, fill=0):
        return np.ascontiguousarray(padded(a, TILES * P, fill).reshape(TILES, P).T)

    def by_batch_t(a):
        a = padded(a, TILES * P)
        return np.ascontiguousarray(a.reshape(BATCHES, ROWS, a.shape[1]).transpose(0, 2, 1))

    def row(a):
        return np.ascontiguousarray(np.asarray(a).reshape(1, -1))

    def vec(a):
        return np.ascontiguousarray(np.asarray(a).reshape(-1))

    def col(a):
        return np.ascontiguousarray(np.asarray(a).reshape(-1, 1))

    seq = np.full((BATCHES + 1) * ROWS, -2, np.int32)
    seq[0] = -1
    seq[1:1 + BATCHES * ROWS] = padded(dst, TILES * P, N)
    arrays = {
        "x": padded(x, NPAD),
        "src_t": by_tile(src), "dst_t": by_tile(dst, N),
        "src_row": padded(src, TILES * P).reshape(BATCHES, ROWS),
        "dst_row": padded(dst, TILES * P, N).reshape(BATCHES, ROWS), "dst_seq": seq,
        "w_t": by_tile(edge_weight), "w2_t": by_tile(edge_weight_n2),
        "ea32": by_batch_t(edge_attr_32), "ea64": by_batch_t(edge_attr_64),
        "W0": L0_gnn_W, "b0": row(L0_gnn_b), "deg_coeff": vec(L0_gnn_deg_coeff),
        "coeff_param": vec(L0_gnn_coeff_param), "scale_param": vec(L0_gnn_scale_param),
        "We": L1_gnn_We, "be": vec(L1_gnn_be), "W1": L1_gnn_W1, "b1": col(L1_gnn_b1),
        "W2": L1_gnn_W2, "b2": row(L1_gnn_b2), "eps_gin": vec(L1_gnn_eps_gin),
        "gamma": vec(L1_gnn_gamma), "beta": vec(L1_gnn_beta),
        "nlw": vec(L2_gnn_node_ln_w), "nlb": vec(L2_gnn_node_ln_b),
        "nWT": np.asarray(L2_gnn_node_W).T, "nb": row(L2_gnn_node_b),
        "elw": col(L2_gnn_edge_ln_w), "elb": col(L2_gnn_edge_ln_b),
        "eWT": np.asarray(L2_gnn_edge_W).T, "eb": vec(L2_gnn_edge_b),
        "rlw": col(L2_gnn_red_ln_w), "rlb": col(L2_gnn_red_ln_b),
        "rlw_r": vec(L2_gnn_red_ln_w), "rlb_r": vec(L2_gnn_red_ln_b),
        "rWT": np.asarray(L2_gnn_red_W).T, "rb": row(L2_gnn_red_b), "rb_v": vec(L2_gnn_red_b),
        "Wl": L3_gnn_W_l, "Wr": L3_gnn_W_r, "att_r": vec(L3_gnn_att),
        "att_c": np.asarray(L3_gnn_att).reshape(HP, 2 * D).T, "bias": vec(L3_gnn_bias),
    }
    nc = _bacc.Bacc("TRN2", target_bir_lowering=False, num_devices=1)
    arrays = {f"in_{name}": np.ascontiguousarray(a) for name, a in arrays.items()}
    ins = {name[3:]: nc.dram_tensor(name, a.shape, mybir.dt.from_np(a.dtype), kind="ExternalInput").ap()
           for name, a in arrays.items()}
    out = nc.dram_tensor("out", (N, D), F32, kind="ExternalOutput").ap()
    build(nc, ins, out)
    return _run(nc, [arrays], core_ids=[0]).results[0]["out"]
```

```python
import numpy as np
from contextlib import ExitStack, contextmanager
import concourse.bass as bass
from concourse import mybir

F32 = mybir.dt.float32
I32 = mybir.dt.int32
ALU = mybir.AluOpType
ACT = mybir.ActivationFunctionType
AX = mybir.AxisListType.X
DVE = mybir.EngineType.DVE
SP = mybir.EngineType.SP

P = 128
N = 3125
E = 103125
D = 64
B = 8
ROWS = B * P
BATCHES = -(-E // (2 * ROWS)) * 2
TILES = BATCHES * B
PAIRS = BATCHES // 2
NB = -(-(N + P) // P)
NPAD = NB * P
TABLES = B
SROWS = NPAD + P
H = 6
HP = H // 2
HALF = D // 2
WH = D + 1
ZH = D + 2
FAR = -1.0e30


class Ctx:

    def __init__(self, nc, phase=""):
        self.nc, self.phase = nc, phase
        self.stack = ExitStack()
        self.used = []

    def sb(self, name, shape, dtype=F32):
        return self.stack.enter_context(self.nc.sbuf_tensor(self.phase + name, shape, dtype))

    def ps(self, name, shape, dtype=F32):
        return self.stack.enter_context(self.nc.psum_tensor(self.phase + name, shape, dtype))

    def sem(self, name):
        self.used.append(self.nc.alloc_semaphore(self.phase + name))
        return self.used[-1]

    def sems(self, *names):
        return [self.sem(n) for n in names]

    def __enter__(self):
        self.stack.__enter__()
        return self

    def __exit__(self, *a):
        if self.used and not a[0]:
            self.nc.clear_and_free_semaphores(self.used)
            self.nc.all_engine_barrier()
        return self.stack.__exit__(*a)


class Kept:
    pass


class Chain:

    def __init__(self, engine, sem):
        self.engine, self.sem, self.count = engine, sem, 0

    def __call__(self, ins):
        self.count += 1
        ins.then_inc(self.sem, 1)
        self.engine.wait_ge(self.sem, self.count)


def pairs(engine, body):
    body(0, False)
    with engine.Fori(1, PAIRS - 1) as t:
        body(t, False)
    body(PAIRS - 1, True)


def ends_apart(engine, body):
    body(0, True, False)
    with engine.Fori(1, PAIRS - 1) as t:
        body(t, False, False)
    body(PAIRS - 1, False, True)


def wait_past(engine, sem, value):
    if not isinstance(value, int) or value > 0:
        engine.wait_ge(sem, value)


def over(ap, n):
    return ap.unsqueeze(2).to_broadcast([ap.shape[0], ap.shape[1], n])


def rows_over(ap, n):
    return ap.unsqueeze(1).to_broadcast([ap.shape[0], n, ap.shape[1]])


def tiles3(ap, a=B):
    return ap.rearrange("p (a b) -> p a b", a=a)


def setup(nc, k, ins):
    with Ctx(nc, "setup_") as c:
        loaded, chain_s, pool_s, act_s, cleared, zero_ready, z_ready, soft_ready, done = c.sems(
            "params_loaded", "dve_step", "pool_step", "act_step", "tables_cleared", "zeros_ready",
            "softplus_arg_ready", "softplus_parts_ready", "spare")
        zeros = c.sb("zeros", [P, SROWS // P * D])
        w2 = c.sb("deg_v", [P, TILES])
        w1 = c.sb("adj_v", [P, TILES])
        dst_f = c.sb("dst_f", [P, TILES])
        base_i = c.sb("base_i", [P, TILES], I32)
        za, zb, zc = c.sb("za", [P, TILES]), c.sb("zb", [P, TILES]), c.sb("zc", [P, TILES])
        small = c.sb("small", [P, 16])
        Wlr, att_row, tmp = c.sb("Wlr", [P, H * D]), c.sb("att_row", [P, H * D]), c.sb("tmp", [P, H * D])
        Watt = c.sb("Watt", [P, H])
        loads = [
            (k.x[:, :, :], ins["x"].rearrange("(b p) d -> p b d", p=P)),
            (k.src_i[:, :], ins["src_t"]), (k.dst_i[:, :], ins["dst_t"]),
            (w1[:, :], ins["w_t"]), (w2[:, :], ins["w2_t"]),
            (base_i[:, :], ins["dst_t"][0:1, :].to_broadcast([P, TILES])),
            (k.W0[0:D, :], ins["W0"]), (k.W0[D:D + 1, :], ins["b0"]),
            (k.deg_coeff[:, :], ins["deg_coeff"].partition_broadcast(P)),
            (k.coeff[:, :], ins["coeff_param"].partition_broadcast(P)),
            (k.scale[:, :], ins["scale_param"].partition_broadcast(P)),
            (k.eps_gin[:, :], ins["eps_gin"].partition_broadcast(P)),
            (k.We[:, :], ins["We"]), (k.be[:, :], ins["be"].partition_broadcast(P)),
            (k.W1[:, :], ins["W1"]), (k.b1[:, :], ins["b1"]),
            (k.W2[0:D, :], ins["W2"]), (k.W2[D:D + 1, :], ins["b2"]),
            (k.gamma[:, :], ins["gamma"].partition_broadcast(P)),
            (k.beta[:, :], ins["beta"].partition_broadcast(P)),
            (k.nlw[:, :], ins["nlw"].partition_broadcast(P)),
            (k.nlb[:, :], ins["nlb"].partition_broadcast(P)),
            (k.nW[0:D, :], ins["nWT"]), (k.nW[D:D + 1, :], ins["nb"]),
            (k.elw[:, :], ins["elw"]), (k.elb[:, :], ins["elb"]),
            (k.eW[:, :], ins["eWT"]), (k.eb[:, :], ins["eb"].partition_broadcast(P)),
            (k.rlw[:, :], ins["rlw"]), (k.rlb[:, :], ins["rlb"]),
            (k.rlw_row[:, :], ins["rlw_r"].partition_broadcast(P)),
            (k.rlb_row[:, :], ins["rlb_r"].partition_broadcast(P)),
            (k.rW[0:D, :], ins["rWT"]), (k.rW[D:D + 1, :], ins["rb"]),
            (k.rb[:, :], ins["rb_v"].partition_broadcast(P)),
            (Wlr[0:D, :], ins["Wl"]), (Wlr[D:P, :], ins["Wr"]),
            (att_row[:, :], ins["att_r"].partition_broadcast(P)),
            (k.bias3[:, :], ins["bias"].partition_broadcast(P)),
        ]
        for j in range(HP):
            for o in range(2):
                loads.append((k.Wl_h[o * D:(o + 1) * D, j, :],
                              ins["Wl"][:, (2 * j + o) * D:(2 * j + o + 1) * D]))
        with nc.Block() as block:
            @block.sync
            def _(sp):
                for dst, src in loads:
                    sp.dma_start(dst, src).then_inc(loaded, 16)
                sp.wait_ge(zero_ready, 1)
                for i in range(TABLES):
                    sp.dma_start(k.scatter_sums[i].rearrange("(p r) d -> p (r d)", p=P),
                                 zeros[:, :]).then_inc(cleared, 16)
                sp.wait_ge(cleared, 16 * TABLES)
                sp.wait_ge(loaded, 16 * len(loads))

            @block.gpsimd
            def _(pool):
                step = Chain(pool, pool_s)
                exact = dict(allow_small_or_imprecise_dtypes=True)
                pool.iota(k.row0[:, :], pattern=[[1, P]], base=0, channel_multiplier=0, **exact)
                pool.iota(k.row1[:, :], pattern=[[1, P]], base=1, channel_multiplier=0, **exact)
                pool.iota(k.col0[:, :], pattern=[[0, 1]], base=0, channel_multiplier=1, **exact)
                pool.iota(k.col1[:, :], pattern=[[0, 1]], base=1, channel_multiplier=1, **exact)
                step(pool.iota(k.spare_row[:, :], pattern=[[0, 1]], base=NPAD, channel_multiplier=1,
                               **exact))

            @block.scalar
            def _(act):
                act.wait_ge(z_ready, 1)
                act.activation(zb[:, :], za[:, :], ACT.Abs).then_inc(act_s, 1)
                act.activation(small[:, 1:2], small[:, 0:1], ACT.Abs).then_inc(act_s, 1)
                act.wait_ge(act_s, 2)
                act.activation(zc[:, :], zb[:, :], ACT.Exp, scale=-1.0).then_inc(act_s, 1)
                act.activation(small[:, 2:3], small[:, 1:2], ACT.Exp, scale=-1.0).then_inc(act_s, 1)
                act.activation(k.coeff_e[:, :], k.coeff_d[:, :], ACT.Exp).then_inc(act_s, 1)
                act.wait_ge(act_s, 5)
                act.activation(zb[:, :], zc[:, :], ACT.Ln, bias=1.0).then_inc(soft_ready, 1)
                act.activation(small[:, 3:4], small[:, 2:3], ACT.Ln, bias=1.0).then_inc(soft_ready, 1)

            @block.vector
            def _(dve):
                step = Chain(dve, chain_s)
                dve.memset(zeros[:, :], 0.0).then_inc(zero_ready, 1)
                dve.memset(k.eps[:, :], 1e-5)
                dve.memset(k.zero_i[:, :], 0)
                dve.memset(k.zero_o[:, :], 0)
                dve.memset(k.zero_o2[:, :], 0)
                dve.memset(k.hT[D:D + 1, :], 1.0)
                step(dve.memset(k.coeff_s[:, :], 0.0))
                dve.wait_ge(loaded, 16 * len(loads))
                dve.wait_ge(pool_s, 1)
                step(dve.tensor_copy(k.src_f[:, :], k.src_i[:, :]))
                step(dve.tensor_copy(dst_f[:, :], k.dst_i[:, :]))
                step(dve.tensor_copy(zc[:, :], base_i[:, :]))
                step(dve.tensor_tensor(k.dst_rel[:, :], dst_f[:, :], zc[:, :], ALU.subtract))
                step(dve.tensor_scalar(k.win_node[:, :], zc[:, :], k.col0[:, :], None, ALU.add))
                step(dve.tensor_scalar(k.src_sp[:, :], k.src_f[:, :], k.spare_row[:, :], None,
                                       ALU.subtract))
                step(dve.tensor_tensor(k.ident[:, :], k.row0[:, :],
                                       k.col0[:, :].to_broadcast([P, P]), ALU.is_equal))
                step(dve.tensor_scalar(k.center[:, :], k.ident[0:D, 0:D], -1.0 / D, None, ALU.add))
                step(dve.tensor_copy(small[:, 0:1], k.scale[:, :]))
                step(dve.tensor_reduce(small[:, 4:5], k.coeff[:, :], AX, ALU.max))
                step(dve.tensor_scalar(k.coeff_d[:, :], k.coeff[:, :], small[:, 4:5], None,
                                       ALU.subtract))
                dve.tensor_scalar(za[:, :], w2[:, :], k.deg_coeff[:, 0:1], k.deg_coeff[:, 1:2],
                                  ALU.mult, ALU.add).then_inc(z_ready, 1)
                step(dve.tensor_tensor(dst_f[:, :], k.src_f[:, :], dst_f[:, :], ALU.not_equal))
                step(dve.tensor_tensor(w1[:, :], w1[:, :], dst_f[:, :], ALU.mult))
                dve.wait_ge(soft_ready, 2)
                step(dve.scalar_tensor_tensor(zb[:, :], za[:, :], 0.0, zb[:, :], ALU.max, ALU.add))
                step(dve.tensor_tensor(k.weight[:, :], w1[:, :], zb[:, :], ALU.mult))
                step(dve.scalar_tensor_tensor(small[:, 5:6], small[:, 0:1], 0.0, small[:, 3:4],
                                              ALU.max, ALU.add))
                step(dve.tensor_reduce(small[:, 6:7], k.coeff_e[:, :], AX, ALU.add))
                step(dve.reciprocal(small[:, 7:8], small[:, 6:7]))
                step(dve.tensor_tensor(small[:, 8:9], small[:, 5:6], small[:, 7:8], ALU.mult))
                step(dve.tensor_scalar(k.coeff_s[:, :], k.coeff_e[:, :], small[:, 8:9], None,
                                       ALU.mult))
                step(dve.tensor_scalar(k.eWw[:, :], k.eW[:, :], k.elw[:, :], None, ALU.mult))
                step(dve.tensor_scalar(k.rWw[:, :], k.rW[0:D, :], k.rlw[:, :], None, ALU.mult))
                step(dve.tensor_copy(k.elb_col[:, :], k.elb[:, 0:1].to_broadcast([D, P])))
                step(dve.tensor_copy(k.rlb_col[:, :], k.rlb[:, 0:1].to_broadcast([D, P])))
                Wz = k.Wz[:, :].rearrange("p (h f) -> p h f", h=H)
                att = k.att_z[:, :].rearrange("p (h f) -> p h f", h=H)
                step(dve.tensor_tensor(tmp[:, :], Wlr[:, :], att_row[:, :], ALU.mult))
                step(dve.tensor_reduce(Watt[:, :], tiles3(tmp[:, :], H), AX, ALU.add))
                step(dve.tensor_copy(Wz[:, :, 0:D], tiles3(Wlr[:, :], H)))
                step(dve.tensor_scalar(Wz[:, :, D], Watt[:, :], 0.2, None, ALU.mult))
                step(dve.tensor_scalar(Wz[:, :, D + 1], Watt[:, :], -0.2, None, ALU.mult))
                step(dve.tensor_scalar(att[:, :, 0:D], tiles3(att_row[:, :], H), 0.8, None, ALU.mult))
                step(dve.memset(att[:, :, D], 1.0))
                step(dve.memset(att[:, :, D + 1], -1.0))

        with nc.psum_tensor("fold", [P, 512], F32) as fold, nc.Block() as block:
            @block.tensor
            def _(pe):
                pe.matmul(fold[0:D, 0:HALF], k.center[:, :], k.eWw[:, :], start=True, stop=True)
                pe.matmul(fold[0:D, 64:64 + D], k.center[:, :], k.rWw[:, :], start=True, stop=True)
                pe.matmul(fold[:, 128:128 + HALF], k.elb_col[:, :], k.eW[:, :],
                          start=True, stop=True)
                pe.matmul(fold[:, 192:192 + D], k.rlb_col[:, :], k.rW[0:D, :],
                          start=True, stop=True).then_inc(done, 1)

            @block.vector
            def _(dve):
                dve.wait_ge(done, 1)
                dve.tensor_copy(k.eR[:, 0:HALF], fold[0:D, 0:HALF])
                dve.tensor_copy(k.eR[:, HALF:HALF + D], k.center[:, :])
                dve.tensor_copy(k.rR[:, 0:D], fold[0:D, 64:64 + D])
                dve.tensor_copy(k.rR[:, D:2 * D], k.center[:, :])
                dve.tensor_tensor(k.ec[:, :], fold[:, 128:128 + HALF], k.eb[:, :], ALU.add)
                dve.tensor_tensor(k.rc[:, :], fold[:, 192:192 + D], k.rb[:, :], ALU.add)


class Norm:

    def __init__(self, c, k):
        self.k = k
        self.var_ready, self.std_ready = c.sems("variance_ready", "std_ready")
        self.stat = c.sb("stat", [P, 4, NB])
        self.n_dve = self.n_act = 0

    def dve(self, dve, step, out, in_, tmp):
        s, k = self.stat, self.k
        self.n_dve += 1
        step(dve.tensor_reduce(s[:, 0, :], in_, AX, ALU.add))
        step(dve.tensor_scalar(s[:, 0, :], s[:, 0, :], 1.0 / D, None, ALU.mult))
        step(dve.tensor_tensor(out, in_, over(s[:, 0, :], D), ALU.subtract))
        step(dve.tensor_tensor(tmp, out, out, ALU.mult))
        dve.tensor_reduce(s[:, 1, :], tmp, AX, ALU.add).then_inc(self.var_ready, 1)
        dve.wait_ge(self.std_ready, self.n_dve)
        step(dve.reciprocal(s[:, 3, :], s[:, 2, :]))
        step(dve.tensor_tensor(out, out, over(s[:, 3, :], D), ALU.mult))

    def act(self, act):
        self.n_act += 1
        act.wait_ge(self.var_ready, self.n_act)
        act.activation(self.stat[:, 2, :], self.stat[:, 1, :], ACT.Sqrt, bias=self.k.eps[:, :],
                       scale=1.0 / D).then_inc(self.std_ready, 1)


def transposed(pe, k, ps, src, rows=P):
    for b in range(NB):
        last = pe.transpose(ps[0:D, b * P:(b + 1) * P], src[:, b, :], k.ident[:, :])
    return last


def node0(nc, k):
    with Ctx(nc, "node0_") as c:
        step_s, h_ready, hT_ready, hTs_ready, wh_ready, nsq_ready, nrm_ready, row_ready, stored = c.sems(
            "dve_step", "h_ready", "hT_in_psum", "hT_ready", "wh_in_psum", "norm_square_ready",
            "norm_ready", "rows_ready", "table_stored")
        norm = Norm(c, k)
        nsq = c.sb("nsq", [P, NB])
        ps = c.ps("node_ps", [P, 4096])
        with nc.Block() as block:
            @block.scalar
            def _(act):
                norm.act(act)
                act.wait_ge(nsq_ready, 1)
                act.activation(k.wh[:, :, D], nsq[:, :], ACT.Sqrt).then_inc(nrm_ready, 1)

            @block.vector
            def _(dve):
                step = Chain(dve, step_s)
                norm.dve(dve, step, k.h[:, :, :], k.x[:, :, :], k.t1[:, :, :])
                dve.tensor_scalar(k.h[:, :, :], k.h[:, :, :], 0.0, None, ALU.max).then_inc(h_ready, 1)
                dve.wait_ge(hT_ready, 1)
                dve.tensor_copy(k.hT[0:D, :], ps[0:D, 0:NPAD]).then_inc(hTs_ready, 1)
                dve.wait_ge(wh_ready, 1)
                step(dve.tensor_copy(k.wh[:, :, 0:D], tiles3(ps[:, 0:NB * D], NB)))
                step(dve.tensor_tensor(k.t1[:, :, :], k.wh[:, :, 0:D], k.wh[:, :, 0:D], ALU.mult))
                dve.tensor_reduce(nsq[:, :], k.t1[:, :, :], AX, ALU.add).then_inc(nsq_ready, 1)

            @block.tensor
            def _(pe):
                pe.wait_ge(h_ready, 1)
                transposed(pe, k, ps, k.h).then_inc(hT_ready, 1)
                pe.wait_ge(hTs_ready, 1)
                for b in range(NB):
                    last = pe.matmul(ps[:, b * D:(b + 1) * D], k.hT[:, b * P:(b + 1) * P],
                                     k.W0[:, :], start=True, stop=True)
                last.then_inc(wh_ready, 1)

            @block.sync
            def _(sp):
                sp.wait_ge(nrm_ready, 1)
                sp.dma_start(k.t_wh.rearrange("(b p) d -> p b d", p=P), k.wh[:, :, :]).then_inc(stored, 16)
                sp.wait_ge(stored, 16)


def node1(nc, k):
    with Ctx(nc, "node1_") as c:
        step_s, hb_ready, stored = c.sems("dve_step", "hb_ready", "table_stored")
        got = [c.sem(f"partial_loaded{i}") for i in range(TABLES)]
        norm = Norm(c, k)
        part = [c.sb(f"partial{i}", [P, NB, D]) for i in range(4)]
        with nc.Block() as block:
            @block.sync
            def _(sp):
                for i in range(TABLES):
                    if i >= 4:
                        sp.wait_ge(step_s, i - 2)
                    sp.dma_start(part[i % 4][:, :, :],
                                 k.scatter_sums[i][0:NPAD, :].rearrange("(b p) d -> p b d", p=P)
                                 ).then_inc(got[i], 16)
                sp.wait_ge(hb_ready, 1)
                sp.dma_start(k.t_h.rearrange("(b p) d -> p b d", p=P), k.t1[:, :, :]).then_inc(stored, 16)
                sp.wait_ge(stored, 16)

            @block.scalar
            def _(act):
                norm.act(act)

            @block.vector
            def _(dve):
                step = Chain(dve, step_s)
                step(dve.tensor_scalar(k.t1[:, :, :], k.wh[:, :, 0:D], k.coeff_s[:, 2:3], None, ALU.mult))
                for i in range(TABLES):
                    dve.wait_ge(got[i], 16)
                    step(dve.tensor_tensor(k.t1[:, :, :], k.t1[:, :, :], part[i % 4][:, :, :], ALU.add))
                step(dve.tensor_tensor(k.x[:, :, :], k.x[:, :, :], k.t1[:, :, :], ALU.add))
                norm.dve(dve, step, k.h[:, :, :], k.x[:, :, :], k.t1[:, :, :])
                step(dve.tensor_scalar(k.h[:, :, :], k.h[:, :, :], 0.0, None, ALU.max))
                dve.tensor_tensor(k.t1[:, :, :], k.h[:, :, :], rows_over(k.be[:, :], NB),
                                  ALU.add).then_inc(hb_ready, 1)
                for acc in k.acc:
                    dve.memset(acc, 0.0)


def node2(nc, k):
    with Ctx(nc, "node2_") as c:
        (step_s, hT_ready, gin_ready, m1_ready, r_ready, m2_ready, h_ready, zT_ready, zTs_ready,
         n_ready, l_ready, lT_ready, lTs_ready, e_ready, hn_ready, stored) = c.sems(
            "dve_step", "hT_in_psum", "gin_ready", "mlp1_in_psum", "mlp1_ready", "mlp2_in_psum",
            "node_norm_ready", "zT_in_psum", "zT_ready", "hn_in_psum", "local_norm_ready",
            "localT_in_psum", "localT_ready", "local_in_psum", "hn_ready", "table_stored")
        norm = Norm(c, k)
        ps = c.ps("node_ps", [P, 4096])
        chunks = [(o, min(512, NPAD - o)) for o in range(0, NPAD, 512)]
        with nc.Block() as block:
            @block.tensor
            def _(pe):
                transposed(pe, k, ps, k.h).then_inc(hT_ready, 1)
                pe.wait_ge(gin_ready, 1)
                for o, w in chunks:
                    last = pe.matmul(ps[0:D, o:o + w], k.W1[:, :], k.accT[0:D, o:o + w],
                                     start=True, stop=True)
                last.then_inc(m1_ready, 1)
                pe.wait_ge(r_ready, 1)
                for b in range(NB):
                    last = pe.matmul(ps[:, b * D:(b + 1) * D], k.hT[:, b * P:(b + 1) * P],
                                     k.W2[:, :], start=True, stop=True)
                last.then_inc(m2_ready, 1)
                pe.wait_ge(h_ready, 1)
                transposed(pe, k, ps, k.t2).then_inc(zT_ready, 1)
                pe.wait_ge(zTs_ready, 1)
                for b in range(NB):
                    last = pe.matmul(ps[:, b * D:b * D + HALF], k.hT[:, b * P:(b + 1) * P],
                                     k.nW[:, :], start=True, stop=True)
                last.then_inc(n_ready, 1)
                pe.wait_ge(l_ready, 1)
                transposed(pe, k, ps, k.t2).then_inc(lT_ready, 1)
                pe.wait_ge(lTs_ready, 1)
                for b in range(NB):
                    last = pe.matmul(ps[:, b * D:(b + 1) * D], k.hT[:, b * P:(b + 1) * P],
                                     k.rW[:, :], start=True, stop=True)
                last.then_inc(e_ready, 1)

            @block.scalar
            def _(act):
                act.wait_ge(m1_ready, 1)
                act.activation(k.hT[0:D, :], ps[0:D, 0:NPAD], ACT.Relu, bias=k.b1[:, :]).then_inc(r_ready, 1)
                for _ in range(4):
                    norm.act(act)

            @block.vector
            def _(dve):
                step = Chain(dve, step_s)
                step(dve.tensor_scalar(k.eps1[:, :], k.eps_gin[:, :], 1.0, None, ALU.add))
                step(dve.tensor_tensor(k.acc[0][0:D, :], k.acc[0][0:D, :], k.acc[1][0:D, :], ALU.add))
                dve.wait_ge(hT_ready, 1)
                dve.scalar_tensor_tensor(k.accT[0:D, 0:NPAD], ps[0:D, 0:NPAD], k.eps1[0:D, :],
                                         k.accT[0:D, 0:NPAD], ALU.mult, ALU.add).then_inc(gin_ready, 1)
                dve.wait_ge(m2_ready, 1)
                m2 = tiles3(ps[:, 0:NB * D], NB)
                step(dve.tensor_copy(k.t1[:, :, :], m2))
                step(dve.scalar_tensor_tensor(k.t1[:, :, :], k.t1[:, :, :], 0.2, k.t1[:, :, :],
                                              ALU.mult, ALU.max))
                norm.dve(dve, step, k.t2[:, :, :], k.t1[:, :, :], k.h[:, :, :])
                step(dve.tensor_tensor(k.t2[:, :, :], k.t2[:, :, :], rows_over(k.gamma[:, :], NB), ALU.mult))
                step(dve.tensor_tensor(k.t2[:, :, :], k.t2[:, :, :], rows_over(k.beta[:, :], NB), ALU.add))
                step(dve.tensor_tensor(k.x[:, :, :], k.x[:, :, :], k.t2[:, :, :], ALU.add))
                norm.dve(dve, step, k.h[:, :, :], k.x[:, :, :], k.t1[:, :, :])
                step(dve.tensor_scalar(k.h[:, :, :], k.h[:, :, :], 0.0, None, ALU.max))
                norm.dve(dve, step, k.t2[:, :, :], k.h[:, :, :], k.t1[:, :, :])
                step(dve.tensor_tensor(k.t2[:, :, :], k.t2[:, :, :], rows_over(k.nlw[:, :], NB), ALU.mult))
                dve.tensor_tensor(k.t2[:, :, :], k.t2[:, :, :], rows_over(k.nlb[:, :], NB),
                                  ALU.add).then_inc(h_ready, 1)
                dve.wait_ge(zT_ready, 1)
                dve.tensor_copy(k.hT[0:D, :], ps[0:D, 0:NPAD]).then_inc(zTs_ready, 1)
                dve.wait_ge(n_ready, 1)
                step(dve.memset(k.wh[:, :, HALF:D], 0.0))
                step(dve.tensor_copy(k.wh[:, :, 0:HALF], m2[:, :, 0:HALF]))
                dve.scalar_tensor_tensor(k.wh[:, :, 0:HALF], k.wh[:, :, 0:HALF], 0.01,
                                         k.wh[:, :, 0:HALF], ALU.mult, ALU.max).then_inc(hn_ready, 1)
                dve.wait_ge(hn_ready, 1)
                norm.dve(dve, step, k.t2[:, :, :], k.wh[:, :, 0:D], k.t1[:, :, :])
                step(dve.tensor_tensor(k.t2[:, :, :], k.t2[:, :, :], rows_over(k.rlw_row[:, :], NB), ALU.mult))
                dve.tensor_tensor(k.t2[:, :, :], k.t2[:, :, :], rows_over(k.rlb_row[:, :], NB),
                                  ALU.add).then_inc(l_ready, 1)
                dve.wait_ge(lT_ready, 1)
                dve.tensor_copy(k.hT[0:D, :], ps[0:D, 0:NPAD]).then_inc(lTs_ready, 1)
                for acc in k.acc:
                    dve.memset(acc, 0.0)
                dve.wait_ge(e_ready, 1)
                step(dve.tensor_copy(k.t1[:, :, :], m2))
                step(dve.scalar_tensor_tensor(k.local[:, :, :], k.t1[:, :, :], 0.01, k.t1[:, :, :],
                                              ALU.mult, ALU.max))

            @block.sync
            def _(sp):
                sp.wait_ge(hn_ready, 1)
                sp.dma_start(k.t_hn.rearrange("(b p) d -> p b d", p=P),
                             k.wh[:, :, 0:HALF]).then_inc(stored, 16)
                sp.wait_ge(stored, 16)


def node3(nc, k):
    with Ctx(nc, "node3_") as c:
        step_s, a_ready, h_ready, stored = c.sems("dve_step", "sums_in_psum", "h_ready", "table_stored")
        norm = Norm(c, k)
        deg = c.sb("deg", [P, 2, NB])
        ps = c.ps("node_ps", [P, 8, 512])
        PER = 7
        with nc.Block() as block:
            @block.tensor
            def _(pe):
                pe.wait_ge(step_s, 1)
                for b in range(NB):
                    o = b % PER * (D + 1)
                    last = pe.matmul(ps[:, b // PER, o:o + D + 1], k.accT[0:D + 1, b * P:(b + 1) * P],
                                     k.ident[0:D + 1, 0:D + 1], start=True, stop=True)
                last.then_inc(a_ready, 1)

            @block.scalar
            def _(act):
                norm.act(act)

            @block.vector
            def _(dve):
                step = Chain(dve, step_s)
                step(dve.tensor_tensor(k.acc[0], k.acc[0], k.acc[1], ALU.add))
                dve.wait_ge(a_ready, 1)
                for g in range(-(-NB // PER)):
                    b0, b1 = g * PER, min(NB, (g + 1) * PER)
                    v = tiles3(ps[:, g, 0:(b1 - b0) * (D + 1)], b1 - b0)
                    step(dve.tensor_tensor(k.t1[:, b0:b1, :], v[:, :, 0:D], k.local[:, b0:b1, :], ALU.add))
                    step(dve.tensor_scalar(deg[:, 0, b0:b1], v[:, :, D], 1.0, None, ALU.add))
                step(dve.reciprocal(deg[:, 1, :], deg[:, 0, :]))
                step(dve.tensor_tensor(k.t1[:, :, :], k.t1[:, :, :], over(deg[:, 1, :], D), ALU.mult))
                step(dve.tensor_tensor(k.x[:, :, :], k.x[:, :, :], k.t1[:, :, :], ALU.add))
                norm.dve(dve, step, k.h[:, :, :], k.x[:, :, :], k.t1[:, :, :])
                dve.tensor_scalar(k.h[:, :, :], k.h[:, :, :], 0.0, None, ALU.max).then_inc(h_ready, 1)

            @block.sync
            def _(sp):
                sp.wait_ge(h_ready, 1)
                sp.dma_start(k.t_h3.rearrange("(b p) d -> p b d", p=P), k.h[:, :, :]).then_inc(stored, 16)
                sp.wait_ge(stored, 16)


def node4(nc, k, out):
    L = 1.0507009873554805
    A = 1.6732632423543772
    with Ctx(nc, "node4_") as c:
        step_s, o_ready, m_ready, e_ready, x_ready, stored = c.sems(
            "dve_step", "heads_in_psum", "negative_part_ready", "exp_ready", "x_ready", "out_stored")
        ps = c.ps("node_ps", [P, 2048])
        with nc.Block() as block:
            @block.tensor
            def _(pe):
                for b in range(NB):
                    for j in range(HP):
                        for acc in (k.accT, k.accT2):
                            last = pe.matmul(ps[:, b * D:(b + 1) * D],
                                             acc[:, j * NPAD + b * P:j * NPAD + (b + 1) * P],
                                             k.Wl_h[:, j, :], start=(j == 0 and acc is k.accT),
                                             stop=(j == HP - 1 and acc is k.accT2))
                last.then_inc(o_ready, 1)

            @block.scalar
            def _(act):
                act.wait_ge(m_ready, 1)
                act.activation(k.t2[:, :, :], k.h[:, :, :], ACT.Exp).then_inc(e_ready, 1)

            @block.vector
            def _(dve):
                step = Chain(dve, step_s)
                dve.wait_ge(o_ready, 1)
                step(dve.tensor_tensor(k.t1[:, :, :], tiles3(ps[:, 0:NB * D], NB),
                                       rows_over(k.bias3[:, :], NB), ALU.add))
                dve.tensor_scalar(k.h[:, :, :], k.t1[:, :, :], 0.0, None, ALU.min).then_inc(m_ready, 1)
                step(dve.tensor_scalar(k.t1[:, :, :], k.t1[:, :, :], 0.0, L, ALU.max, ALU.mult))
                step(dve.tensor_tensor(k.x[:, :, :], k.x[:, :, :], k.t1[:, :, :], ALU.add))
                dve.wait_ge(e_ready, 1)
                step(dve.tensor_scalar(k.t2[:, :, :], k.t2[:, :, :], -1.0, L * A, ALU.add, ALU.mult))
                dve.tensor_tensor(k.x[:, :, :], k.x[:, :, :], k.t2[:, :, :], ALU.add).then_inc(x_ready, 1)

            @block.sync
            def _(sp):
                full = N // P
                sp.wait_ge(x_ready, 1)
                sp.dma_start(out[0:full * P, :].rearrange("(b p) d -> p b d", p=P),
                             k.x[:, 0:full, :]).then_inc(stored, 16)
                sp.dma_start(out[full * P:N, :], k.x[0:N - full * P, full, :]).then_inc(stored, 16)
                sp.wait_ge(stored, 32)


class Gather:

    def __init__(self, c, k, table, slot, free):
        self.k, self.table, self.slot, self.free = k, table, slot, free
        self.idx = [c.sb(f"gather_idx{h}", [P, B], I32) for h in (0, 1)]
        self.gate = c.sem("pool_gate")
        self.idx_loaded = [c.sem(f"idx_loaded{h}") for h in (0, 1)]
        self.gathered = [c.sem(f"gathered{h}") for h in (0, 1)]

    def load(self, sp, t, h):
        wait_past(sp, self.gathered[h], B * 16 * t)
        sp.dma_start(self.idx[h][:, :], self.k.src_t[:, bass.ds(t * 2 * B + h * B, B)]
                     ).then_inc(self.idx_loaded[h], 16)

    def gather(self, nc, pool, t, h, kept=None):
        n = 2 * t + h + 1
        pool.wait_ge(self.idx_loaded[h], 16 * (t + 1))
        pool.wait_ge(self.free, n)
        if kept:
            wait_past(pool, kept[h], 16 * t)
        wait_past(pool, self.gate, n - 1)
        nc.gpsimd.tensor_tensor(self.k.zero_o[:, :], self.k.zero_i[:, :], self.k.zero_i[:, :],
                                ALU.add).then_inc(self.gate, 1)
        for j in range(B):
            nc.gpsimd.indirect_dma_start(
                self.slot(h, j), None, self.table[:, :],
                bass.IndirectOffsetOnAxis(ap=self.idx[h][:, j:j + 1], axis=0)).then_inc(self.gathered[h], 16)

    def loop(self, nc, pool, kept=None):
        def body(t, last):
            self.gather(nc, pool, t, 0, kept)
            self.gather(nc, pool, t, 1, kept)
        pairs(pool, body)


def window_starts(nc, k, engine, t, h):
    return nc.values_load_multi_w_load_instructions(
        k.dst_i[0:1, bass.ds(t * 2 * B + h * B, B)], [engine], min_val=0, max_val=N,
        skip_runtime_bounds_check_because="dst is a node's number, 0 to N - 1, or N in the padding")[1]


def onehot(dve, k, out, t, h):
    return dve.tensor_tensor(out, over(k.dst_rel[:, bass.ds(t * 2 * B + h * B, B)], P),
                             rows_over(k.row0[:, :], B), ALU.is_equal)


def edge0(nc, k):
    with Ctx(nc, "edge0_") as c:
        g = [c.sb(f"src_rows{h}", [P, B, WH]) for h in (0, 1)]
        win = [c.sb(f"window{h}", [P, B, WH]) for h in (0, 1)]
        drow = [c.sb(f"dst_row{h}", [P, ROWS], I32) for h in (0, 1)]
        srow = [c.sb(f"src_row{h}", [P, ROWS], I32) for h in (0, 1)]
        oht = [c.sb(f"onehot_t{h}", [P, ROWS]) for h in (0, 1)]
        same = [c.sb(f"same_src{h}", [P, ROWS]) for h in (0, 1)]
        vw = [c.sb(f"weighted{h}", [P, B, D]) for h in (0, 1)]
        val = [c.sb(f"sums{h}", [P, B, D]) for h in (0, 1)]
        sidx = [c.sb(f"scatter_idx{h}", [P, B], I32) for h in (0, 1)]
        rank = c.sb("rank", [P, ROWS])
        prod = c.sb("prod", [P, B, D])
        s = c.sb("small", [P, 16, B])
        wc = [c.ps(f"dst_rows_ps{h}", [P, B, P]) for h in (0, 1)]
        dup = [c.ps(f"sums_ps{h}", [P, B, D]) for h in (0, 1)]
        rows_ready = [c.sem(f"rows_loaded{h}") for h in (0, 1)]
        win_ready = [c.sem(f"window_loaded{h}") for h in (0, 1)]
        scattered = [c.sem(f"scattered{h}") for h in (0, 1)]
        (oht_ready, same_ready, vw_ready, wc_ready, dup_ready, val_ready, sidx_ready, gate2) = c.sems(
            "onehot_ready", "same_ready", "weighted_ready", "dst_rows_in_psum", "sums_in_psum",
            "sums_ready", "scatter_idx_ready", "pool_gate2")
        (rank_done, last_done, stands_done, moved_done, prod_done, norms_done, dot_done, floor_done,
         recip_done, sim_done, parts_done, signed_done, weight_done) = c.sems(
            "rank_done", "last_done", "stands_done", "moved_done", "prod_done", "norms_done",
            "dot_done", "floor_done", "recip_done", "sim_done", "parts_done", "signed_done",
            "weight_done")
        ga = Gather(c, k, k.t_wh, lambda h, j: g[h][:, j, :], norms_done)
        with nc.Block() as block:
            @block.sync
            def _(sp):
                def body(t, last):
                    for h in (0, 1):
                        n = 2 * t + h + 1
                        ga.load(sp, t, h)
                        sp.wait_ge(wc_ready, n)
                        sp.wait_ge(same_ready, n)
                        sp.dma_start(drow[h][:, :], k.dst_row[bass.ds(2 * t + h, 1), :].to_broadcast([P, ROWS])
                                     ).then_inc(rows_ready[h], 16)
                        sp.dma_start(srow[h][:, :], k.src_row[bass.ds(2 * t + h, 1), :].to_broadcast([P, ROWS])
                                     ).then_inc(rows_ready[h], 16)
                        for j, base in enumerate(window_starts(nc, k, SP, t, h)):
                            sp.dma_start(win[h][:, j, :], k.t_wh[bass.ds(base, P), :]
                                         ).then_inc(win_ready[h], 16)
                pairs(sp, body)

            @block.gpsimd
            def _(pool):
                def scatter(n, h, t):
                    pool.wait_ge(val_ready, n + 2)
                    pool.wait_ge(sidx_ready, n)
                    wait_past(pool, scattered[1 - h], B * 16 * (t + h))
                    pool.wait_ge(gate2, n)
                    nc.gpsimd.tensor_tensor(k.zero_o2[:, :], k.zero_i[:, :], k.zero_i[:, :],
                                            ALU.add).then_inc(gate2, 1)
                    for j in range(B):
                        nc.gpsimd.indirect_dma_start(
                            k.scatter_sums[j], bass.IndirectOffsetOnAxis(ap=sidx[h][:, j:j + 1], axis=0),
                            val[h][:, j, :], None, compute_op=ALU.add).then_inc(scattered[h], 16)

                pool.sem_inc(gate2, 1)
                ga.gather(nc, pool, 0, 0)

                def body(t, last):
                    ga.gather(nc, pool, t, 1)
                    scatter(2 * t + 1, 0, t)
                    if not last:
                        ga.gather(nc, pool, t + 1, 0)
                    scatter(2 * t + 2, 1, t)
                pairs(pool, body)
                for h in (0, 1):
                    pool.wait_ge(scattered[h], B * 16 * PAIRS)

            @block.tensor
            def _(pe):
                pe.sem_inc(wc_ready, 2)
                pe.sem_inc(dup_ready, 2)

                def body(t, last):
                    for h in (0, 1):
                        n = 2 * t + h + 1
                        pe.wait_ge(win_ready[h], B * 16 * (t + 1))
                        pe.wait_ge(oht_ready, n)
                        for j in range(B):
                            last_mm = pe.matmul(wc[h][:, j, 0:WH], oht[h][:, j * P:(j + 1) * P],
                                                win[h][:, j, :], start=True, stop=True)
                        last_mm.then_inc(wc_ready, 1)
                        pe.wait_ge(vw_ready, n)
                        pe.wait_ge(val_ready, n)
                        for j in range(B):
                            mm = pe.matmul(dup[h][:, j, :], same[h][:, j * P:(j + 1) * P],
                                           vw[h][:, j, :], start=True, stop=True)
                        mm.then_inc(dup_ready, 1)
                pairs(pe, body)

            @block.scalar
            def _(act):
                act.sem_inc(val_ready, 2)

                def body(t, last):
                    for h in (0, 1):
                        n = 2 * t + h + 1
                        act.wait_ge(dup_ready, n + 2)
                        wait_past(act, scattered[h], B * 16 * t)
                        act.activation(val[h][:, :, :], dup[h][:, :, :], ACT.Copy).then_inc(val_ready, 1)
                pairs(act, body)

            @block.vector
            def _(dve):
                dve.sem_inc(same_ready, 2)
                dve.sem_inc(norms_done, 2)

                def body(t, last):
                    for h in (0, 1):
                        n = 2 * t + h + 1
                        cols = bass.ds(t * 2 * B + h * B, B)
                        dve.wait_ge(rows_ready[h], 32 * (t + 1))
                        dve.tensor_tensor(tiles3(oht[h][:, :]), tiles3(drow[h][:, :]),
                                          over(k.win_node[:, cols], P), ALU.is_equal).then_inc(oht_ready, 1)
                        dve.wait_ge(dup_ready, n)
                        dve.tensor_tensor(tiles3(same[h][:, :]), tiles3(srow[h][:, :]),
                                          over(k.src_f[:, cols], P), ALU.is_equal).then_inc(same_ready, 1)
                        dve.wait_ge(same_ready, n + 2)
                        dve.tensor_tensor(tiles3(rank[:, :]), tiles3(same[h][:, :]),
                                          rows_over(k.row1[:, :], B), ALU.mult).then_inc(rank_done, 1)
                        dve.wait_ge(rank_done, n)
                        dve.tensor_reduce(s[:, 0, :], tiles3(rank[:, :]), AX, ALU.max).then_inc(last_done, 1)
                        dve.wait_ge(last_done, n)
                        dve.tensor_scalar(s[:, 1, :], s[:, 0, :], k.col1[:, :], None,
                                          ALU.is_equal).then_inc(stands_done, 1)
                        dve.wait_ge(stands_done, n)
                        dve.tensor_tensor(s[:, 2, :], s[:, 1, :], k.src_sp[:, cols],
                                          ALU.mult).then_inc(moved_done, 1)
                        dve.wait_ge(moved_done, n)
                        wait_past(dve, scattered[h], B * 16 * t)
                        dve.tensor_scalar(sidx[h][:, :], s[:, 2, :], k.spare_row[:, :], None,
                                          ALU.add).then_inc(sidx_ready, 1)
                        dve.wait_ge(ga.gathered[h], B * 16 * (t + 1))
                        dve.wait_ge(wc_ready, n + 2)
                        dve.tensor_tensor(prod[:, :, :], g[h][:, :, 0:D], wc[h][:, :, 0:D],
                                          ALU.mult).then_inc(prod_done, 1)
                        dve.tensor_tensor(s[:, 3, :], g[h][:, :, D], wc[h][:, :, D],
                                          ALU.mult).then_inc(norms_done, 1)
                        dve.wait_ge(norms_done, n + 2)
                        dve.tensor_reduce(s[:, 4, :], prod[:, :, :], AX, ALU.add).then_inc(dot_done, 1)
                        dve.tensor_scalar(s[:, 5, :], s[:, 3, :], 1e-8, None, ALU.max).then_inc(floor_done, 1)
                        dve.wait_ge(floor_done, n)
                        dve.reciprocal(s[:, 6, :], s[:, 5, :]).then_inc(recip_done, 1)
                        dve.wait_ge(recip_done, n)
                        dve.tensor_tensor(s[:, 7, :], s[:, 4, :], s[:, 6, :], ALU.mult).then_inc(sim_done, 1)
                        dve.wait_ge(sim_done, n)
                        dve.tensor_scalar(s[:, 8, :], s[:, 7, :], 0.0, k.coeff_s[:, 0:1], ALU.max, ALU.mult)
                        dve.tensor_scalar(s[:, 9, :], s[:, 7, :], 0.0, k.coeff_s[:, 1:2], ALU.min,
                                          ALU.mult).then_inc(parts_done, 1)
                        dve.wait_ge(parts_done, n)
                        dve.tensor_tensor(s[:, 10, :], s[:, 8, :], s[:, 9, :], ALU.add).then_inc(signed_done, 1)
                        dve.wait_ge(signed_done, n)
                        dve.tensor_tensor(s[:, 11, :], s[:, 10, :], k.weight[:, cols],
                                          ALU.mult).then_inc(weight_done, 1)
                        dve.wait_ge(weight_done, n)
                        dve.tensor_tensor(vw[h][:, :, :], wc[h][:, :, 0:D], over(s[:, 11, :], D),
                                          ALU.mult).then_inc(vw_ready, 1)
                pairs(dve, body)


def accumulate(nc, dve, k, ps, rows, t, h, n, added):
    for j, base in enumerate(window_starts(nc, k, DVE, t, h)):
        dve.wait_ge(added[j - 2], n if j != 1 else n + 1)
        acc = k.acc[j % 2][0:rows, bass.ds(base, P)]
        dve.tensor_tensor(acc, acc, ps[0:rows, j, :], ALU.add).then_inc(added[j], 1)


def edge1(nc, k):
    with Ctx(nc, "edge1_") as c:
        g = [c.sb(f"src_rows{h}", [P, B, D]) for h in (0, 1)]
        ea = [c.sb(f"edge_attr{h}", [32, ROWS]) for h in (0, 1)]
        oh = [c.sb(f"onehot{h}", [P, B, P]) for h in (0, 1)]
        msg = [c.sb(f"msg{h}", [P, B, D]) for h in (0, 1)]
        m = [c.ps(f"msg_ps{h}", [P, B, D]) for h in (0, 1)]
        sp_ = [c.ps(f"sums_ps{h}", [D, B, P]) for h in (0, 1)]
        ea_ready = [c.sem(f"edge_attr_loaded{h}") for h in (0, 1)]
        oh_ready, m_ready, msg_ready, sums_ready = c.sems(
            "onehot_ready", "msg_in_psum", "msg_ready", "sums_in_psum")
        ga = Gather(c, k, k.t_h, lambda h, j: g[h][:, j, :], m_ready)
        added = [c.sem(f"added{j}") for j in range(B)]
        with nc.Block() as block:
            @block.sync
            def _(sp):
                def body(t, last):
                    for h in (0, 1):
                        ga.load(sp, t, h)
                        sp.wait_ge(m_ready, 2 * t + h + 1)
                        sp.dma_start(ea[h][:, :], k.ea32[bass.ds(2 * t + h, 1)].rearrange("a f e -> (a f) e")
                                     ).then_inc(ea_ready[h], 16)
                pairs(sp, body)

            @block.gpsimd
            def _(pool):
                ga.loop(nc, pool)

            @block.tensor
            def _(pe):
                def messages(n, h, tt):
                    pe.wait_ge(msg_ready, n)
                    pe.wait_ge(ea_ready[h], 16 * tt)
                    pe.wait_ge(ga.gathered[h], B * 16 * tt)
                    pe.matmul(m[h][:, :, :], k.ident[:, :], g[h][:, :, :], start=True, stop=False)
                    for j in range(B):
                        mm = pe.matmul(m[h][:, j, :], ea[h][:, j * P:(j + 1) * P], k.We[:, :],
                                       start=False, stop=(j == B - 1))
                    mm.then_inc(m_ready, 1)

                pe.sem_inc(sums_ready, 2)
                pe.sem_inc(m_ready, 2)
                messages(1, 0, 1)

                def body(t, last):
                    for h in (0, 1):
                        n = 2 * t + h + 1
                        if not (last and h):
                            messages(n + 1, 1 - h, t + 1 + h)
                        pe.wait_ge(added[B - 1], n)
                        pe.wait_ge(oh_ready, n)
                        pe.wait_ge(msg_ready, n + 2)
                        for j in range(B):
                            mm = pe.matmul(sp_[h][:, j, :], msg[h][:, j, :], oh[h][:, j, :],
                                           start=True, stop=True)
                        mm.then_inc(sums_ready, 1)
                pairs(pe, body)

            @block.scalar
            def _(act):
                act.sem_inc(msg_ready, 2)

                def body(t, last):
                    for h in (0, 1):
                        n = 2 * t + h + 1
                        act.wait_ge(m_ready, n + 2)
                        act.wait_ge(sums_ready, n)
                        act.activation(msg[h][:, :, :], m[h][:, :, :], ACT.Relu).then_inc(msg_ready, 1)
                pairs(act, body)

            @block.vector
            def _(dve):
                dve.sem_inc(added[B - 2], 1)
                dve.sem_inc(added[B - 1], 2)
                onehot(dve, k, oh[0][:, :, :], 0, 0).then_inc(oh_ready, 1)

                def body(t, last):
                    for h in (0, 1):
                        n = 2 * t + h + 1
                        if not (last and h):
                            onehot(dve, k, oh[1 - h][:, :, :], t + h, 1 - h).then_inc(oh_ready, 1)
                        dve.wait_ge(sums_ready, n + 2)
                        accumulate(nc, dve, k, sp_[h], D, t, h, n, added)
                pairs(dve, body)


def edge2(nc, k):
    with Ctx(nc, "edge2_") as c:
        cat = [c.sb(f"cat{h}", [P, B, D]) for h in (0, 1)]
        ea = [c.sb(f"edge_attr{h}", [D, ROWS]) for h in (0, 1)]
        oh = [c.sb(f"onehot{h}", [P, B, P]) for h in (0, 1)]
        msg = [c.sb(f"msg{h}", [P, B, D + 1]) for h in (0, 1)]
        catT = c.sb("cat_t", [D, ROWS])
        junk = c.sb("squares", [P, 2, B, D])
        st = c.sb("stat", [P, 6, B])
        he = c.sb("he_pre", [P, B, HALF])
        he2 = c.sb("he_pre2", [P, B, HALF])
        u, u2 = c.sb("u", [P, B, D]), c.sb("u2", [P, B, D])
        hep = c.ps("he_ps", [P, B, P])
        catTp = c.ps("cat_t_ps", [D, ROWS])
        rp = c.ps("msg_ps", [P, B, P])
        sums = c.ps("sums_ps", [D + 1, B, P])
        ea_ready = [c.sem(f"edge_attr_loaded{h}") for h in (0, 1)]
        (hep_ready, sq1, std1_ready, inv1, he_sc, he_b, cat_ready, catTp_ready, catT_ready, rp_ready,
         sq2, std2_ready, inv2, u_sc, u_b, oh_ready, msg_ready, sums_ready, ones_ready) = c.sems(
            "he_in_psum", "squares1_done", "std1_ready", "inverse1_done", "he_scaled", "he_shifted",
            "cat_ready", "cat_t_in_psum", "cat_t_ready", "msg_in_psum", "squares2_done", "std2_ready",
            "inverse2_done", "msg_scaled", "msg_shifted", "onehot_ready", "msg_ready", "sums_in_psum",
            "ones_ready")
        ga = Gather(c, k, k.t_hn, lambda h, j: cat[h][:, j, 0:HALF], catTp_ready)
        added = [c.sem(f"added{j}") for j in range(B)]

        with nc.Block() as block:
            @block.sync
            def _(sp):
                def body(t, last):
                    for h in (0, 1):
                        ga.load(sp, t, h)
                        wait_past(sp, hep_ready, 2 * t + h - 1)
                        sp.dma_start(ea[h][:, :], k.ea64[bass.ds(2 * t + h, 1)].rearrange("a f e -> (a f) e")
                                     ).then_inc(ea_ready[h], 16)
                pairs(sp, body)

            @block.gpsimd
            def _(pool):
                ga.loop(nc, pool)

            @block.tensor
            def _(pe):
                def edge_part(h, tt):
                    pe.wait_ge(ea_ready[h], 16 * tt)
                    for j in range(B):
                        mm = pe.matmul(hep[:, j, 0:HALF + D], ea[h][:, j * P:(j + 1) * P], k.eR[:, :],
                                       start=True, stop=True)
                    mm.then_inc(hep_ready, 1)

                def sum_up(n, h):
                    pe.wait_ge(msg_ready, n)
                    pe.wait_ge(oh_ready, n)
                    for j in range(B):
                        mm = pe.matmul(sums[:, j, :], msg[h][:, j, :], oh[h][:, j, :], start=True, stop=True)
                    mm.then_inc(sums_ready, 1)

                pe.sem_inc(catTp_ready, 2)
                edge_part(0, 1)
                pe.wait_ge(ones_ready, 1)

                def body(t, first, last):
                    for h in (0, 1):
                        n = 2 * t + h + 1
                        pe.wait_ge(ga.gathered[h], B * 16 * (t + 1))
                        pe.wait_ge(cat_ready, n)
                        for j in range(B):
                            if j == 0:
                                mm = pe.matmul(catTp[:, 0:P], cat[h][:, 0, :], k.ident[:, :],
                                               start=True, stop=True)
                            else:
                                mm = pe.transpose(catTp[:, j * P:(j + 1) * P], cat[h][:, j, :], k.ident[:, :])
                        mm.then_inc(catTp_ready, 1)
                        if not (last and h):
                            edge_part(1 - h, t + 1 + h)
                        if not (first and h == 0):
                            if not (first and h == 1):
                                pe.wait_ge(added[B - 1], n)
                            sum_up(n - 1, 1 - h)
                        pe.wait_ge(catT_ready, n)
                        for j in range(B):
                            mm = pe.matmul(rp[:, j, :], catT[:, j * P:(j + 1) * P], k.rR[:, :],
                                           start=True, stop=True)
                        mm.then_inc(rp_ready, 1)
                ends_apart(pe, body)
                pe.wait_ge(added[B - 1], BATCHES + 1)
                sum_up(BATCHES, 1)

            @block.scalar
            def _(act):
                def root(ps, q, n, sq, ready):
                    for j in range(B):
                        a = act.activation(junk[:, q, j, :], ps[:, j, :], ACT.Square,
                                           accum_out=st[:, 3 * q, j:j + 1])
                    a.then_inc(sq, 1)
                    act.wait_ge(sq, n)
                    act.activation(st[:, 3 * q + 1, :], st[:, 3 * q, :], ACT.Sqrt, bias=k.eps[:, :],
                                   scale=1.0 / D).then_inc(ready, 1)

                act.wait_ge(hep_ready, 1)
                root(hep[:, :, HALF:HALF + D], 0, 1, sq1, std1_ready)

                def body(t, first, last):
                    for h in (0, 1):
                        n = 2 * t + h + 1
                        act.wait_ge(catTp_ready, n + 2)
                        act.activation(catT[:, :], catTp[:, :], ACT.Copy).then_inc(catT_ready, 1)
                        if not (last and h):
                            act.wait_ge(hep_ready, n + 1)
                            root(hep[:, :, HALF:HALF + D], 0, n + 1, sq1, std1_ready)
                        act.wait_ge(rp_ready, n)
                        root(rp[:, :, D:2 * D], 1, n, sq2, std2_ready)
                ends_apart(act, body)

            @block.vector
            def _(dve):
                dve.sem_inc(added[B - 2], 1)
                dve.sem_inc(added[B - 1], 2)
                dve.memset(msg[0][:, :, D], 1.0)
                dve.memset(msg[1][:, :, D], 1.0).then_inc(ones_ready, 1)

                def edge_row(n, h):
                    dve.wait_ge(std1_ready, n)
                    dve.reciprocal(st[:, 2, :], st[:, 1, :]).then_inc(inv1, 1)
                    dve.wait_ge(inv1, n)
                    dve.tensor_tensor(he[:, :, :], hep[:, :, 0:HALF], over(st[:, 2, :], HALF),
                                      ALU.mult).then_inc(he_sc, 1)
                    dve.wait_ge(he_sc, n)
                    dve.tensor_tensor(he2[:, :, :], he[:, :, :], rows_over(k.ec[:, :], B),
                                      ALU.add).then_inc(he_b, 1)
                    dve.wait_ge(he_b, n)
                    dve.scalar_tensor_tensor(cat[h][:, :, HALF:D], he2[:, :, :], 0.01, he2[:, :, :],
                                             ALU.mult, ALU.max).then_inc(cat_ready, 1)

                def message(n, h):
                    dve.wait_ge(std2_ready, n)
                    dve.reciprocal(st[:, 5, :], st[:, 4, :]).then_inc(inv2, 1)
                    dve.wait_ge(inv2, n)
                    dve.tensor_tensor(u[:, :, :], rp[:, :, 0:D], over(st[:, 5, :], D),
                                      ALU.mult).then_inc(u_sc, 1)
                    dve.wait_ge(u_sc, n)
                    dve.tensor_tensor(u2[:, :, :], u[:, :, :], rows_over(k.rc[:, :], B),
                                      ALU.add).then_inc(u_b, 1)
                    dve.wait_ge(u_b, n)
                    dve.scalar_tensor_tensor(msg[h][:, :, 0:D], u2[:, :, :], 0.01, u2[:, :, :],
                                             ALU.mult, ALU.max).then_inc(msg_ready, 1)

                def add(n, h, t):
                    dve.wait_ge(sums_ready, n)
                    accumulate(nc, dve, k, sums, D + 1, t, h, n, added)

                def body(t, first, last):
                    for h in (0, 1):
                        n = 2 * t + h + 1
                        edge_row(n, h)
                        if not (first and h == 0):
                            onehot(dve, k, oh[1 - h][:, :, :], t - 1 + h, 1 - h).then_inc(oh_ready, 1)
                        if not first:
                            add(n - 2, h, t - 1)
                        if not (first and h == 0):
                            message(n - 1, 1 - h)
                ends_apart(dve, body)
                onehot(dve, k, oh[1][:, :, :], PAIRS - 1, 1).then_inc(oh_ready, 1)
                add(BATCHES - 1, 0, PAIRS - 1)
                message(BATCHES, 1)
                add(BATCHES, 1, PAIRS - 1)


def edge3a(nc, k):
    with Ctx(nc, "edge3a_") as c:
        g = [c.sb(f"src_rows{h}", [P, B, D]) for h in (0, 1)]
        win = [c.sb(f"window{h}", [P, B, D]) for h in (0, 1)]
        drow = [c.sb(f"dst_row{h}", [P, ROWS], I32) for h in (0, 1)]
        oht = [c.sb(f"onehot_t{h}", [P, ROWS]) for h in (0, 1)]
        hcT = [c.sb(f"both_ends_t{h}", [P, ROWS]) for h in (0, 1)]
        terms = c.sb("terms", [P, B, H * ZH])
        scs = [c.sb(f"scores{h}", [P, H, B]) for h in (0, 1)]
        scT = [c.sb(f"scores_t{h}", [H * B, P]) for h in (0, 1)]
        hcTp = c.ps("both_ends_t_ps", [P, ROWS])
        zp = [c.ps(f"z_ps{b}", [P, 2, 512]) for b in (0, 1)]
        scTp = c.ps("scores_t_ps", [H * B, P])
        rows_ready = [c.sem(f"rows_loaded{h}") for h in (0, 1)]
        win_ready = [c.sem(f"window_loaded{h}") for h in (0, 1)]
        kept = [c.sem(f"rows_kept{h}") for h in (0, 1)]
        stored = [c.sem(f"scores_stored{h}") for h in (0, 1)]
        oht_ready, hcTp_ready, hcT_ready, z_ready, terms_ready, summed, scTp_ready, scT_ready = c.sems(
            "onehot_ready", "both_ends_t_in_psum", "both_ends_t_ready", "z_in_psum", "terms_ready",
            "terms_summed", "scores_t_in_psum", "scores_t_ready")
        ga = Gather(c, k, k.t_h3, lambda h, j: g[h][:, j, :], hcTp_ready)
        with nc.Block() as block:
            @block.sync
            def _(sp):
                def load(t, h):
                    n = 2 * t + h + 1
                    sp.wait_ge(hcTp_ready, n)
                    sp.wait_ge(oht_ready, n)
                    sp.dma_start(drow[h][:, :], k.dst_row[bass.ds(2 * t + h, 1), :].to_broadcast([P, ROWS])
                                 ).then_inc(rows_ready[h], 16)
                    for j, base in enumerate(window_starts(nc, k, SP, t, h)):
                        sp.dma_start(win[h][:, j, :], k.t_h3[bass.ds(base, P), :]
                                     ).then_inc(win_ready[h], 16)

                ga.load(sp, 0, 0)
                ga.load(sp, 0, 1)
                load(0, 0)
                load(0, 1)

                def body(t, last):
                    for h in (0, 1):
                        sp.wait_ge(ga.gathered[h], B * 16 * (t + 1))
                        if not last:
                            ga.load(sp, t + 1, h)
                        sp.dma_start(k.kept[bass.ds(2 * t + h, 1)].rearrange("a p (b d) -> (a p) b d", b=B),
                                     g[h][:, :, :]).then_inc(kept[h], 16)
                        if not last:
                            load(t + 1, h)
                pairs(sp, body)
                for h in (0, 1):
                    sp.wait_ge(kept[h], 16 * PAIRS)

            @block.gpsimd
            def _(pool):
                ga.loop(nc, pool, kept)

            @block.tensor
            def _(pe):
                pe.sem_inc(hcTp_ready, 2)
                pe.sem_inc(z_ready, 8)
                pe.sem_inc(scTp_ready, 2)

                def turn(n, h, tt):
                    pe.wait_ge(hcT_ready, n)
                    pe.wait_ge(oht_ready, n + 2)
                    pe.wait_ge(win_ready[h], B * 16 * tt)
                    for j in range(B):
                        cols = slice(j * P, (j + 1) * P)
                        pe.matmul(hcTp[D:P, cols], win[h][:, j, :], oht[h][:, cols], start=True, stop=True)
                    pe.wait_ge(ga.gathered[h], B * 16 * tt)
                    for j in range(B):
                        cols = slice(j * P, (j + 1) * P)
                        mm = pe.matmul(hcTp[0:D, cols], g[h][:, j, :], k.ident[:, :], start=True, stop=True)
                    mm.then_inc(hcTp_ready, 1)

                def project(n, h, q):
                    pe.wait_ge(terms_ready, 4 * (n - 1) + q + 1)
                    for i in (0, 1):
                        j = 2 * q + i
                        mm = pe.matmul(zp[q % 2][:, i, 0:H * ZH], hcT[h][:, j * P:(j + 1) * P],
                                       k.Wz[:, :], start=True, stop=True)
                    mm.then_inc(z_ready, 1)

                def turn_scores(n, h):
                    pe.wait_ge(scT_ready, n)
                    pe.wait_ge(summed, 2 * n + 4)
                    pe.matmul(scTp[:, :], scs[h][:, :, :].rearrange("p h b -> p (h b)"), k.ident[:, :],
                              start=True, stop=True).then_inc(scTp_ready, 1)

                turn(1, 0, 1)

                def body(t, first, last):
                    for h in (0, 1):
                        n = 2 * t + h + 1
                        pe.wait_ge(hcT_ready, n + 1)
                        project(n, h, 0)
                        project(n, h, 1)
                        if not (last and h):
                            turn(n + 1, 1 - h, t + 1 + h)
                        if not (first and h == 0):
                            turn_scores(n - 1, 1 - h)
                        project(n, h, 2)
                        project(n, h, 3)
                ends_apart(pe, body)
                turn_scores(BATCHES, 1)

            @block.scalar
            def _(act):
                act.sem_inc(hcT_ready, 1)
                act.sem_inc(scT_ready, 1)

                def turned(n, h):
                    act.wait_ge(hcTp_ready, n + 2)
                    act.wait_ge(z_ready, 4 * n)
                    act.activation(hcT[h][:, :], hcTp[:, :], ACT.Copy).then_inc(hcT_ready, 1)

                def store(n, h, at, tt):
                    act.wait_ge(scTp_ready, n + 2)
                    wait_past(act, stored[h], 16 * tt)
                    act.activation(scT[h][:, :], scTp[:, :], ACT.Copy).then_inc(scT_ready, 1)
                    act.wait_ge(scT_ready, n + 1)
                    act.dma_start(k.scores_d[bass.ds(at, 1)].rearrange("a q e -> (a q) e"),
                                  scT[h][:, :]).then_inc(stored[h], 16)

                turned(1, 0)

                def body(t, first, last):
                    for h in (0, 1):
                        n = 2 * t + h + 1
                        if not (last and h):
                            turned(n + 1, 1 - h)
                        if not (first and h == 0):
                            store(n - 1, 1 - h, 2 * t + h - 1, t - 1 + h)
                body(0, True, False)
                body(1, False, False)
                with act.Fori(2, PAIRS - 1) as t:
                    body(t, False, False)
                body(PAIRS - 1, False, True)
                store(BATCHES, 1, BATCHES - 1, PAIRS - 1)
                for h in (0, 1):
                    act.wait_ge(stored[h], 16 * PAIRS)

            @block.vector
            def _(dve):
                dve.sem_inc(oht_ready, 2)
                dve.sem_inc(terms_ready, 2)
                dve.sem_inc(summed, 4)

                def onehot_t(n, h, t):
                    dve.wait_ge(hcTp_ready, n)
                    dve.wait_ge(rows_ready[h], 16 * (t + 1))
                    dve.tensor_tensor(tiles3(oht[h][:, :]), tiles3(drow[h][:, :]),
                                      over(k.win_node[:, bass.ds(t * 2 * B + h * B, B)], P),
                                      ALU.is_equal).then_inc(oht_ready, 1)

                def weigh(n, q):
                    dve.wait_ge(z_ready, 4 * (n - 1) + q + 9)
                    dve.wait_ge(summed, 2 * n + q // 2 + 1)
                    dve.scalar_tensor_tensor(terms[:, 2 * q:2 * q + 2, :], zp[q % 2][:, :, 0:H * ZH], 0.0,
                                             rows_over(k.att_z[:, :], 2), ALU.max, ALU.mult
                                             ).then_inc(terms_ready, 1)

                def sum_terms(n, h, half):
                    dve.wait_ge(terms_ready, 4 * (n - 1) + 2 * half + 4)
                    dve.wait_ge(scTp_ready, n)
                    j = half * B // 2
                    dve.tensor_reduce(scs[h][:, :, j:j + B // 2].rearrange("p h b -> p b h"),
                                      terms[:, j:j + B // 2, :].rearrange("p b (h f) -> p b h f", h=H),
                                      AX, ALU.add).then_inc(summed, 1)

                onehot_t(1, 0, 0)
                onehot_t(2, 1, 0)

                def body(t, last):
                    for h in (0, 1):
                        n = 2 * t + h + 1
                        weigh(n, 0)
                        weigh(n, 1)
                        sum_terms(n, h, 0)
                        if not last:
                            onehot_t(n + 2, h, t + 1)
                        weigh(n, 2)
                        weigh(n, 3)
                        sum_terms(n, h, 1)
                pairs(dve, body)


def softmax(nc, k):
    Q = BATCHES
    sc = k.accT[0:Q, 0:H * ROWS].rearrange("p (h e) -> p h e", h=H)
    with Ctx(nc, "softmax_") as c:
        mx = c.sb("running", [Q, H, ROWS])
        ids = c.sb("dst_seq", [Q, ROWS + 2], I32)
        start = c.sb("starts", [Q, ROWS])
        end = c.sb("ends", [Q, ROWS])
        keep = c.sb("keeps", [Q, ROWS])
        src = c.sb("src", [Q, ROWS], I32)
        loop = c.sb("loop", [Q, 1, ROWS])
        times = c.sb("times", [Q, 1, ROWS])
        edge = c.sb("edge", [Q, 2, H])
        edgeT = c.sb("edge_t", [H, 2, Q])
        carryT = c.sb("carry_t", [H, Q + 2])
        carry = c.sb("carry", [Q, H])
        loaded, step_s, edge_ready, edgeT_ready, carryT_ready, carry_ready, m_ready, p_ready, a_ready, stored = c.sems(
            "loaded", "dve_step", "edge_ready", "edge_t_ready", "carry_t_ready", "carry_ready",
            "shifted_ready", "exp_ready", "alpha_ready", "alpha_stored")
        ps = c.ps("carry_ps", [P, 512])
        with nc.Block() as block:
            @block.sync
            def _(sp):
                sp.dma_start(sc, k.scores_d.rearrange("q (h b) e -> q h (b e)", h=H)).then_inc(loaded, 16)
                sp.dma_start(ids[:, 0:ROWS], k.dst_seq[0:Q * ROWS].rearrange("(q e) -> q e", q=Q)
                             ).then_inc(loaded, 16)
                sp.dma_start(ids[:, ROWS:ROWS + 2],
                             k.dst_seq[ROWS:ROWS + Q * ROWS].rearrange("(q e) -> q e", q=Q)[:, 0:2]
                             ).then_inc(loaded, 16)
                sp.dma_start(src[:, :], k.src_row[:, :]).then_inc(loaded, 16)
                sp.wait_ge(a_ready, 1)
                sp.dma_start(k.scores_d.rearrange("q (h b) e -> q h (b e)", h=H), mx[:, :, :]
                             ).then_inc(stored, 16)
                sp.wait_ge(stored, 16)

            @block.tensor
            def _(pe):
                for i, (a, o) in enumerate([(1, 0), (H, 0), (H, 2), (H, 0), (H, 2)]):
                    pe.wait_ge(edge_ready, i + 1)
                    pe.transpose(ps[0:a, 0:Q], edge[:, 0, 0:a], k.ident[0:Q, 0:Q])
                    pe.transpose(ps[0:a, P:P + Q], edge[:, 1, 0:a], k.ident[0:Q, 0:Q]
                                 ).then_inc(edgeT_ready, 1)
                    pe.wait_ge(carryT_ready, i + 1)
                    pe.transpose(ps[0:Q, 256:256 + a], carryT[0:a, o:o + Q], k.ident[0:a, 0:a]
                                 ).then_inc(carry_ready, 1)

            @block.scalar
            def _(act):
                act.wait_ge(m_ready, 1)
                act.activation(sc, mx[:, :, :], ACT.Exp).then_inc(p_ready, 1)

            @block.vector
            def _(dve):
                step = Chain(dve, step_s)
                passes = [0]

                def scan(out, data, flags, op0, op1, nothing, back, heads=H):
                    passes[0] += 1
                    way = slice(None, None, -1) if back else slice(None)

                    def run(initial):
                        for h in range(heads):
                            last = dve.tensor_tensor_scan(out[:, h, way], flags[:, way], data[:, h, way],
                                                          initial(h), op0, op1)
                        step(last)
                    run(lambda h: nothing)
                    step(dve.tensor_copy(edge[:, 0, 0:heads], out[:, :, 0 if back else ROWS - 1]))
                    step(dve.tensor_reduce(carry[:, 0:1], flags[:, :], AX, ALU.min))
                    dve.tensor_copy(edge[:, 1, 0:heads], carry[:, 0:1].to_broadcast([Q, heads])).then_inc(edge_ready, 1)
                    dve.wait_ge(edgeT_ready, passes[0])
                    step(dve.tensor_copy(edgeT[0:heads, 0, :], ps[0:heads, 0:Q]))
                    step(dve.tensor_copy(edgeT[0:heads, 1, :], ps[0:heads, P:P + Q]))
                    step(dve.memset(carryT[:, :], nothing))
                    dve.tensor_tensor_scan(carryT[0:heads, 1:Q + 1][:, way], edgeT[0:heads, 1, way], edgeT[0:heads, 0, way],
                                           nothing, op0, op1).then_inc(carryT_ready, 1)
                    dve.wait_ge(carry_ready, passes[0])
                    step(dve.tensor_copy(carry[:, 0:heads], ps[0:Q, 256:256 + heads]))
                    run(lambda h: carry[:, h:h + 1])

                dve.wait_ge(loaded, 64)
                step(dve.tensor_tensor(keep[:, :], ids[:, 1:ROWS + 1], ids[:, 0:ROWS], ALU.is_equal))
                step(dve.tensor_tensor(start[:, :], ids[:, 1:ROWS + 1], ids[:, 0:ROWS], ALU.not_equal))
                step(dve.tensor_scalar(start[:, :], start[:, :], FAR, None, ALU.mult))
                step(dve.tensor_tensor(end[:, :], ids[:, 1:ROWS + 1], ids[:, 2:ROWS + 2], ALU.not_equal))
                step(dve.tensor_scalar(end[:, :], end[:, :], FAR, None, ALU.mult))
                step(dve.tensor_tensor(loop[:, 0, :], ids[:, 1:ROWS + 1], src[:, :], ALU.is_equal))
                scan(times, loop, keep, ALU.mult, ALU.add, 0.0, False, 1)
                step(dve.tensor_scalar(times[:, :, :], times[:, :, :], 1.0, None, ALU.is_equal))
                step(dve.tensor_tensor(times[:, :, :], times[:, :, :], loop[:, :, :], ALU.mult))
                step(dve.tensor_scalar(times[:, :, :], times[:, :, :], 1.0, None, ALU.add))
                scan(mx, sc, start, ALU.add, ALU.max, FAR, False)
                scan(mx, mx, end, ALU.add, ALU.max, FAR, True)
                dve.tensor_tensor(mx[:, :, :], sc, mx[:, :, :], ALU.subtract).then_inc(m_ready, 1)
                dve.wait_ge(p_ready, 1)
                step(dve.tensor_tensor(sc, sc, times[:, :, :].to_broadcast([Q, H, ROWS]), ALU.mult))
                scan(mx, sc, keep, ALU.mult, ALU.add, 0.0, False)
                scan(mx, mx, end, ALU.add, ALU.max, FAR, True)
                step(dve.tensor_scalar(mx[:, :, :], mx[:, :, :], 1e-16, float(H), ALU.add, ALU.mult))
                step(dve.reciprocal(mx[:, :, :], mx[:, :, :]))
                dve.tensor_tensor(mx[:, :, :], mx[:, :, :], sc, ALU.mult).then_inc(a_ready, 1)


def edge3b(nc, k):
    DVE_T, POOL_T, ACT_T = range(0, 2), range(2, 5), range(5, 8)
    with Ctx(nc, "edge3b_") as c:
        raw = [c.sb(f"alpha_t{h}", [H * B, P]) for h in (0, 1)]
        al = [c.sb(f"alpha{h}", [P, H, B]) for h in (0, 1)]
        st = [c.sb(f"src_rows{h}", [P, B, D]) for h in (0, 1)]
        hp = [c.sb(f"weighted{h}", [P, B, H, D]) for h in (0, 1)]
        oh = [c.sb(f"onehot{h}", [P, B, P]) for h in (0, 1)]
        alp = [c.ps(f"alpha_ps{h}", [P, H * B]) for h in (0, 1)]
        sums = [c.ps(f"sums_ps{i}", [P, HP, P]) for i in range(4)]
        raw_ready = [c.sem(f"alpha_loaded{h}") for h in (0, 1)]
        st_ready = [c.sem(f"rows_loaded{h}") for h in (0, 1)]
        alp_ready, al_ready, hp_dve, hp_pool, hp_act, oh_ready, zeroed = c.sems(
            "alpha_in_psum", "alpha_ready", "weighted_by_vector", "weighted_by_gpsimd",
            "weighted_by_scalar", "onehot_ready", "second_accumulator_zeroed")
        summed = [c.sem(f"sums_in_psum{j}") for j in range(B)]
        added = [c.sem(f"added{j}") for j in range(B)]
        starts = [0, 0, 0, 0, 1, 1, 1, 2]

        def weigh(engine, h, tiles):
            a, b = tiles[0], tiles[-1] + 1
            rows = st[h][:, a:b, :].unsqueeze(2).to_broadcast([P, b - a, H, D])
            weights = al[h][:, :, a:b].rearrange("p h b -> p b h").unsqueeze(3).to_broadcast([P, b - a, H, D])
            return engine.tensor_tensor(hp[h][:, a:b, :, :], rows, weights, ALU.mult)

        with nc.Block() as block:
            @block.sync
            def _(sp):
                def body(t, last):
                    for h in (0, 1):
                        n = 2 * t + h + 1
                        at = bass.ds(2 * t + h, 1)
                        sp.wait_ge(alp_ready, n)
                        sp.dma_start(raw[h][:, :], k.scores_d[at].rearrange("a q e -> (a q) e")
                                     ).then_inc(raw_ready[h], 16)
                        for used in (hp_dve, hp_pool, hp_act):
                            sp.wait_ge(used, n)
                        sp.dma_start(st[h][:, :, :], k.kept[at].rearrange("a p (b d) -> (a p) b d", b=B)
                                     ).then_inc(st_ready[h], 16)
                pairs(sp, body)

            @block.gpsimd
            def _(pool):
                nc.gpsimd.memset(k.accT2[:, :], 0.0).then_inc(zeroed, 1)
                pool.sem_inc(hp_pool, 2)

                def body(t, last):
                    for h in (0, 1):
                        n = 2 * t + h + 1
                        pool.wait_ge(st_ready[h], 16 * (t + 1))
                        pool.wait_ge(summed[B - 1], n)
                        pool.wait_ge(al_ready, n)
                        weigh(nc.gpsimd, h, POOL_T).then_inc(hp_pool, 1)
                pairs(pool, body)

            @block.scalar
            def _(act):
                act.sem_inc(hp_act, 2)

                def body(t, last):
                    for h in (0, 1):
                        n = 2 * t + h + 1
                        act.wait_ge(st_ready[h], 16 * (t + 1))
                        act.wait_ge(summed[B - 1], n)
                        act.wait_ge(al_ready, n)
                        for j in ACT_T:
                            for a in range(H):
                                w = act.activation(hp[h][:, j, a, :], st[h][:, j, :], ACT.Copy,
                                                   scale=al[h][:, a, j:j + 1])
                        w.then_inc(hp_act, 1)
                pairs(act, body)

            @block.tensor
            def _(pe):
                pe.sem_inc(alp_ready, 2)
                pe.sem_inc(summed[B - 1], 2)

                def alphas(h, tt):
                    pe.wait_ge(raw_ready[h], 16 * tt)
                    pe.matmul(alp[h][:, :], raw[h][:, :], k.ident[0:H * B, 0:H * B], start=True,
                              stop=True).then_inc(alp_ready, 1)

                alphas(0, 1)

                def body(t, last):
                    for h in (0, 1):
                        n = 2 * t + h + 1
                        if not (last and h):
                            alphas(1 - h, t + 1 + h)
                        pe.wait_ge(oh_ready, n)
                        pe.wait_ge(hp_dve, n + 2)
                        for j in range(B):
                            if j == POOL_T[0]:
                                pe.wait_ge(hp_pool, n + 2)
                            if j == ACT_T[0]:
                                pe.wait_ge(hp_act, n + 2)
                            o = (j + 4) % B
                            pe.wait_ge(added[o], n + starts[o] - (j < 4))
                            for i in range(HP):
                                mm = pe.matmul(sums[j % 4][:, i, :],
                                               hp[h][:, j, 2 * i:2 * i + 2, :].rearrange("p a d -> p (a d)"),
                                               oh[h][:, j, :], start=True, stop=True)
                            mm.then_inc(summed[j], 1)
                pairs(pe, body)

            @block.vector
            def _(dve):
                dve.memset(k.accT[:, :], 0.0)
                dve.wait_ge(zeroed, 1)
                for j in range(B):
                    if starts[j]:
                        dve.sem_inc(added[j], starts[j])
                dve.sem_inc(hp_dve, 2)
                acc3 = [a[:, :].rearrange("p (a w) -> p a w", a=HP) for a in (k.accT, k.accT2)]

                def prepare(n, h, t):
                    dve.wait_ge(alp_ready, n + 2)
                    dve.wait_ge(hp_pool, n)
                    dve.wait_ge(hp_act, n)
                    dve.tensor_copy(al[h][:, :, :].rearrange("p h b -> p (h b)"), alp[h][:, :]).then_inc(al_ready, 1)
                    onehot(dve, k, oh[h][:, :, :], t, h).then_inc(oh_ready, 1)
                    dve.wait_ge(st_ready[h], 16 * (t + 1))
                    dve.wait_ge(al_ready, n)
                    weigh(dve, h, DVE_T).then_inc(hp_dve, 1)

                prepare(1, 0, 0)

                def body(t, last):
                    for h in (0, 1):
                        n = 2 * t + h + 1
                        if not (last and h):
                            prepare(n + 1, 1 - h, t + h)
                        for j, base in enumerate(window_starts(nc, k, DVE, t, h)):
                            dve.wait_ge(summed[j], n + 2 if j == B - 1 else n)
                            dve.wait_ge(added[j - 2], n + starts[j - 2] - (j < 2))
                            acc = acc3[j % 2][:, :, bass.ds(base, P)]
                            dve.tensor_tensor(acc, acc, sums[j % 4][:, :, :], ALU.add).then_inc(added[j], 1)
                pairs(dve, body)


def build(nc, ins, out, stop=99):
    k = Kept()
    dram = lambda name, shape: nc.dram_tensor(name, shape, F32).ap()
    k.t_wh = dram("table_wh", (NPAD, WH))
    k.t_h = dram("table_h", (NPAD, D))
    k.t_hn = dram("table_hn", (NPAD, HALF))
    k.t_h3 = dram("table_h3", (NPAD, D))
    k.kept = dram("kept_rows", (BATCHES, P, B * D))
    k.scores_d = dram("scores_by_batch", (BATCHES, H * B, P))
    k.scatter_sums = [dram(f"scatter_sums{i}", (SROWS, D)) for i in range(TABLES)]
    k.src_t, k.dst_row, k.src_row, k.ea32, k.ea64, k.dst_seq = (
        ins["src_t"], ins["dst_row"], ins["src_row"], ins["ea32"], ins["ea64"], ins["dst_seq"])
    with Ctx(nc) as c:
        k.x = c.sb("x", [P, NB, D])
        k.h = c.sb("h", [P, NB, D])
        k.t1 = c.sb("t1", [P, NB, D])
        k.wh = c.sb("wh", [P, NB, WH])
        k.local = c.sb("local", [P, NB, D])
        k.accT = c.sb("accT", [P, HP * NPAD])
        k.src_i = c.sb("src_i", [P, TILES], I32)
        k.dst_i = c.sb("dst_i", [P, TILES], I32)
        k.src_f = c.sb("src_f", [P, TILES])
        k.dst_rel = c.sb("dst_rel", [P, TILES])
        k.win_node = c.sb("win_node", [P, TILES])
        k.src_sp = c.sb("src_sp", [P, TILES])
        k.weight = c.sb("weight", [P, TILES])
        k.ident = c.sb("ident", [P, P])
        k.row0 = c.sb("row0", [P, P])
        k.row1 = c.sb("row1", [P, P])
        k.col0 = c.sb("col0", [P, 1])
        k.col1 = c.sb("col1", [P, 1])
        k.spare_row = c.sb("spare_row", [P, 1])
        k.eps = c.sb("eps", [P, 1])
        k.zero_i = c.sb("zero_i", [P, 1], I32)
        k.zero_o = c.sb("zero_o", [P, 1], I32)
        k.zero_o2 = c.sb("zero_o2", [P, 1], I32)
        k.center = c.sb("center", [D, D])
        k.W0 = c.sb("W0", [D + 1, D])
        k.deg_coeff = c.sb("deg_coeff", [P, 2])
        k.coeff = c.sb("coeff", [P, 3])
        k.coeff_d = c.sb("coeff_d", [P, 3])
        k.coeff_e = c.sb("coeff_e", [P, 3])
        k.coeff_s = c.sb("coeff_s", [P, 3])
        k.scale = c.sb("scale", [P, 1])
        k.eps_gin = c.sb("eps_gin", [P, 1])
        k.eps1 = c.sb("eps1", [P, 1])
        k.We = c.sb("We", [32, D])
        k.be = c.sb("be", [P, D])
        k.W1 = c.sb("W1", [D, D])
        k.b1 = c.sb("b1", [D, 1])
        k.W2 = c.sb("W2", [D + 1, D])
        k.gamma = c.sb("gamma", [P, D])
        k.beta = c.sb("beta", [P, D])
        k.nlw = c.sb("nlw", [P, D])
        k.nlb = c.sb("nlb", [P, D])
        k.nW = c.sb("nW", [D + 1, HALF])
        k.elw = c.sb("elw", [D, 1])
        k.elb = c.sb("elb", [D, 1])
        k.eW = c.sb("eW", [D, HALF])
        k.eb = c.sb("eb", [P, HALF])
        k.rlw = c.sb("rlw", [D, 1])
        k.rlb = c.sb("rlb", [D, 1])
        k.rlw_row = c.sb("rlw_row", [P, D])
        k.rlb_row = c.sb("rlb_row", [P, D])
        k.rW = c.sb("rW", [D + 1, D])
        k.rb = c.sb("rb", [P, D])
        k.Wz = c.sb("Wz", [P, H * ZH])
        k.att_z = c.sb("att_z", [P, H * ZH])
        k.bias3 = c.sb("bias3", [P, D])
        k.Wl_h = c.sb("Wl_h", [P, HP, D])
        k.eWw = c.sb("eWw", [D, HALF])
        k.rWw = c.sb("rWw", [D, D])
        k.eR = c.sb("eR", [D, HALF + D])
        k.rR = c.sb("rR", [D, 2 * D])
        k.ec = c.sb("ec", [P, HALF])
        k.rc = c.sb("rc", [P, D])
        k.elb_col = c.sb("elb_col", [D, P])
        k.rlb_col = c.sb("rlb_col", [D, P])
        k.hT = k.accT[0:D + 1, NPAD:2 * NPAD]
        k.acc = [k.accT[0:D + 1, 0:NPAD], k.accT[0:D + 1, 2 * NPAD:3 * NPAD]]
        k.t2 = k.accT[:, 2 * NPAD:2 * NPAD + NB * D].rearrange("p (b d) -> p b d", b=NB)
        setup(nc, k, ins)
        node0(nc, k)
        edge0(nc, k)
        node1(nc, k)
        if stop > 1:
            edge1(nc, k)
            node2(nc, k)
        if stop > 2:
            edge2(nc, k)
            node3(nc, k)
        if stop > 3:
            edge3a(nc, k)
            softmax(nc, k)
            with Ctx(nc, "layer3_") as layer:
                k.accT2 = layer.sb("accT2", [P, HP * NPAD])
                edge3b(nc, k)
                node4(nc, k, out)


def kernel(x, src, dst, edge_attr_32, edge_attr_64, edge_weight, edge_weight_n2, L0_gnn_W, L0_gnn_b,
           L0_gnn_deg_coeff, L0_gnn_coeff_param, L0_gnn_scale_param, L1_gnn_We, L1_gnn_be, L1_gnn_W1,
           L1_gnn_b1, L1_gnn_W2, L1_gnn_b2, L1_gnn_eps_gin, L1_gnn_gamma, L1_gnn_beta,
           L2_gnn_node_ln_w, L2_gnn_node_ln_b, L2_gnn_node_W, L2_gnn_node_b, L2_gnn_edge_ln_w,
           L2_gnn_edge_ln_b, L2_gnn_edge_W, L2_gnn_edge_b, L2_gnn_red_ln_w, L2_gnn_red_ln_b,
           L2_gnn_red_W, L2_gnn_red_b, L3_gnn_W_l, L3_gnn_W_r, L3_gnn_att, L3_gnn_bias):
    import concourse.bacc as _bacc
    from concourse.bass_utils import run_bass_kernel_spmd as _run

    def padded(a, rows, fill=0):
        a = np.asarray(a)
        out = np.full((rows,) + a.shape[1:], fill, a.dtype)
        out[:a.shape[0]] = a
        return out

    def by_tile(a, fill=0):
        return np.ascontiguousarray(padded(a, TILES * P, fill).reshape(TILES, P).T)

    def by_batch_t(a):
        a = padded(a, TILES * P)
        return np.ascontiguousarray(a.reshape(BATCHES, ROWS, a.shape[1]).transpose(0, 2, 1))

    def row(a):
        return np.ascontiguousarray(np.asarray(a).reshape(1, -1))

    def vec(a):
        return np.ascontiguousarray(np.asarray(a).reshape(-1))

    def col(a):
        return np.ascontiguousarray(np.asarray(a).reshape(-1, 1))

    seq = np.full((BATCHES + 1) * ROWS, -2, np.int32)
    seq[0] = -1
    seq[1:1 + BATCHES * ROWS] = padded(dst, TILES * P, N)
    arrays = {
        "x": padded(x, NPAD),
        "src_t": by_tile(src), "dst_t": by_tile(dst, N),
        "src_row": padded(src, TILES * P).reshape(BATCHES, ROWS),
        "dst_row": padded(dst, TILES * P, N).reshape(BATCHES, ROWS), "dst_seq": seq,
        "w_t": by_tile(edge_weight), "w2_t": by_tile(edge_weight_n2),
        "ea32": by_batch_t(edge_attr_32), "ea64": by_batch_t(edge_attr_64),
        "W0": L0_gnn_W, "b0": row(L0_gnn_b), "deg_coeff": vec(L0_gnn_deg_coeff),
        "coeff_param": vec(L0_gnn_coeff_param), "scale_param": vec(L0_gnn_scale_param),
        "We": L1_gnn_We, "be": vec(L1_gnn_be), "W1": L1_gnn_W1, "b1": col(L1_gnn_b1),
        "W2": L1_gnn_W2, "b2": row(L1_gnn_b2), "eps_gin": vec(L1_gnn_eps_gin),
        "gamma": vec(L1_gnn_gamma), "beta": vec(L1_gnn_beta),
        "nlw": vec(L2_gnn_node_ln_w), "nlb": vec(L2_gnn_node_ln_b),
        "nWT": np.asarray(L2_gnn_node_W).T, "nb": row(L2_gnn_node_b),
        "elw": col(L2_gnn_edge_ln_w), "elb": col(L2_gnn_edge_ln_b),
        "eWT": np.asarray(L2_gnn_edge_W).T, "eb": vec(L2_gnn_edge_b),
        "rlw": col(L2_gnn_red_ln_w), "rlb": col(L2_gnn_red_ln_b),
        "rlw_r": vec(L2_gnn_red_ln_w), "rlb_r": vec(L2_gnn_red_ln_b),
        "rWT": np.asarray(L2_gnn_red_W).T, "rb": row(L2_gnn_red_b), "rb_v": vec(L2_gnn_red_b),
        "Wl": L3_gnn_W_l, "Wr": L3_gnn_W_r, "att_r": vec(L3_gnn_att), "bias": vec(L3_gnn_bias),
    }
    nc = _bacc.Bacc("TRN2", target_bir_lowering=False, num_devices=1)
    arrays = {f"in_{name}": np.ascontiguousarray(a) for name, a in arrays.items()}
    ins = {name[3:]: nc.dram_tensor(name, a.shape, mybir.dt.from_np(a.dtype), kind="ExternalInput").ap()
           for name, a in arrays.items()}
    out = nc.dram_tensor("out", (N, D), F32, kind="ExternalOutput").ap()
    build(nc, ins, out)
    return _run(nc, [arrays], core_ids=[0]).results[0]["out"]
```

```python
import numpy as np
from contextlib import ExitStack, contextmanager
import concourse.bass as bass
from concourse import mybir

F32 = mybir.dt.float32
I32 = mybir.dt.int32
ALU = mybir.AluOpType
ACT = mybir.ActivationFunctionType
AX = mybir.AxisListType.X
DVE = mybir.EngineType.DVE
SP = mybir.EngineType.SP

P = 128
N = 3125
E = 103125
D = 64
B = 8
ROWS = B * P
BATCHES = -(-E // (2 * ROWS)) * 2
TILES = BATCHES * B
PAIRS = BATCHES // 2
NB = -(-(N + P) // P)
NPAD = NB * P
TABLES = B
SROWS = NPAD + P
H = 6
HP = H // 2
HALF = D // 2
WH = D + 1
ZH = D + 2
FAR = -1.0e30


class Ctx:

    def __init__(self, nc, phase=""):
        self.nc, self.phase = nc, phase
        self.stack = ExitStack()
        self.used = []

    def sb(self, name, shape, dtype=F32):
        return self.stack.enter_context(self.nc.sbuf_tensor(self.phase + name, shape, dtype))

    def ps(self, name, shape, dtype=F32):
        return self.stack.enter_context(self.nc.psum_tensor(self.phase + name, shape, dtype))

    def sem(self, name):
        self.used.append(self.nc.alloc_semaphore(self.phase + name))
        return self.used[-1]

    def sems(self, *names):
        return [self.sem(n) for n in names]

    def __enter__(self):
        self.stack.__enter__()
        return self

    def __exit__(self, *a):
        if self.used and not a[0]:
            self.nc.clear_and_free_semaphores(self.used)
            self.nc.all_engine_barrier()
        return self.stack.__exit__(*a)


class Kept:
    pass


class Chain:

    def __init__(self, engine, sem):
        self.engine, self.sem, self.count = engine, sem, 0

    def __call__(self, ins):
        self.count += 1
        ins.then_inc(self.sem, 1)
        self.engine.wait_ge(self.sem, self.count)


def pairs(engine, body):
    body(0, False)
    with engine.Fori(1, PAIRS - 1) as t:
        body(t, False)
    body(PAIRS - 1, True)


def ends_apart(engine, body):
    body(0, True, False)
    with engine.Fori(1, PAIRS - 1) as t:
        body(t, False, False)
    body(PAIRS - 1, False, True)


def wait_past(engine, sem, value):
    if not isinstance(value, int) or value > 0:
        engine.wait_ge(sem, value)


def over(ap, n):
    return ap.unsqueeze(2).to_broadcast([ap.shape[0], ap.shape[1], n])


def rows_over(ap, n):
    return ap.unsqueeze(1).to_broadcast([ap.shape[0], n, ap.shape[1]])


def tiles3(ap, a=B):
    return ap.rearrange("p (a b) -> p a b", a=a)


def setup(nc, k, ins):
    with Ctx(nc, "setup_") as c:
        loaded, chain_s, pool_s, act_s, zero_ready, z_ready, soft_ready, done, x_loaded = c.sems(
            "params_loaded", "dve_step", "pool_step", "act_step", "zeros_ready",
            "softplus_arg_ready", "softplus_parts_ready", "fold_in_psum", "x_loaded")
        zeros = k.accT[:, 0:SROWS // P * D]
        w2 = c.sb("deg_v", [P, TILES])
        norm = Norm(c, k)
        w1 = c.sb("adj_v", [P, TILES])
        dst_f = c.sb("dst_f", [P, TILES])
        base_i = c.sb("base_i", [P, TILES], I32)
        za, zb, zc = c.sb("za", [P, TILES]), c.sb("zb", [P, TILES]), c.sb("zc", [P, TILES])
        small = c.sb("small", [P, 16])
        Wlr, tmp = c.sb("Wlr", [P, H * D]), c.sb("tmp", [P, H * D])
        Watt = c.sb("Watt", [P, H])
        loads = [
            (k.vectors[:, :], ins["vectors"].partition_broadcast(P)),
            (k.src_i[:, :], ins["src_t"]), (k.dst_i[:, :], ins["dst_t"]),
            (w1[:, :], ins["w_t"]), (w2[:, :], ins["w2_t"]),
            (base_i[:, :], ins["dst_t"][0:1, :].to_broadcast([P, TILES])),
            (k.W0[0:D, :], ins["W0"]), (k.W0[D:D + 1, :], ins["b0"]),
            (k.We[:, :], ins["We"]), (k.W1[:, :], ins["W1"]), (k.b1[:, :], ins["b1"]),
            (k.W2[0:D, :], ins["W2"]), (k.W2[D:D + 1, :], ins["b2"]),
            (k.nW[0:D, :], ins["nWT"]), (k.nW[D:D + 1, :], ins["nb"]),
            (k.elw[:, :], ins["elw"]), (k.elb[:, :], ins["elb"]), (k.eW[:, :], ins["eWT"]),
            (k.rlw[:, :], ins["rlw"]), (k.rlb[:, :], ins["rlb"]),
            (k.rW[0:D, :], ins["rWT"]), (k.rW[D:D + 1, :], ins["rb"]),
            (Wlr[0:D, :], ins["Wl"]), (Wlr[D:P, :], ins["Wr"]),
        ]
        for j in range(HP):
            for o in range(2):
                loads.append((k.Wl_h[o * D:(o + 1) * D, j, :],
                              ins["Wl"][:, (2 * j + o) * D:(2 * j + o + 1) * D]))
        with nc.Block() as block:
            @block.sync
            def _(sp):
                sp.dma_start(k.x[:, :, :], ins["x"].rearrange("(p b) d -> p b d", p=P)).then_inc(x_loaded, 16)
                for dst, src in loads[8:]:
                    sp.dma_start(dst, src).then_inc(loaded, 16)
                sp.wait_ge(zero_ready, 1)
                for i in range(TABLES):
                    sp.dma_start(k.scatter_sums[i].rearrange("(p r) d -> p (r d)", p=P),
                                 zeros).then_inc(k.tables_cleared, 16)
                sp.wait_ge(loaded, 16 * len(loads))

            @block.gpsimd
            def _(pool):
                step = Chain(pool, pool_s)
                exact = dict(allow_small_or_imprecise_dtypes=True)
                pool.iota(k.row0[:, :], pattern=[[1, P]], base=0, channel_multiplier=0, **exact)
                pool.iota(k.row1[:, :], pattern=[[1, P]], base=1, channel_multiplier=0, **exact)
                pool.iota(k.col0[:, :], pattern=[[0, 1]], base=0, channel_multiplier=1, **exact)
                pool.iota(k.col1[:, :], pattern=[[0, 1]], base=1, channel_multiplier=1, **exact)
                step(pool.iota(k.spare_row[:, :], pattern=[[0, 1]], base=NPAD, channel_multiplier=1,
                               **exact))

            @block.scalar
            def _(act):
                for dst, src in loads[:8]:
                    act.dma_start(dst, src).then_inc(loaded, 16)
                norm.act(act)
                act.wait_ge(z_ready, 1)
                act.activation(zb[:, :], za[:, :], ACT.Abs).then_inc(act_s, 1)
                act.activation(small[:, 1:2], small[:, 0:1], ACT.Abs).then_inc(act_s, 1)
                act.wait_ge(act_s, 2)
                act.activation(zc[:, :], zb[:, :], ACT.Exp, scale=-1.0).then_inc(act_s, 1)
                act.activation(small[:, 2:3], small[:, 1:2], ACT.Exp, scale=-1.0).then_inc(act_s, 1)
                act.activation(k.coeff_e[:, :], k.coeff_d[:, :], ACT.Exp).then_inc(act_s, 1)
                act.wait_ge(act_s, 5)
                act.activation(zb[:, :], zc[:, :], ACT.Ln, bias=1.0).then_inc(soft_ready, 1)
                act.activation(small[:, 3:4], small[:, 2:3], ACT.Ln, bias=1.0).then_inc(soft_ready, 1)

            @block.vector
            def _(dve):
                step = Chain(dve, chain_s)
                dve.memset(zeros, 0.0).then_inc(zero_ready, 1)
                dve.memset(k.eps[:, :], 1e-5)
                dve.memset(k.hT[D:D + 1, :], 1.0)
                step(dve.memset(k.coeff_s[:, :], 0.0))
                dve.wait_ge(x_loaded, 16)
                norm.dve(dve, step, k.h[:, :, :], k.x[:, :, :], k.t1[:, :, :], relu=True)
                dve.wait_ge(loaded, 16 * len(loads))
                dve.wait_ge(pool_s, 1)
                step(dve.tensor_copy(k.src_f[:, :], k.src_i[:, :]))
                step(dve.tensor_copy(dst_f[:, :], k.dst_i[:, :]))
                step(dve.tensor_copy(zc[:, :], base_i[:, :]))
                step(dve.tensor_tensor(k.dst_rel[:, :], dst_f[:, :], zc[:, :], ALU.subtract))
                step(dve.tensor_scalar(k.win_node[:, :], zc[:, :], k.col0[:, :], None, ALU.add))
                step(dve.tensor_scalar(k.src_sp[:, :], k.src_f[:, :], k.spare_row[:, :], None,
                                       ALU.subtract))
                step(dve.tensor_tensor(k.ident[:, :], k.row0[:, :],
                                       k.col0[:, :].to_broadcast([P, P]), ALU.is_equal))
                step(dve.tensor_scalar(k.center[:, :], k.ident[0:D, 0:D], -1.0 / D, None, ALU.add))
                step(dve.tensor_copy(small[:, 0:1], k.scale[:, :]))
                step(dve.tensor_reduce(small[:, 4:5], k.coeff[:, :], AX, ALU.max))
                step(dve.tensor_scalar(k.coeff_d[:, :], k.coeff[:, :], small[:, 4:5], None,
                                       ALU.subtract))
                dve.tensor_scalar(za[:, :], w2[:, :], k.deg_coeff[:, 0:1], k.deg_coeff[:, 1:2],
                                  ALU.mult, ALU.add).then_inc(z_ready, 1)
                step(dve.tensor_tensor(dst_f[:, :], k.src_f[:, :], dst_f[:, :], ALU.not_equal))
                step(dve.tensor_tensor(w1[:, :], w1[:, :], dst_f[:, :], ALU.mult))
                dve.wait_ge(soft_ready, 2)
                step(dve.scalar_tensor_tensor(zb[:, :], za[:, :], 0.0, zb[:, :], ALU.max, ALU.add))
                step(dve.tensor_tensor(k.weight[:, :], w1[:, :], zb[:, :], ALU.mult))
                step(dve.scalar_tensor_tensor(small[:, 5:6], small[:, 0:1], 0.0, small[:, 3:4],
                                              ALU.max, ALU.add))
                step(dve.tensor_reduce(small[:, 6:7], k.coeff_e[:, :], AX, ALU.add))
                step(dve.reciprocal(small[:, 7:8], small[:, 6:7]))
                step(dve.tensor_tensor(small[:, 8:9], small[:, 5:6], small[:, 7:8], ALU.mult))
                step(dve.tensor_scalar(k.coeff_s[:, :], k.coeff_e[:, :], small[:, 8:9], None,
                                       ALU.mult))
                step(dve.tensor_scalar(k.eWw[:, :], k.eW[:, :], k.elw[:, :], None, ALU.mult))
                step(dve.tensor_scalar(k.rWw[:, :], k.rW[0:D, :], k.rlw[:, :], None, ALU.mult))
                step(dve.tensor_copy(k.elb_col[:, :], k.elb[:, 0:1].to_broadcast([D, P])))
                step(dve.tensor_copy(k.rlb_col[:, :], k.rlb[:, 0:1].to_broadcast([D, P])))
                Wz = k.Wz[:, :].rearrange("p (h f) -> p h f", h=H)
                att = k.att_z[:, :].rearrange("p (h f) -> p h f", h=H)
                step(dve.tensor_tensor(tmp[:, :], Wlr[:, :], k.att_row[:, :], ALU.mult))
                step(dve.tensor_reduce(Watt[:, :], tiles3(tmp[:, :], H), AX, ALU.add))
                step(dve.tensor_copy(Wz[:, :, 0:D], tiles3(Wlr[:, :], H)))
                step(dve.tensor_scalar(Wz[:, :, D], Watt[:, :], 0.2, None, ALU.mult))
                step(dve.tensor_scalar(Wz[:, :, D + 1], Watt[:, :], -0.2, None, ALU.mult))
                step(dve.tensor_scalar(att[:, :, 0:D], tiles3(k.att_row[:, :], H), 0.8, None, ALU.mult))
                step(dve.memset(att[:, :, D], 1.0))
                step(dve.memset(att[:, :, D + 1], -1.0))

        with nc.psum_tensor("fold", [P, 512], F32) as fold, nc.Block() as block:
            @block.tensor
            def _(pe):
                pe.matmul(fold[0:D, 0:HALF], k.center[:, :], k.eWw[:, :], start=True, stop=True)
                pe.matmul(fold[0:D, 64:64 + D], k.center[:, :], k.rWw[:, :], start=True, stop=True)
                pe.matmul(fold[:, 128:128 + HALF], k.elb_col[:, :], k.eW[:, :],
                          start=True, stop=True)
                pe.matmul(fold[:, 192:192 + D], k.rlb_col[:, :], k.rW[0:D, :],
                          start=True, stop=True).then_inc(done, 1)

            @block.vector
            def _(dve):
                dve.wait_ge(done, 1)
                dve.tensor_copy(k.eR[:, 0:HALF], fold[0:D, 0:HALF])
                dve.tensor_copy(k.eR[:, HALF:HALF + D], k.center[:, :])
                dve.tensor_copy(k.rR[:, 0:D], fold[0:D, 64:64 + D])
                dve.tensor_copy(k.rR[:, D:2 * D], k.center[:, :])
                dve.tensor_tensor(k.ec[:, :], fold[:, 128:128 + HALF], k.eb[:, :], ALU.add)
                dve.tensor_tensor(k.rc[:, :], fold[:, 192:192 + D], k.rb[:, :], ALU.add)


def block_columns(ap, b):
    return ap.rearrange("p (q b) -> p b q", b=NB)[:, b, :]


class Norm:

    def __init__(self, c, k):
        self.k = k
        self.var_ready, self.std_ready = c.sems("variance_ready", "std_ready")
        self.stat = c.sb("stat", [P, 4, NB])
        self.n_dve = self.n_act = 0

    def dve(self, dve, step, out, in_, tmp, relu=False):
        s, k = self.stat, self.k
        self.n_dve += 1
        step(dve.tensor_reduce(s[:, 0, :], in_, AX, ALU.add))
        step(dve.scalar_tensor_tensor(out, over(s[:, 0, :], D), -1.0 / D, in_, ALU.mult, ALU.add))
        step(dve.tensor_tensor(tmp, out, out, ALU.mult))
        dve.tensor_reduce(s[:, 1, :], tmp, AX, ALU.add).then_inc(self.var_ready, 1)
        dve.wait_ge(self.std_ready, self.n_dve)
        step(dve.reciprocal(s[:, 3, :], s[:, 2, :]))
        if relu:
            step(dve.scalar_tensor_tensor(out, out, 0.0, over(s[:, 3, :], D), ALU.max, ALU.mult))
        else:
            step(dve.tensor_tensor(out, out, over(s[:, 3, :], D), ALU.mult))

    def act(self, act):
        self.n_act += 1
        act.wait_ge(self.var_ready, self.n_act)
        act.activation(self.stat[:, 2, :], self.stat[:, 1, :], ACT.Sqrt, bias=self.k.eps[:, :],
                       scale=1.0 / D).then_inc(self.std_ready, 1)


def transposed(pe, k, ps, src):
    for b in range(NB):
        last = pe.transpose(ps[0:D, b * P:(b + 1) * P], src[:, b, :], k.ident[:, :])
    return last


def node0(nc, k):
    with Ctx(nc, "node0_") as c:
        step_s, hT_ready, hTs_ready, wh_ready, nsq_ready, nrm_ready, row_ready, stored = c.sems(
            "dve_step", "hT_in_psum", "hT_ready", "wh_in_psum", "norm_square_ready",
            "norm_ready", "rows_ready", "table_stored")
        nsq = c.sb("nsq", [P, NB])
        ps = c.ps("node_ps", [P, 4096])
        with nc.Block() as block:
            @block.scalar
            def _(act):
                act.wait_ge(nsq_ready, 1)
                act.activation(k.wh[:, :, D], nsq[:, :], ACT.Sqrt).then_inc(nrm_ready, 1)

            @block.vector
            def _(dve):
                step = Chain(dve, step_s)
                dve.wait_ge(hT_ready, 1)
                dve.tensor_copy(k.hT[0:D, :], ps[0:D, 0:NPAD]).then_inc(hTs_ready, 1)
                dve.wait_ge(wh_ready, 1)
                step(dve.tensor_copy(k.wh[:, :, 0:D], tiles3(ps[:, 0:NB * D], NB)))
                step(dve.tensor_tensor(k.t1[:, :, :], k.wh[:, :, 0:D], k.wh[:, :, 0:D], ALU.mult))
                dve.tensor_reduce(nsq[:, :], k.t1[:, :, :], AX, ALU.add).then_inc(nsq_ready, 1)

            @block.tensor
            def _(pe):
                transposed(pe, k, ps, k.h).then_inc(hT_ready, 1)
                pe.wait_ge(hTs_ready, 1)
                for b in range(NB):
                    last = pe.matmul(ps[:, b * D:(b + 1) * D], k.hT[:, b * P:(b + 1) * P],
                                     k.W0[:, :], start=True, stop=True)
                last.then_inc(wh_ready, 1)

            @block.sync
            def _(sp):
                sp.wait_ge(nrm_ready, 1)
                sp.dma_start(k.t_wh.rearrange("(p b) d -> p b d", p=P), k.wh[:, :, :]).then_inc(stored, 16)
                sp.wait_ge(stored, 16)
                sp.wait_ge(k.tables_cleared, 16 * TABLES)


def node1(nc, k):
    with Ctx(nc, "node1_") as c:
        step_s, hb_ready, stored = c.sems("dve_step", "hb_ready", "table_stored")
        got = [c.sem(f"partial_loaded{i}") for i in range(TABLES)]
        norm = Norm(c, k)
        part = [c.sb(f"partial{i}", [P, NB, D]) for i in range(4)]
        with nc.Block() as block:
            @block.gpsimd
            def _(pool):
                for acc in k.acc:
                    nc.gpsimd.memset(acc, 0.0)

            @block.sync
            def _(sp):
                for i in range(TABLES):
                    if i >= 4:
                        sp.wait_ge(step_s, i - 2)
                    sp.dma_start(part[i % 4][:, :, :],
                                 k.scatter_sums[i][0:NPAD, :].rearrange("(p b) d -> p b d", p=P)
                                 ).then_inc(got[i], 16)
                sp.wait_ge(hb_ready, 1)
                sp.dma_start(k.t_h.rearrange("(p b) d -> p b d", p=P), k.t1[:, :, :]).then_inc(stored, 16)
                sp.wait_ge(stored, 16)

            @block.scalar
            def _(act):
                norm.act(act)

            @block.vector
            def _(dve):
                step = Chain(dve, step_s)
                step(dve.tensor_scalar(k.t1[:, :, :], k.wh[:, :, 0:D], k.coeff_s[:, 2:3], None, ALU.mult))
                for i in range(TABLES):
                    dve.wait_ge(got[i], 16)
                    step(dve.tensor_tensor(k.t1[:, :, :], k.t1[:, :, :], part[i % 4][:, :, :], ALU.add))
                step(dve.tensor_tensor(k.x[:, :, :], k.x[:, :, :], k.t1[:, :, :], ALU.add))
                norm.dve(dve, step, k.h[:, :, :], k.x[:, :, :], k.t1[:, :, :], relu=True)
                dve.tensor_tensor(k.t1[:, :, :], k.h[:, :, :], rows_over(k.be[:, :], NB),
                                  ALU.add).then_inc(hb_ready, 1)


def node2(nc, k):
    with Ctx(nc, "node2_") as c:
        (step_s, hT_ready, gin_ready, m1_ready, r_ready, m2_ready, h_ready, zT_ready, zTs_ready,
         n_ready, l_ready, lT_ready, lTs_ready, e_ready, hn_ready, stored) = c.sems(
            "dve_step", "hT_in_psum", "gin_ready", "mlp1_in_psum", "mlp1_ready", "mlp2_in_psum",
            "node_norm_ready", "zT_in_psum", "zT_ready", "hn_in_psum", "local_norm_ready",
            "localT_in_psum", "localT_ready", "local_in_psum", "hn_ready", "table_stored")
        norm = Norm(c, k)
        ps = c.ps("node_ps", [P, 4096])
        chunks = [(o, min(512, NPAD - o)) for o in range(0, NPAD, 512)]
        with nc.Block() as block:
            @block.tensor
            def _(pe):
                transposed(pe, k, ps, k.h).then_inc(hT_ready, 1)
                pe.wait_ge(gin_ready, 1)
                for o, w in chunks:
                    last = pe.matmul(ps[0:D, o:o + w], k.W1[:, :], k.acc[1][0:D, o:o + w],
                                     start=True, stop=True)
                last.then_inc(m1_ready, 1)
                pe.wait_ge(r_ready, 1)
                for b in range(NB):
                    last = pe.matmul(ps[:, b * D:(b + 1) * D], k.hT[:, b * P:(b + 1) * P],
                                     k.W2[:, :], start=True, stop=True)
                last.then_inc(m2_ready, 1)
                pe.wait_ge(h_ready, 1)
                transposed(pe, k, ps, k.t2).then_inc(zT_ready, 1)
                pe.wait_ge(zTs_ready, 1)
                for b in range(NB):
                    last = pe.matmul(ps[:, b * D:b * D + HALF], k.hT[:, b * P:(b + 1) * P],
                                     k.nW[:, :], start=True, stop=True)
                last.then_inc(n_ready, 1)
                pe.wait_ge(l_ready, 1)
                transposed(pe, k, ps, k.t2).then_inc(lT_ready, 1)
                pe.wait_ge(lTs_ready, 1)
                for b in range(NB):
                    last = pe.matmul(ps[:, b * D:(b + 1) * D], k.hT[:, b * P:(b + 1) * P],
                                     k.rW[:, :], start=True, stop=True)
                last.then_inc(e_ready, 1)

            @block.gpsimd
            def _(pool):
                pool.wait_ge(gin_ready, 1)
                nc.gpsimd.memset(k.acc[0], 0.0)
                pool.wait_ge(lT_ready, 1)
                nc.gpsimd.memset(k.acc[1], 0.0)

            @block.scalar
            def _(act):
                act.wait_ge(m1_ready, 1)
                act.activation(k.hT[0:D, :], ps[0:D, 0:NPAD], ACT.Relu, bias=k.b1[:, :]).then_inc(r_ready, 1)
                for _ in range(4):
                    norm.act(act)

            @block.vector
            def _(dve):
                step = Chain(dve, step_s)
                step(dve.tensor_scalar(k.eps1[:, :], k.eps_gin[:, :], 1.0, None, ALU.add))
                step(dve.tensor_tensor(k.acc[0][0:D, :], k.acc[0][0:D, :], k.acc[1][0:D, :], ALU.add))
                dve.wait_ge(hT_ready, 1)
                dve.scalar_tensor_tensor(k.acc[1][0:D, :].rearrange("p (b q) -> p b q", b=NB),
                                         ps[0:D, 0:NPAD].rearrange("p (b q) -> p b q", b=NB), k.eps1[0:D, :],
                                         k.acc[0][0:D, :].rearrange("p (q b) -> p b q", b=NB),
                                         ALU.mult, ALU.add).then_inc(gin_ready, 1)
                dve.wait_ge(m2_ready, 1)
                m2 = tiles3(ps[:, 0:NB * D], NB)
                step(dve.tensor_copy(k.t1[:, :, :], m2))
                step(dve.scalar_tensor_tensor(k.t1[:, :, :], k.t1[:, :, :], 0.2, k.t1[:, :, :],
                                              ALU.mult, ALU.max))
                norm.dve(dve, step, k.t2[:, :, :], k.t1[:, :, :], k.h[:, :, :])
                step(dve.tensor_tensor(k.t2[:, :, :], k.t2[:, :, :], rows_over(k.gamma[:, :], NB), ALU.mult))
                step(dve.tensor_tensor(k.t2[:, :, :], k.t2[:, :, :], rows_over(k.beta[:, :], NB), ALU.add))
                step(dve.tensor_tensor(k.x[:, :, :], k.x[:, :, :], k.t2[:, :, :], ALU.add))
                norm.dve(dve, step, k.h[:, :, :], k.x[:, :, :], k.t1[:, :, :], relu=True)
                norm.dve(dve, step, k.t2[:, :, :], k.h[:, :, :], k.t1[:, :, :])
                step(dve.tensor_tensor(k.t2[:, :, :], k.t2[:, :, :], rows_over(k.nlw[:, :], NB), ALU.mult))
                dve.tensor_tensor(k.t2[:, :, :], k.t2[:, :, :], rows_over(k.nlb[:, :], NB),
                                  ALU.add).then_inc(h_ready, 1)
                dve.wait_ge(zT_ready, 1)
                dve.tensor_copy(k.hT[0:D, :], ps[0:D, 0:NPAD]).then_inc(zTs_ready, 1)
                dve.wait_ge(n_ready, 1)
                step(dve.memset(k.wh[:, :, HALF:D], 0.0))
                step(dve.tensor_copy(k.wh[:, :, 0:HALF], m2[:, :, 0:HALF]))
                dve.scalar_tensor_tensor(k.wh[:, :, 0:HALF], k.wh[:, :, 0:HALF], 0.01,
                                         k.wh[:, :, 0:HALF], ALU.mult, ALU.max).then_inc(hn_ready, 1)
                dve.wait_ge(hn_ready, 1)
                norm.dve(dve, step, k.t2[:, :, :], k.wh[:, :, 0:D], k.t1[:, :, :])
                step(dve.tensor_tensor(k.t2[:, :, :], k.t2[:, :, :], rows_over(k.rlw_row[:, :], NB), ALU.mult))
                dve.tensor_tensor(k.t2[:, :, :], k.t2[:, :, :], rows_over(k.rlb_row[:, :], NB),
                                  ALU.add).then_inc(l_ready, 1)
                dve.wait_ge(lT_ready, 1)
                dve.tensor_copy(k.hT[0:D, :], ps[0:D, 0:NPAD]).then_inc(lTs_ready, 1)
                dve.wait_ge(e_ready, 1)
                step(dve.tensor_copy(k.t1[:, :, :], m2))
                step(dve.scalar_tensor_tensor(k.local[:, :, :], k.t1[:, :, :], 0.01, k.t1[:, :, :],
                                              ALU.mult, ALU.max))

            @block.sync
            def _(sp):
                sp.wait_ge(hn_ready, 1)
                sp.dma_start(k.t_hn.rearrange("(p b) d -> p b d", p=P),
                             k.wh[:, :, 0:HALF]).then_inc(stored, 16)
                sp.wait_ge(stored, 16)


def node3(nc, k):
    with Ctx(nc, "node3_") as c:
        step_s, a_ready, h_ready, stored = c.sems("dve_step", "sums_in_psum", "h_ready", "table_stored")
        norm = Norm(c, k)
        deg = c.sb("deg", [P, 2, NB])
        ps = c.ps("node_ps", [P, 8, 512])
        PER = 7
        with nc.Block() as block:
            @block.tensor
            def _(pe):
                pe.wait_ge(step_s, 1)
                for b in range(NB):
                    o = b % PER * (D + 1)
                    last = pe.transpose(ps[:, b // PER, o:o + D + 1], block_columns(k.acc[0], b),
                                        k.ident[0:D + 1, 0:D + 1])
                last.then_inc(a_ready, 1)

            @block.scalar
            def _(act):
                norm.act(act)

            @block.vector
            def _(dve):
                step = Chain(dve, step_s)
                step(dve.tensor_tensor(k.acc[0], k.acc[0], k.acc[1], ALU.add))
                dve.wait_ge(a_ready, 1)
                for g in range(-(-NB // PER)):
                    b0, b1 = g * PER, min(NB, (g + 1) * PER)
                    v = tiles3(ps[:, g, 0:(b1 - b0) * (D + 1)], b1 - b0)
                    step(dve.tensor_tensor(k.t1[:, b0:b1, :], v[:, :, 0:D], k.local[:, b0:b1, :], ALU.add))
                    step(dve.tensor_scalar(deg[:, 0, b0:b1], v[:, :, D], 1.0, None, ALU.add))
                step(dve.reciprocal(deg[:, 1, :], deg[:, 0, :]))
                step(dve.tensor_tensor(k.t1[:, :, :], k.t1[:, :, :], over(deg[:, 1, :], D), ALU.mult))
                step(dve.tensor_tensor(k.x[:, :, :], k.x[:, :, :], k.t1[:, :, :], ALU.add))
                norm.dve(dve, step, k.h[:, :, :], k.x[:, :, :], k.t1[:, :, :], relu=True)
                dve.sem_inc(h_ready, 1)

            @block.sync
            def _(sp):
                sp.wait_ge(h_ready, 1)
                sp.dma_start(k.t_h3.rearrange("(p b) d -> p b d", p=P), k.h[:, :, :]).then_inc(stored, 16)
                sp.wait_ge(stored, 16)


def node4(nc, k, out):
    L = 1.0507009873554805
    A = 1.6732632423543772
    with Ctx(nc, "node4_") as c:
        step_s, one_summed, two_summed, oT_ready, copied, o_ready, m_ready, e_ready, x_ready, stored = c.sems(
            "dve_step", "summed_by_gpsimd", "summed_by_vector", "heads_t_in_psum", "heads_t_ready", "heads_in_psum", "negative_part_ready", "exp_ready", "x_ready", "out_stored")
        ps = c.ps("node_ps", [P, 4096])
        half = NPAD // 1024 * 512
        oT = k.accT2[0:D, 0:NPAD]

        def part(acc, j):
            return acc[:, j * NPAD:(j + 1) * NPAD]

        with nc.Block() as block:
            @block.gpsimd
            def _(pool):
                nc.gpsimd.tensor_tensor(part(k.accT, 1), part(k.accT, 1), part(k.accT2, 1),
                                        ALU.add).then_inc(one_summed, 1)

            @block.tensor
            def _(pe):
                for i, (j, ready, count) in enumerate([(0, two_summed, 1), (2, two_summed, 2), (1, one_summed, 1)]):
                    pe.wait_ge(ready, count)
                    for o in range(0, NPAD, 512):
                        w = min(512, NPAD - o)
                        last = pe.matmul(ps[0:D, o:o + w], k.Wl_h[:, j, :], part(k.accT, j)[:, o:o + w],
                                         start=(i == 0), stop=(i == HP - 1))
                last.then_inc(oT_ready, 1)
                pe.wait_ge(copied, 2)
                for b in range(NB):
                    last = pe.transpose(ps[:, b * D:(b + 1) * D], block_columns(oT, b), k.ident[0:D, 0:D])
                last.then_inc(o_ready, 1)

            @block.scalar
            def _(act):
                act.wait_ge(oT_ready, 1)
                act.activation(oT[:, 0:half], ps[0:D, 0:half], ACT.Copy).then_inc(copied, 1)
                act.wait_ge(m_ready, 1)
                act.activation(k.t2[:, :, :], k.h[:, :, :], ACT.Exp).then_inc(e_ready, 1)

            @block.vector
            def _(dve):
                step = Chain(dve, step_s)
                for j in (0, 2):
                    dve.tensor_tensor(part(k.accT, j), part(k.accT, j), part(k.accT2, j),
                                      ALU.add).then_inc(two_summed, 1)
                dve.wait_ge(oT_ready, 1)
                dve.tensor_copy(oT[:, half:NPAD], ps[0:D, half:NPAD]).then_inc(copied, 1)
                dve.wait_ge(o_ready, 1)
                step(dve.tensor_tensor(k.t1[:, :, :], tiles3(ps[:, 0:NB * D], NB),
                                       rows_over(k.bias3[:, :], NB), ALU.add))
                dve.tensor_scalar(k.h[:, :, :], k.t1[:, :, :], 0.0, None, ALU.min).then_inc(m_ready, 1)
                step(dve.tensor_scalar(k.t1[:, :, :], k.t1[:, :, :], 0.0, L, ALU.max, ALU.mult))
                step(dve.tensor_tensor(k.x[:, :, :], k.x[:, :, :], k.t1[:, :, :], ALU.add))
                dve.wait_ge(e_ready, 1)
                step(dve.tensor_scalar(k.t2[:, :, :], k.t2[:, :, :], -1.0, L * A, ALU.add, ALU.mult))
                dve.tensor_tensor(k.x[:, :, :], k.x[:, :, :], k.t2[:, :, :], ALU.add).then_inc(x_ready, 1)

            @block.sync
            def _(sp):
                full = N // NB
                sp.wait_ge(x_ready, 1)
                sp.dma_start(out[0:full * NB, :].rearrange("(p b) d -> p b d", b=NB),
                             k.x[0:full, :, :]).then_inc(stored, 16)
                sp.dma_start(out[full * NB:N, :].rearrange("(p b) d -> p b d", p=1),
                             k.x[full:full + 1, 0:N - full * NB, :]).then_inc(stored, 16)
                sp.wait_ge(stored, 32)


class Gather:

    def __init__(self, c, k, table, slot, free):
        self.k, self.table, self.slot, self.free = k, table, slot, free
        self.idx = [c.sb(f"gather_idx{h}", [P, B], I32) for h in (0, 1)]
        self.gate = c.sem("pool_gate")
        self.idx_loaded = [c.sem(f"idx_loaded{h}") for h in (0, 1)]
        self.gathered = [c.sem(f"gathered{h}") for h in (0, 1)]

    def load(self, sp, t, h):
        wait_past(sp, self.gathered[h], B * 16 * t)
        sp.dma_start(self.idx[h][:, :], self.k.src_t[:, bass.ds(t * 2 * B + h * B, B)]
                     ).then_inc(self.idx_loaded[h], 16)

    def gather(self, nc, pool, t, h, kept=None):
        n = 2 * t + h + 1
        pool.wait_ge(self.idx_loaded[h], 16 * (t + 1))
        pool.wait_ge(self.free, n)
        if kept:
            wait_past(pool, kept[h], 16 * t)
        pool.sem_inc(self.gate, 1)
        for j in range(B):
            nc.gpsimd.indirect_dma_start(
                self.slot(h, j), None, self.table[:, :],
                bass.IndirectOffsetOnAxis(ap=self.idx[h][:, j:j + 1], axis=0)).then_inc(self.gathered[h], 16)

    def loop(self, nc, pool, kept=None):
        def body(t, last):
            self.gather(nc, pool, t, 0, kept)
            self.gather(nc, pool, t, 1, kept)
        pairs(pool, body)


def window_starts(nc, k, engine, t, h):
    return nc.values_load_multi_w_load_instructions(
        k.dst_i[0:1, bass.ds(t * 2 * B + h * B, B)], [engine], min_val=0, max_val=N,
        skip_runtime_bounds_check_because="dst is a node's number, 0 to N - 1, or N in the padding")[1]


def onehot(dve, k, out, t, h):
    return dve.tensor_tensor(out, over(k.dst_rel[:, bass.ds(t * 2 * B + h * B, B)], P),
                             rows_over(k.row0[:, :], B), ALU.is_equal)


def edge0(nc, k):
    with Ctx(nc, "edge0_") as c:
        g = [c.sb(f"src_rows{h}", [P, B, WH]) for h in (0, 1)]
        win = [c.sb(f"window{h}", [P, B, WH]) for h in (0, 1)]
        drow = [c.sb(f"dst_row{h}", [P, ROWS], I32) for h in (0, 1)]
        srow = [c.sb(f"src_row{h}", [P, ROWS], I32) for h in (0, 1)]
        oht = [c.sb(f"onehot_t{h}", [P, ROWS]) for h in (0, 1)]
        same = [c.sb(f"same_src{h}", [P, ROWS]) for h in (0, 1)]
        vw = [c.sb(f"weighted{h}", [P, B, D]) for h in (0, 1)]
        val = [c.sb(f"sums{h}", [P, B, D]) for h in (0, 1)]
        sidx = [c.sb(f"scatter_idx{h}", [P, B], I32) for h in (0, 1)]
        rank = c.sb("rank", [P, ROWS])
        prod = c.sb("prod", [P, B, D])
        s = c.sb("small", [P, 16, B])
        wc = [c.ps(f"dst_rows_ps{h}", [P, B, P]) for h in (0, 1)]
        dup = [c.ps(f"sums_ps{h}", [P, B, D]) for h in (0, 1)]
        rows_ready = [c.sem(f"rows_loaded{h}") for h in (0, 1)]
        win_ready = [c.sem(f"window_loaded{h}") for h in (0, 1)]
        scattered = [c.sem(f"scattered{h}") for h in (0, 1)]
        (oht_ready, same_ready, vw_ready, wc_ready, dup_ready, val_ready, sidx_ready) = c.sems(
            "onehot_ready", "same_ready", "weighted_ready", "dst_rows_in_psum", "sums_in_psum",
            "sums_ready", "scatter_idx_ready")
        (rank_done, last_done, stands_done, moved_done, prod_done, norms_done, dot_done, floor_done,
         recip_done, sim_done, parts_done, signed_done, weight_done) = c.sems(
            "rank_done", "last_done", "stands_done", "moved_done", "prod_done", "norms_done",
            "dot_done", "floor_done", "recip_done", "sim_done", "parts_done", "signed_done",
            "weight_done")
        ga = Gather(c, k, k.t_wh, lambda h, j: g[h][:, j, :], norms_done)
        with nc.Block() as block:
            @block.sync
            def _(sp):
                def body(t, last):
                    for h in (0, 1):
                        n = 2 * t + h + 1
                        ga.load(sp, t, h)
                        sp.wait_ge(wc_ready, n)
                        sp.wait_ge(same_ready, n)
                        sp.dma_start(drow[h][:, :], k.dst_row[bass.ds(2 * t + h, 1), :].to_broadcast([P, ROWS])
                                     ).then_inc(rows_ready[h], 16)
                        sp.dma_start(srow[h][:, :], k.src_row[bass.ds(2 * t + h, 1), :].to_broadcast([P, ROWS])
                                     ).then_inc(rows_ready[h], 16)
                        for j, base in enumerate(window_starts(nc, k, SP, t, h)):
                            sp.dma_start(win[h][:, j, :], k.t_wh[bass.ds(base, P), :]
                                         ).then_inc(win_ready[h], 16)
                pairs(sp, body)

            @block.gpsimd
            def _(pool):
                def scatter(n, h, t):
                    pool.wait_ge(val_ready, n + 2)
                    pool.wait_ge(sidx_ready, n)
                    wait_past(pool, scattered[1 - h], B * 16 * (t + h))
                    pool.sem_inc(ga.gate, 1)
                    for j in range(B):
                        nc.gpsimd.indirect_dma_start(
                            k.scatter_sums[j], bass.IndirectOffsetOnAxis(ap=sidx[h][:, j:j + 1], axis=0),
                            val[h][:, j, :], None, compute_op=ALU.add).then_inc(scattered[h], 16)

                ga.gather(nc, pool, 0, 0)

                def body(t, last):
                    ga.gather(nc, pool, t, 1)
                    scatter(2 * t + 1, 0, t)
                    if not last:
                        ga.gather(nc, pool, t + 1, 0)
                    scatter(2 * t + 2, 1, t)
                pairs(pool, body)
                for h in (0, 1):
                    pool.wait_ge(scattered[h], B * 16 * PAIRS)

            @block.tensor
            def _(pe):
                pe.sem_inc(wc_ready, 2)
                pe.sem_inc(dup_ready, 2)

                def body(t, last):
                    for h in (0, 1):
                        n = 2 * t + h + 1
                        pe.wait_ge(win_ready[h], B * 16 * (t + 1))
                        pe.wait_ge(oht_ready, n)
                        for j in range(B):
                            last_mm = pe.matmul(wc[h][:, j, 0:WH], oht[h][:, j * P:(j + 1) * P],
                                                win[h][:, j, :], start=True, stop=True)
                        last_mm.then_inc(wc_ready, 1)
                        pe.wait_ge(vw_ready, n)
                        pe.wait_ge(val_ready, n)
                        for j in range(B):
                            mm = pe.matmul(dup[h][:, j, :], same[h][:, j * P:(j + 1) * P],
                                           vw[h][:, j, :], start=True, stop=True)
                        mm.then_inc(dup_ready, 1)
                pairs(pe, body)

            @block.scalar
            def _(act):
                act.sem_inc(val_ready, 2)

                def body(t, last):
                    for h in (0, 1):
                        n = 2 * t + h + 1
                        act.wait_ge(dup_ready, n + 2)
                        wait_past(act, scattered[h], B * 16 * t)
                        act.activation(val[h][:, :, :], dup[h][:, :, :], ACT.Copy).then_inc(val_ready, 1)
                pairs(act, body)

            @block.vector
            def _(dve):
                dve.sem_inc(same_ready, 2)
                dve.sem_inc(norms_done, 2)

                def body(t, last):
                    for h in (0, 1):
                        n = 2 * t + h + 1
                        cols = bass.ds(t * 2 * B + h * B, B)
                        dve.wait_ge(rows_ready[h], 32 * (t + 1))
                        dve.tensor_tensor(tiles3(oht[h][:, :]), tiles3(drow[h][:, :]),
                                          over(k.win_node[:, cols], P), ALU.is_equal).then_inc(oht_ready, 1)
                        dve.wait_ge(dup_ready, n)
                        dve.tensor_tensor(tiles3(same[h][:, :]), tiles3(srow[h][:, :]),
                                          over(k.src_f[:, cols], P), ALU.is_equal).then_inc(same_ready, 1)
                        dve.wait_ge(same_ready, n + 2)
                        dve.tensor_tensor(tiles3(rank[:, :]), tiles3(same[h][:, :]),
                                          rows_over(k.row1[:, :], B), ALU.mult).then_inc(rank_done, 1)
                        dve.wait_ge(rank_done, n)
                        dve.tensor_reduce(s[:, 0, :], tiles3(rank[:, :]), AX, ALU.max).then_inc(last_done, 1)
                        dve.wait_ge(last_done, n)
                        dve.tensor_scalar(s[:, 1, :], s[:, 0, :], k.col1[:, :], None,
                                          ALU.is_equal).then_inc(stands_done, 1)
                        dve.wait_ge(stands_done, n)
                        dve.tensor_tensor(s[:, 2, :], s[:, 1, :], k.src_sp[:, cols],
                                          ALU.mult).then_inc(moved_done, 1)
                        dve.wait_ge(moved_done, n)
                        wait_past(dve, scattered[h], B * 16 * t)
                        dve.tensor_scalar(sidx[h][:, :], s[:, 2, :], k.spare_row[:, :], None,
                                          ALU.add).then_inc(sidx_ready, 1)
                        dve.wait_ge(ga.gathered[h], B * 16 * (t + 1))
                        dve.wait_ge(wc_ready, n + 2)
                        dve.tensor_tensor(prod[:, :, :], g[h][:, :, 0:D], wc[h][:, :, 0:D],
                                          ALU.mult).then_inc(prod_done, 1)
                        dve.tensor_tensor(s[:, 3, :], g[h][:, :, D], wc[h][:, :, D],
                                          ALU.mult).then_inc(norms_done, 1)
                        dve.wait_ge(norms_done, n + 2)
                        dve.tensor_reduce(s[:, 4, :], prod[:, :, :], AX, ALU.add).then_inc(dot_done, 1)
                        dve.tensor_scalar(s[:, 5, :], s[:, 3, :], 1e-8, None, ALU.max).then_inc(floor_done, 1)
                        dve.wait_ge(floor_done, n)
                        dve.reciprocal(s[:, 6, :], s[:, 5, :]).then_inc(recip_done, 1)
                        dve.wait_ge(recip_done, n)
                        dve.tensor_tensor(s[:, 7, :], s[:, 4, :], s[:, 6, :], ALU.mult).then_inc(sim_done, 1)
                        dve.wait_ge(sim_done, n)
                        dve.tensor_scalar(s[:, 8, :], s[:, 7, :], 0.0, k.coeff_s[:, 0:1], ALU.max, ALU.mult)
                        dve.tensor_scalar(s[:, 9, :], s[:, 7, :], 0.0, k.coeff_s[:, 1:2], ALU.min,
                                          ALU.mult).then_inc(parts_done, 1)
                        dve.wait_ge(parts_done, n)
                        dve.tensor_tensor(s[:, 10, :], s[:, 8, :], s[:, 9, :], ALU.add).then_inc(signed_done, 1)
                        dve.wait_ge(signed_done, n)
                        dve.tensor_tensor(s[:, 11, :], s[:, 10, :], k.weight[:, cols],
                                          ALU.mult).then_inc(weight_done, 1)
                        dve.wait_ge(weight_done, n)
                        dve.tensor_tensor(vw[h][:, :, :], wc[h][:, :, 0:D], over(s[:, 11, :], D),
                                          ALU.mult).then_inc(vw_ready, 1)
                pairs(dve, body)


def accumulate(nc, dve, k, ps, rows, t, h, n, added):
    for j, base in enumerate(window_starts(nc, k, DVE, t, h)):
        dve.wait_ge(added[j - 2], n if j != 1 else n + 1)
        acc = k.acc[j % 2][0:rows, bass.ds(base, P)]
        dve.tensor_tensor(acc, acc, ps[0:rows, j, :], ALU.add).then_inc(added[j], 1)


def edge1(nc, k):
    with Ctx(nc, "edge1_") as c:
        g = [c.sb(f"src_rows{h}", [P, B, D]) for h in (0, 1)]
        ea = [c.sb(f"edge_attr{h}", [32, ROWS]) for h in (0, 1)]
        oh = [c.sb(f"onehot{h}", [P, B, P]) for h in (0, 1)]
        msg = [c.sb(f"msg{h}", [P, B, D]) for h in (0, 1)]
        m = [c.ps(f"msg_ps{h}", [P, B, D]) for h in (0, 1)]
        sp_ = [c.ps(f"sums_ps{h}", [D, B, P]) for h in (0, 1)]
        ea_ready = [c.sem(f"edge_attr_loaded{h}") for h in (0, 1)]
        oh_ready, m_ready, msg_ready, sums_ready = c.sems(
            "onehot_ready", "msg_in_psum", "msg_ready", "sums_in_psum")
        ga = Gather(c, k, k.t_h, lambda h, j: g[h][:, j, :], m_ready)
        added = [c.sem(f"added{j}") for j in range(B)]
        with nc.Block() as block:
            @block.sync
            def _(sp):
                def body(t, last):
                    for h in (0, 1):
                        ga.load(sp, t, h)
                        sp.wait_ge(m_ready, 2 * t + h + 1)
                        sp.dma_start(ea[h][:, :], k.ea32[bass.ds(2 * t + h, 1)].rearrange("a f e -> (a f) e")
                                     ).then_inc(ea_ready[h], 16)
                pairs(sp, body)

            @block.gpsimd
            def _(pool):
                ga.loop(nc, pool)

            @block.tensor
            def _(pe):
                def messages(n, h, tt):
                    pe.wait_ge(msg_ready, n)
                    pe.wait_ge(ea_ready[h], 16 * tt)
                    pe.wait_ge(ga.gathered[h], B * 16 * tt)
                    pe.matmul(m[h][:, :, :], k.ident[:, :], g[h][:, :, :], start=True, stop=False)
                    for j in range(B):
                        mm = pe.matmul(m[h][:, j, :], ea[h][:, j * P:(j + 1) * P], k.We[:, :],
                                       start=False, stop=(j == B - 1))
                    mm.then_inc(m_ready, 1)

                pe.sem_inc(sums_ready, 2)
                pe.sem_inc(m_ready, 2)
                messages(1, 0, 1)

                def body(t, last):
                    for h in (0, 1):
                        n = 2 * t + h + 1
                        if not (last and h):
                            messages(n + 1, 1 - h, t + 1 + h)
                        pe.wait_ge(added[B - 1], n)
                        pe.wait_ge(oh_ready, n)
                        pe.wait_ge(msg_ready, n + 2)
                        for j in range(B):
                            mm = pe.matmul(sp_[h][:, j, :], msg[h][:, j, :], oh[h][:, j, :],
                                           start=True, stop=True)
                        mm.then_inc(sums_ready, 1)
                pairs(pe, body)

            @block.scalar
            def _(act):
                act.sem_inc(msg_ready, 2)

                def body(t, last):
                    for h in (0, 1):
                        n = 2 * t + h + 1
                        act.wait_ge(m_ready, n + 2)
                        act.wait_ge(sums_ready, n)
                        act.activation(msg[h][:, :, :], m[h][:, :, :], ACT.Relu).then_inc(msg_ready, 1)
                pairs(act, body)

            @block.vector
            def _(dve):
                dve.sem_inc(added[B - 2], 1)
                dve.sem_inc(added[B - 1], 2)
                onehot(dve, k, oh[0][:, :, :], 0, 0).then_inc(oh_ready, 1)

                def body(t, last):
                    for h in (0, 1):
                        n = 2 * t + h + 1
                        if not (last and h):
                            onehot(dve, k, oh[1 - h][:, :, :], t + h, 1 - h).then_inc(oh_ready, 1)
                        dve.wait_ge(sums_ready, n + 2)
                        accumulate(nc, dve, k, sp_[h], D, t, h, n, added)
                pairs(dve, body)


def edge2(nc, k):
    with Ctx(nc, "edge2_") as c:
        cat = [c.sb(f"cat{h}", [P, B, D]) for h in (0, 1)]
        ea = [c.sb(f"edge_attr{h}", [D, ROWS]) for h in (0, 1)]
        oh = [c.sb(f"onehot{h}", [P, B, P]) for h in (0, 1)]
        msg = [c.sb(f"msg{h}", [P, B, D + 1]) for h in (0, 1)]
        catT = c.sb("cat_t", [D, ROWS])
        junk = c.sb("squares", [P, 2, B, D])
        st = c.sb("stat", [P, 6, B])
        he = c.sb("he_pre", [P, B, HALF])
        he2 = c.sb("he_pre2", [P, B, HALF])
        u, u2 = c.sb("u", [P, B, D]), c.sb("u2", [P, B, D])
        hep = c.ps("he_ps", [P, B, P])
        catTp = c.ps("cat_t_ps", [D, ROWS])
        rp = c.ps("msg_ps", [P, B, P])
        sums = c.ps("sums_ps", [D + 1, B, P])
        ea_ready = [c.sem(f"edge_attr_loaded{h}") for h in (0, 1)]
        (hep_ready, sq1, std1_ready, inv1, he_sc, he_b, cat_ready, catTp_ready, catT_ready, rp_ready,
         sq2, std2_ready, inv2, u_sc, u_b, oh_ready, msg_ready, sums_ready, ones_ready) = c.sems(
            "he_in_psum", "squares1_done", "std1_ready", "inverse1_done", "he_scaled", "he_shifted",
            "cat_ready", "cat_t_in_psum", "cat_t_ready", "msg_in_psum", "squares2_done", "std2_ready",
            "inverse2_done", "msg_scaled", "msg_shifted", "onehot_ready", "msg_ready", "sums_in_psum",
            "ones_ready")
        ga = Gather(c, k, k.t_hn, lambda h, j: cat[h][:, j, 0:HALF], catTp_ready)
        added = [c.sem(f"added{j}") for j in range(B)]

        with nc.Block() as block:
            @block.sync
            def _(sp):
                def body(t, last):
                    for h in (0, 1):
                        ga.load(sp, t, h)
                        wait_past(sp, hep_ready, 2 * t + h - 1)
                        sp.dma_start(ea[h][:, :], k.ea64[bass.ds(2 * t + h, 1)].rearrange("a f e -> (a f) e")
                                     ).then_inc(ea_ready[h], 16)
                pairs(sp, body)

            @block.gpsimd
            def _(pool):
                ga.loop(nc, pool)

            @block.tensor
            def _(pe):
                def edge_part(h, tt):
                    pe.wait_ge(ea_ready[h], 16 * tt)
                    for j in range(B):
                        mm = pe.matmul(hep[:, j, 0:HALF + D], ea[h][:, j * P:(j + 1) * P], k.eR[:, :],
                                       start=True, stop=True)
                    mm.then_inc(hep_ready, 1)

                def sum_up(n, h):
                    pe.wait_ge(msg_ready, n)
                    pe.wait_ge(oh_ready, n)
                    for j in range(B):
                        mm = pe.matmul(sums[:, j, :], msg[h][:, j, :], oh[h][:, j, :], start=True, stop=True)
                    mm.then_inc(sums_ready, 1)

                pe.sem_inc(catTp_ready, 2)
                edge_part(0, 1)
                pe.wait_ge(ones_ready, 1)

                def body(t, first, last):
                    for h in (0, 1):
                        n = 2 * t + h + 1
                        pe.wait_ge(ga.gathered[h], B * 16 * (t + 1))
                        pe.wait_ge(cat_ready, n)
                        for j in range(B):
                            if j == 0:
                                mm = pe.matmul(catTp[:, 0:P], cat[h][:, 0, :], k.ident[:, :],
                                               start=True, stop=True)
                            else:
                                mm = pe.transpose(catTp[:, j * P:(j + 1) * P], cat[h][:, j, :], k.ident[:, :])
                        mm.then_inc(catTp_ready, 1)
                        if not (last and h):
                            edge_part(1 - h, t + 1 + h)
                        pe.wait_ge(catT_ready, n)
                        if not (first and h == 0):
                            pe.wait_ge(u_sc, n - 1)
                        for j in range(B):
                            mm = pe.matmul(rp[:, j, :], catT[:, j * P:(j + 1) * P], k.rR[:, :],
                                           start=True, stop=True)
                        mm.then_inc(rp_ready, 1)
                        if not (first and h == 0):
                            if not (first and h == 1):
                                pe.wait_ge(added[B - 1], n)
                            sum_up(n - 1, 1 - h)
                ends_apart(pe, body)
                pe.wait_ge(added[B - 1], BATCHES + 1)
                sum_up(BATCHES, 1)

            @block.scalar
            def _(act):
                def root(ps, q, n, sq, ready):
                    for j in range(B):
                        a = act.activation(junk[:, q, j, :], ps[:, j, :], ACT.Square,
                                           accum_out=st[:, 3 * q, j:j + 1])
                    a.then_inc(sq, 1)
                    act.wait_ge(sq, n)
                    act.activation(st[:, 3 * q + 1, :], st[:, 3 * q, :], ACT.Sqrt, bias=k.eps[:, :],
                                   scale=1.0 / D).then_inc(ready, 1)

                act.wait_ge(hep_ready, 1)
                root(hep[:, :, HALF:HALF + D], 0, 1, sq1, std1_ready)

                def body(t, first, last):
                    for h in (0, 1):
                        n = 2 * t + h + 1
                        act.wait_ge(catTp_ready, n + 2)
                        act.activation(catT[:, :], catTp[:, :], ACT.Copy).then_inc(catT_ready, 1)
                        if not (last and h):
                            act.wait_ge(hep_ready, n + 1)
                            root(hep[:, :, HALF:HALF + D], 0, n + 1, sq1, std1_ready)
                        act.wait_ge(rp_ready, n)
                        root(rp[:, :, D:2 * D], 1, n, sq2, std2_ready)
                ends_apart(act, body)

            @block.vector
            def _(dve):
                dve.sem_inc(added[B - 2], 1)
                dve.sem_inc(added[B - 1], 2)
                dve.memset(msg[0][:, :, D], 1.0)
                dve.memset(msg[1][:, :, D], 1.0).then_inc(ones_ready, 1)

                def edge_row(n, h):
                    dve.wait_ge(std1_ready, n)
                    dve.reciprocal(st[:, 2, :], st[:, 1, :]).then_inc(inv1, 1)
                    dve.wait_ge(inv1, n)
                    dve.tensor_tensor(he[:, :, :], hep[:, :, 0:HALF], over(st[:, 2, :], HALF),
                                      ALU.mult).then_inc(he_sc, 1)
                    dve.wait_ge(he_sc, n)
                    dve.tensor_tensor(he2[:, :, :], he[:, :, :], rows_over(k.ec[:, :], B),
                                      ALU.add).then_inc(he_b, 1)
                    dve.wait_ge(he_b, n)
                    dve.scalar_tensor_tensor(cat[h][:, :, HALF:D], he2[:, :, :], 0.01, he2[:, :, :],
                                             ALU.mult, ALU.max).then_inc(cat_ready, 1)

                def message(n, h):
                    dve.wait_ge(std2_ready, n)
                    dve.reciprocal(st[:, 5, :], st[:, 4, :]).then_inc(inv2, 1)
                    dve.wait_ge(inv2, n)
                    dve.tensor_tensor(u[:, :, :], rp[:, :, 0:D], over(st[:, 5, :], D),
                                      ALU.mult).then_inc(u_sc, 1)
                    dve.wait_ge(u_sc, n)
                    dve.tensor_tensor(u2[:, :, :], u[:, :, :], rows_over(k.rc[:, :], B),
                                      ALU.add).then_inc(u_b, 1)
                    dve.wait_ge(u_b, n)
                    dve.scalar_tensor_tensor(msg[h][:, :, 0:D], u2[:, :, :], 0.01, u2[:, :, :],
                                             ALU.mult, ALU.max).then_inc(msg_ready, 1)

                def add(n, h, t):
                    dve.wait_ge(sums_ready, n)
                    accumulate(nc, dve, k, sums, D + 1, t, h, n, added)

                def body(t, first, last):
                    for h in (0, 1):
                        n = 2 * t + h + 1
                        edge_row(n, h)
                        if not (first and h == 0):
                            onehot(dve, k, oh[1 - h][:, :, :], t - 1 + h, 1 - h).then_inc(oh_ready, 1)
                        if not first:
                            add(n - 2, h, t - 1)
                        if not (first and h == 0):
                            message(n - 1, 1 - h)
                ends_apart(dve, body)
                onehot(dve, k, oh[1][:, :, :], PAIRS - 1, 1).then_inc(oh_ready, 1)
                add(BATCHES - 1, 0, PAIRS - 1)
                message(BATCHES, 1)
                add(BATCHES, 1, PAIRS - 1)


def edge3a(nc, k):
    with Ctx(nc, "edge3a_") as c:
        g = [c.sb(f"src_rows{h}", [P, B, D]) for h in (0, 1)]
        win = [c.sb(f"window{h}", [P, B, D]) for h in (0, 1)]
        drow = [c.sb(f"dst_row{h}", [P, ROWS], I32) for h in (0, 1)]
        oht = [c.sb(f"onehot_t{h}", [P, ROWS]) for h in (0, 1)]
        hcT = [c.sb(f"both_ends_t{h}", [P, ROWS]) for h in (0, 1)]
        terms = c.sb("terms", [P, B, H * ZH])
        scs = [c.sb(f"scores{h}", [P, H, B]) for h in (0, 1)]
        scT = [c.sb(f"scores_t{h}", [H * B, P]) for h in (0, 1)]
        hcTp = c.ps("both_ends_t_ps", [P, ROWS])
        zp = [c.ps(f"z_ps{b}", [P, 2, 512]) for b in (0, 1)]
        scTp = c.ps("scores_t_ps", [H * B, P])
        rows_ready = [c.sem(f"rows_loaded{h}") for h in (0, 1)]
        win_ready = [c.sem(f"window_loaded{h}") for h in (0, 1)]
        kept = [c.sem(f"rows_kept{h}") for h in (0, 1)]
        stored = [c.sem(f"scores_stored{h}") for h in (0, 1)]
        oht_ready, hcTp_ready, hcT_ready, z_ready, terms_ready, summed, scTp_ready, scT_ready = c.sems(
            "onehot_ready", "both_ends_t_in_psum", "both_ends_t_ready", "z_in_psum", "terms_ready",
            "terms_summed", "scores_t_in_psum", "scores_t_ready")
        ga = Gather(c, k, k.t_h3, lambda h, j: g[h][:, j, :], hcTp_ready)
        with nc.Block() as block:
            @block.sync
            def _(sp):
                def load(t, h):
                    n = 2 * t + h + 1
                    sp.wait_ge(hcTp_ready, n)
                    sp.wait_ge(oht_ready, n)
                    sp.dma_start(drow[h][:, :], k.dst_row[bass.ds(2 * t + h, 1), :].to_broadcast([P, ROWS])
                                 ).then_inc(rows_ready[h], 16)
                    for j, base in enumerate(window_starts(nc, k, SP, t, h)):
                        sp.dma_start(win[h][:, j, :], k.t_h3[bass.ds(base, P), :]
                                     ).then_inc(win_ready[h], 16)

                ga.load(sp, 0, 0)
                ga.load(sp, 0, 1)
                load(0, 0)
                load(0, 1)

                def body(t, last):
                    for h in (0, 1):
                        sp.wait_ge(ga.gathered[h], B * 16 * (t + 1))
                        if not last:
                            ga.load(sp, t + 1, h)
                        sp.dma_start(k.kept[bass.ds(2 * t + h, 1)].rearrange("a p (b d) -> (a p) b d", b=B),
                                     g[h][:, :, :]).then_inc(kept[h], 16)
                        if not last:
                            load(t + 1, h)
                pairs(sp, body)
                for h in (0, 1):
                    sp.wait_ge(kept[h], 16 * PAIRS)

            @block.gpsimd
            def _(pool):
                ga.loop(nc, pool, kept)

            @block.tensor
            def _(pe):
                pe.sem_inc(hcTp_ready, 2)
                pe.sem_inc(z_ready, 8)
                pe.sem_inc(scTp_ready, 2)

                def turn(n, h, tt):
                    pe.wait_ge(hcT_ready, n)
                    pe.wait_ge(oht_ready, n + 2)
                    pe.wait_ge(win_ready[h], B * 16 * tt)
                    for j in range(B):
                        cols = slice(j * P, (j + 1) * P)
                        pe.matmul(hcTp[D:P, cols], win[h][:, j, :], oht[h][:, cols], start=True, stop=True)
                    pe.wait_ge(ga.gathered[h], B * 16 * tt)
                    for j in range(B):
                        cols = slice(j * P, (j + 1) * P)
                        mm = pe.matmul(hcTp[0:D, cols], g[h][:, j, :], k.ident[:, :], start=True, stop=True)
                    mm.then_inc(hcTp_ready, 1)

                def project(n, h, q):
                    pe.wait_ge(terms_ready, 4 * (n - 1) + q + 1)
                    for i in (0, 1):
                        j = 2 * q + i
                        mm = pe.matmul(zp[q % 2][:, i, 0:H * ZH], hcT[h][:, j * P:(j + 1) * P],
                                       k.Wz[:, :], start=True, stop=True)
                    mm.then_inc(z_ready, 1)

                def turn_scores(n, h):
                    pe.wait_ge(scT_ready, n)
                    pe.wait_ge(summed, 2 * n + 4)
                    pe.matmul(scTp[:, :], scs[h][:, :, :].rearrange("p h b -> p (h b)"), k.ident[:, :],
                              start=True, stop=True).then_inc(scTp_ready, 1)

                turn(1, 0, 1)

                def body(t, first, last):
                    for h in (0, 1):
                        n = 2 * t + h + 1
                        pe.wait_ge(hcT_ready, n + 1)
                        project(n, h, 0)
                        project(n, h, 1)
                        if not (last and h):
                            turn(n + 1, 1 - h, t + 1 + h)
                        if not (first and h == 0):
                            turn_scores(n - 1, 1 - h)
                        project(n, h, 2)
                        project(n, h, 3)
                ends_apart(pe, body)
                turn_scores(BATCHES, 1)

            @block.scalar
            def _(act):
                act.sem_inc(hcT_ready, 1)
                act.sem_inc(scT_ready, 1)

                def turned(n, h):
                    act.wait_ge(hcTp_ready, n + 2)
                    act.wait_ge(z_ready, 4 * n)
                    act.activation(hcT[h][:, :], hcTp[:, :], ACT.Copy).then_inc(hcT_ready, 1)

                def store(n, h, at, tt):
                    act.wait_ge(scTp_ready, n + 2)
                    wait_past(act, stored[h], 16 * tt)
                    act.activation(scT[h][:, :], scTp[:, :], ACT.Copy).then_inc(scT_ready, 1)
                    act.wait_ge(scT_ready, n + 1)
                    act.dma_start(k.scores_d[:, bass.ds(at, 1)].rearrange("h a b e -> h (a b) e"),
                                  scT[h][:, :]).then_inc(stored[h], 16)

                turned(1, 0)

                def body(t, first, last):
                    for h in (0, 1):
                        n = 2 * t + h + 1
                        if not (last and h):
                            turned(n + 1, 1 - h)
                        if not (first and h == 0):
                            store(n - 1, 1 - h, 2 * t + h - 1, t - 1 + h)
                body(0, True, False)
                body(1, False, False)
                with act.Fori(2, PAIRS - 1) as t:
                    body(t, False, False)
                body(PAIRS - 1, False, True)
                store(BATCHES, 1, BATCHES - 1, PAIRS - 1)
                for h in (0, 1):
                    act.wait_ge(stored[h], 16 * PAIRS)

            @block.vector
            def _(dve):
                dve.sem_inc(oht_ready, 2)
                dve.sem_inc(terms_ready, 2)
                dve.sem_inc(summed, 4)

                def onehot_t(n, h, t):
                    dve.wait_ge(hcTp_ready, n)
                    dve.wait_ge(rows_ready[h], 16 * (t + 1))
                    dve.tensor_tensor(tiles3(oht[h][:, :]), tiles3(drow[h][:, :]),
                                      over(k.win_node[:, bass.ds(t * 2 * B + h * B, B)], P),
                                      ALU.is_equal).then_inc(oht_ready, 1)

                def weigh(n, q):
                    dve.wait_ge(z_ready, 4 * (n - 1) + q + 9)
                    dve.wait_ge(summed, 2 * n + q // 2 + 1)
                    dve.scalar_tensor_tensor(terms[:, 2 * q:2 * q + 2, :], zp[q % 2][:, :, 0:H * ZH], 0.0,
                                             rows_over(k.att_z[:, :], 2), ALU.max, ALU.mult
                                             ).then_inc(terms_ready, 1)

                def sum_terms(n, h, half):
                    dve.wait_ge(terms_ready, 4 * (n - 1) + 2 * half + 4)
                    dve.wait_ge(scTp_ready, n)
                    j = half * B // 2
                    dve.tensor_reduce(scs[h][:, :, j:j + B // 2].rearrange("p h b -> p b h"),
                                      terms[:, j:j + B // 2, :].rearrange("p b (h f) -> p b h f", h=H),
                                      AX, ALU.add).then_inc(summed, 1)

                onehot_t(1, 0, 0)
                onehot_t(2, 1, 0)

                def body(t, last):
                    for h in (0, 1):
                        n = 2 * t + h + 1
                        weigh(n, 0)
                        weigh(n, 1)
                        sum_terms(n, h, 0)
                        if not last:
                            onehot_t(n + 2, h, t + 1)
                        weigh(n, 2)
                        weigh(n, 3)
                        sum_terms(n, h, 1)
                pairs(dve, body)


def softmax(nc, k):
    Q = P
    BY_DVE = 4
    sc = k.accT[0:Q, 0:H * TILES].rearrange("p (h e) -> p h e", h=H)
    with Ctx(nc, "softmax_") as c:
        mx = c.sb("running", [Q, H, TILES])
        ids = c.sb("dst_seq", [Q, TILES + 2], I32)
        start = c.sb("starts", [Q, TILES])
        end = c.sb("ends", [Q, TILES])
        keep = c.sb("keeps", [Q, TILES])
        src = c.sb("src", [Q, TILES], I32)
        loop = c.sb("loop", [Q, 1, TILES])
        times = c.sb("times", [Q, 1, TILES])
        edge = c.sb("edge", [Q, 2, H])
        edgeT = c.sb("edge_t", [H, 2, Q])
        carryT = c.sb("carry_t", [H, Q + 2])
        carry = c.sb("carry", [Q, H])
        counted, counted_p, inverted = c.sems("counted_by_vector", "counted_by_gpsimd", "inverted")
        loaded, step_s, edge_ready, edgeT_ready, carryT_ready, carry_ready, m_ready, p_ready, a_ready, stored = c.sems(
            "loaded", "dve_step", "edge_ready", "edge_t_ready", "carry_t_ready", "carry_ready",
            "shifted_ready", "exp_ready", "alpha_ready", "alpha_stored")
        ps = c.ps("carry_ps", [P, 512])
        with nc.Block() as block:
            @block.sync
            def _(sp):
                runs = k.scores_d.rearrange("h n b e -> h (n b e)").rearrange("h (q e) -> q h e", q=Q)
                sp.dma_start(sc, runs).then_inc(loaded, 16)
                sp.dma_start(ids[:, 0:TILES], k.dst_seq[0:Q * TILES].rearrange("(q e) -> q e", q=Q)
                             ).then_inc(loaded, 16)
                sp.dma_start(ids[:, TILES:TILES + 2],
                             k.dst_seq[TILES:TILES + Q * TILES].rearrange("(q e) -> q e", q=Q)[:, 0:2]
                             ).then_inc(loaded, 16)
                sp.dma_start(src[:, :], k.src_run[:, :]).then_inc(loaded, 16)
                for h in range(H):
                    sp.wait_ge(a_ready, h + 1)
                    sp.dma_start(runs[:, h, :], mx[:, h, :]).then_inc(stored, 16)
                sp.wait_ge(stored, 16 * H)

            @block.gpsimd
            def _(pool):
                for h in range(BY_DVE, H):
                    pool.wait_ge(p_ready, h + 1)
                    nc.gpsimd.tensor_tensor(sc[:, h, :], sc[:, h, :], times[:, 0, :],
                                            ALU.mult).then_inc(counted_p, 1)
                nc.gpsimd.memset(k.accT2[:, :], 0.0)
                for h in range(H):
                    pool.wait_ge(inverted, h + 1)
                    nc.gpsimd.tensor_tensor(mx[:, h, :], mx[:, h, :], sc[:, h, :], ALU.mult).then_inc(a_ready, 1)

            @block.tensor
            def _(pe):
                for i, (a, o) in enumerate([(1, 0), (H, 0), (H, 2), (H, 0), (H, 2)]):
                    pe.wait_ge(edge_ready, i + 1)
                    pe.transpose(ps[0:a, 0:Q], edge[:, 0, 0:a], k.ident[0:Q, 0:Q])
                    pe.transpose(ps[0:a, P:P + Q], edge[:, 1, 0:a], k.ident[0:Q, 0:Q]
                                 ).then_inc(edgeT_ready, 1)
                    pe.wait_ge(carryT_ready, i + 1)
                    pe.transpose(ps[0:Q, 256:256 + a], carryT[0:a, o:o + Q], k.ident[0:a, 0:a]
                                 ).then_inc(carry_ready, 1)

            @block.scalar
            def _(act):
                for h in range(H):
                    act.wait_ge(m_ready, h + 1)
                    act.activation(sc[:, h, :], mx[:, h, :], ACT.Exp).then_inc(p_ready, 1)

            @block.vector
            def _(dve):
                step = Chain(dve, step_s)
                passes = [0]

                def scan(out, data, flags, op0, op1, nothing, back, heads=H, ready=None):
                    passes[0] += 1
                    way = slice(None, None, -1) if back else slice(None)

                    def run(initial):
                        for h in range(heads):
                            if ready:
                                dve.wait_ge(*ready[h])
                            last = dve.tensor_tensor_scan(out[:, h, way], flags[:, way], data[:, h, way],
                                                          initial(h), op0, op1)
                        step(last)
                    run(lambda h: nothing)
                    step(dve.tensor_copy(edge[:, 0, 0:heads], out[:, :, 0 if back else TILES - 1]))
                    step(dve.tensor_reduce(carry[:, 0:1], flags[:, :], AX, ALU.min))
                    dve.tensor_copy(edge[:, 1, 0:heads], carry[:, 0:1].to_broadcast([Q, heads])).then_inc(edge_ready, 1)
                    dve.wait_ge(edgeT_ready, passes[0])
                    step(dve.tensor_copy(edgeT[0:heads, 0, :], ps[0:heads, 0:Q]))
                    step(dve.tensor_copy(edgeT[0:heads, 1, :], ps[0:heads, P:P + Q]))
                    step(dve.memset(carryT[:, :], nothing))
                    dve.tensor_tensor_scan(carryT[0:heads, 1:Q + 1][:, way], edgeT[0:heads, 1, way], edgeT[0:heads, 0, way],
                                           nothing, op0, op1).then_inc(carryT_ready, 1)
                    dve.wait_ge(carry_ready, passes[0])
                    step(dve.tensor_copy(carry[:, 0:heads], ps[0:Q, 256:256 + heads]))
                    run(lambda h: carry[:, h:h + 1])

                dve.wait_ge(loaded, 64)
                step(dve.tensor_tensor(keep[:, :], ids[:, 1:TILES + 1], ids[:, 0:TILES], ALU.is_equal))
                step(dve.tensor_tensor(start[:, :], ids[:, 1:TILES + 1], ids[:, 0:TILES], ALU.not_equal))
                step(dve.tensor_scalar(start[:, :], start[:, :], FAR, None, ALU.mult))
                step(dve.tensor_tensor(end[:, :], ids[:, 1:TILES + 1], ids[:, 2:TILES + 2], ALU.not_equal))
                step(dve.tensor_scalar(end[:, :], end[:, :], FAR, None, ALU.mult))
                step(dve.tensor_tensor(loop[:, 0, :], ids[:, 1:TILES + 1], src[:, :], ALU.is_equal))
                scan(times, loop, keep, ALU.mult, ALU.add, 0.0, False, 1)
                step(dve.tensor_scalar(times[:, :, :], times[:, :, :], 1.0, None, ALU.is_equal))
                step(dve.tensor_tensor(times[:, :, :], times[:, :, :], loop[:, :, :], ALU.mult))
                step(dve.tensor_scalar(times[:, :, :], times[:, :, :], 1.0, None, ALU.add))
                scan(mx, sc, start, ALU.add, ALU.max, FAR, False)
                scan(mx, mx, end, ALU.add, ALU.max, FAR, True)
                for h in range(H):
                    dve.tensor_tensor(mx[:, h, :], sc[:, h, :], mx[:, h, :], ALU.subtract).then_inc(m_ready, 1)
                for h in range(BY_DVE):
                    dve.wait_ge(p_ready, h + 1)
                    dve.tensor_tensor(sc[:, h, :], sc[:, h, :], times[:, 0, :], ALU.mult).then_inc(counted, 1)
                scan(mx, sc, keep, ALU.mult, ALU.add, 0.0, False, ready=[
                    (counted, h + 1) if h < BY_DVE else (counted_p, h - BY_DVE + 1) for h in range(H)])
                scan(mx, mx, end, ALU.add, ALU.max, FAR, True)
                step(dve.tensor_scalar(mx[:, :, :], mx[:, :, :], 1e-16, float(H), ALU.add, ALU.mult))
                for h in range(H):
                    dve.reciprocal(mx[:, h, :], mx[:, h, :]).then_inc(inverted, 1)


def edge3b(nc, k):
    POOL_T, ACT_T = range(0, 5), range(5, 8)
    with Ctx(nc, "edge3b_") as c:
        raw = [c.sb(f"alpha_t{h}", [H * B, P]) for h in (0, 1)]
        al = [c.sb(f"alpha{h}", [P, H, B]) for h in (0, 1)]
        st = [c.sb(f"src_rows{h}", [P, B, D]) for h in (0, 1)]
        hp = [c.sb(f"weighted{h}", [P, B, H, D]) for h in (0, 1)]
        oh = [c.sb(f"onehot{h}", [P, B, P]) for h in (0, 1)]
        alp = [c.ps(f"alpha_ps{h}", [P, H * B]) for h in (0, 1)]
        sums = [c.ps(f"sums_ps{i}", [P, HP, P]) for i in range(4)]
        raw_ready = [c.sem(f"alpha_loaded{h}") for h in (0, 1)]
        st_ready = [c.sem(f"rows_loaded{h}") for h in (0, 1)]
        alp_ready, al_ready, hp_pool, hp_act, oh_ready, zeroed = c.sems(
            "alpha_in_psum", "alpha_ready", "weighted_by_gpsimd",
            "weighted_by_scalar", "onehot_ready", "accumulator_zeroed")
        summed = [c.sem(f"sums_in_psum{j}") for j in range(B)]
        added = [c.sem(f"added{j}") for j in range(B)]
        starts = [0, 0, 0, 0, 1, 1, 1, 2]

        def weigh(engine, h, tiles):
            a, b = tiles[0], tiles[-1] + 1
            rows = st[h][:, a:b, :].unsqueeze(2).to_broadcast([P, b - a, H, D])
            weights = al[h][:, :, a:b].rearrange("p h b -> p b h").unsqueeze(3).to_broadcast([P, b - a, H, D])
            return engine.tensor_tensor(hp[h][:, a:b, :, :], rows, weights, ALU.mult)

        with nc.Block() as block:
            @block.sync
            def _(sp):
                def body(t, last):
                    for h in (0, 1):
                        n = 2 * t + h + 1
                        at = bass.ds(2 * t + h, 1)
                        sp.wait_ge(alp_ready, n)
                        sp.dma_start(raw[h][:, :], k.scores_d[:, at].rearrange("h a b e -> h (a b) e")
                                     ).then_inc(raw_ready[h], 16)
                        for used in (hp_pool, hp_act):
                            sp.wait_ge(used, n)
                        sp.dma_start(st[h][:, :, :], k.kept[at].rearrange("a p (b d) -> (a p) b d", b=B)
                                     ).then_inc(st_ready[h], 16)
                pairs(sp, body)

            @block.gpsimd
            def _(pool):
                pool.sem_inc(hp_pool, 2)

                def body(t, last):
                    for h in (0, 1):
                        n = 2 * t + h + 1
                        pool.wait_ge(st_ready[h], 16 * (t + 1))
                        pool.wait_ge(summed[B - 1], n)
                        pool.wait_ge(al_ready, n)
                        weigh(nc.gpsimd, h, POOL_T).then_inc(hp_pool, 1)
                pairs(pool, body)

            @block.scalar
            def _(act):
                act.sem_inc(hp_act, 2)

                def body(t, last):
                    for h in (0, 1):
                        n = 2 * t + h + 1
                        act.wait_ge(st_ready[h], 16 * (t + 1))
                        act.wait_ge(summed[B - 1], n)
                        act.wait_ge(al_ready, n)
                        for j in ACT_T:
                            for a in range(H):
                                w = act.activation(hp[h][:, j, a, :], st[h][:, j, :], ACT.Copy,
                                                   scale=al[h][:, a, j:j + 1])
                        w.then_inc(hp_act, 1)
                pairs(act, body)

            @block.tensor
            def _(pe):
                pe.sem_inc(alp_ready, 2)
                pe.sem_inc(summed[B - 1], 2)

                def alphas(h, tt):
                    pe.wait_ge(raw_ready[h], 16 * tt)
                    pe.matmul(alp[h][:, :], raw[h][:, :], k.ident[0:H * B, 0:H * B], start=True,
                              stop=True).then_inc(alp_ready, 1)

                alphas(0, 1)

                def body(t, last):
                    for h in (0, 1):
                        n = 2 * t + h + 1
                        if not (last and h):
                            alphas(1 - h, t + 1 + h)
                        pe.wait_ge(oh_ready, n)
                        pe.wait_ge(hp_pool, n + 2)
                        for j in range(B):
                            if j == ACT_T[0]:
                                pe.wait_ge(hp_act, n + 2)
                            o = (j + 4) % B
                            pe.wait_ge(added[o], n + starts[o] - (j < 4))
                            for i in range(HP):
                                mm = pe.matmul(sums[j % 4][:, i, :],
                                               hp[h][:, j, 2 * i:2 * i + 2, :].rearrange("p a d -> p (a d)"),
                                               oh[h][:, j, :], start=True, stop=True)
                            mm.then_inc(summed[j], 1)
                pairs(pe, body)

            @block.vector
            def _(dve):
                for j in range(B):
                    if starts[j]:
                        dve.sem_inc(added[j], starts[j])
                acc3 = [a[:, :].rearrange("p (a w) -> p a w", a=HP) for a in (k.accT, k.accT2)]

                def prepare(n, h, t):
                    dve.wait_ge(alp_ready, n + 2)
                    dve.wait_ge(hp_pool, n)
                    dve.wait_ge(hp_act, n)
                    dve.tensor_copy(al[h][:, :, :].rearrange("p h b -> p (h b)"), alp[h][:, :]).then_inc(al_ready, 1)
                    onehot(dve, k, oh[h][:, :, :], t, h).then_inc(oh_ready, 1)

                prepare(1, 0, 0)
                dve.memset(k.accT[:, :], 0.0).then_inc(zeroed, 1)
                dve.wait_ge(zeroed, 1)

                def body(t, last):
                    for h in (0, 1):
                        n = 2 * t + h + 1
                        if not (last and h):
                            prepare(n + 1, 1 - h, t + h)
                        for j, base in enumerate(window_starts(nc, k, DVE, t, h)):
                            dve.wait_ge(summed[j], n + 2 if j == B - 1 else n)
                            dve.wait_ge(added[j - 2], n + starts[j - 2] - (j < 2))
                            acc = acc3[j % 2][:, :, bass.ds(base, P)]
                            dve.tensor_tensor(acc, acc, sums[j % 4][:, :, :], ALU.add).then_inc(added[j], 1)
                pairs(dve, body)


def build(nc, ins, out):
    k = Kept()
    dram = lambda name, shape: nc.dram_tensor(name, shape, F32).ap()
    k.t_wh = dram("table_wh", (NPAD, WH))
    k.t_h = dram("table_h", (NPAD, D))
    k.t_hn = dram("table_hn", (NPAD, HALF))
    k.t_h3 = dram("table_h3", (NPAD, D))
    k.kept = dram("kept_rows", (BATCHES, P, B * D))
    k.scores_d = dram("scores_by_head", (H, BATCHES, B, P))
    k.scatter_sums = [dram(f"scatter_sums{i}", (SROWS, D)) for i in range(TABLES)]
    k.src_run = ins["src_run"]
    k.src_t, k.dst_row, k.src_row, k.ea32, k.ea64, k.dst_seq = (
        ins["src_t"], ins["dst_row"], ins["src_row"], ins["ea32"], ins["ea64"], ins["dst_seq"])
    with Ctx(nc) as c:
        k.x = c.sb("x", [P, NB, D])
        k.h = c.sb("h", [P, NB, D])
        k.t1 = c.sb("t1", [P, NB, D])
        k.wh = c.sb("wh", [P, NB, WH])
        k.local = c.sb("local", [P, NB, D])
        k.accT = c.sb("accT", [P, HP * NPAD])
        k.src_i = c.sb("src_i", [P, TILES], I32)
        k.dst_i = c.sb("dst_i", [P, TILES], I32)
        k.src_f = c.sb("src_f", [P, TILES])
        k.dst_rel = c.sb("dst_rel", [P, TILES])
        k.win_node = c.sb("win_node", [P, TILES])
        k.src_sp = c.sb("src_sp", [P, TILES])
        k.weight = c.sb("weight", [P, TILES])
        k.ident = c.sb("ident", [P, P])
        k.row0 = c.sb("row0", [P, P])
        k.row1 = c.sb("row1", [P, P])
        k.col0 = c.sb("col0", [P, 1])
        k.col1 = c.sb("col1", [P, 1])
        k.spare_row = c.sb("spare_row", [P, 1])
        k.eps = c.sb("eps", [P, 1])
        k.center = c.sb("center", [D, D])
        k.W0 = c.sb("W0", [D + 1, D])
        widths = [2, 3, 1, 1, D, HALF, D, D, D, D, D, D, D, D, H * D]
        k.vectors = c.sb("vectors", [P, sum(widths)])
        (k.deg_coeff, k.coeff, k.scale, k.eps_gin, k.be, k.eb, k.gamma, k.beta, k.nlw, k.nlb,
         k.rlw_row, k.rlb_row, k.rb, k.bias3, k.att_row) = (
            k.vectors[:, sum(widths[:i]):sum(widths[:i + 1])] for i in range(len(widths)))
        k.coeff_d = c.sb("coeff_d", [P, 3])
        k.coeff_e = c.sb("coeff_e", [P, 3])
        k.coeff_s = c.sb("coeff_s", [P, 3])
        k.eps1 = c.sb("eps1", [P, 1])
        k.We = c.sb("We", [32, D])
        k.W1 = c.sb("W1", [D, D])
        k.b1 = c.sb("b1", [D, 1])
        k.W2 = c.sb("W2", [D + 1, D])
        k.nW = c.sb("nW", [D + 1, HALF])
        k.elw = c.sb("elw", [D, 1])
        k.elb = c.sb("elb", [D, 1])
        k.eW = c.sb("eW", [D, HALF])
        k.rlw = c.sb("rlw", [D, 1])
        k.rlb = c.sb("rlb", [D, 1])
        k.rW = c.sb("rW", [D + 1, D])
        k.Wz = c.sb("Wz", [P, H * ZH])
        k.att_z = c.sb("att_z", [P, H * ZH])
        k.Wl_h = c.sb("Wl_h", [P, HP, D])
        k.eWw = c.sb("eWw", [D, HALF])
        k.rWw = c.sb("rWw", [D, D])
        k.eR = c.sb("eR", [D, HALF + D])
        k.rR = c.sb("rR", [D, 2 * D])
        k.ec = c.sb("ec", [P, HALF])
        k.rc = c.sb("rc", [P, D])
        k.elb_col = c.sb("elb_col", [D, P])
        k.rlb_col = c.sb("rlb_col", [D, P])
        k.tables_cleared = c.sem("tables_cleared")
        k.hT = k.accT[0:D + 1, NPAD:2 * NPAD]
        k.acc = [k.accT[0:D + 1, 0:NPAD], k.accT[0:D + 1, 2 * NPAD:3 * NPAD]]
        k.t2 = k.accT[:, 2 * NPAD:2 * NPAD + NB * D].rearrange("p (b d) -> p b d", b=NB)
        setup(nc, k, ins)
        node0(nc, k)
        edge0(nc, k)
        node1(nc, k)
        edge1(nc, k)
        node2(nc, k)
        edge2(nc, k)
        node3(nc, k)
        edge3a(nc, k)
        with Ctx(nc, "layer3_") as layer:
            k.accT2 = layer.sb("accT2", [P, HP * NPAD])
            softmax(nc, k)
            edge3b(nc, k)
            node4(nc, k, out)


def kernel(x, src, dst, edge_attr_32, edge_attr_64, edge_weight, edge_weight_n2, L0_gnn_W, L0_gnn_b,
           L0_gnn_deg_coeff, L0_gnn_coeff_param, L0_gnn_scale_param, L1_gnn_We, L1_gnn_be, L1_gnn_W1,
           L1_gnn_b1, L1_gnn_W2, L1_gnn_b2, L1_gnn_eps_gin, L1_gnn_gamma, L1_gnn_beta,
           L2_gnn_node_ln_w, L2_gnn_node_ln_b, L2_gnn_node_W, L2_gnn_node_b, L2_gnn_edge_ln_w,
           L2_gnn_edge_ln_b, L2_gnn_edge_W, L2_gnn_edge_b, L2_gnn_red_ln_w, L2_gnn_red_ln_b,
           L2_gnn_red_W, L2_gnn_red_b, L3_gnn_W_l, L3_gnn_W_r, L3_gnn_att, L3_gnn_bias):
    import concourse.bacc as _bacc
    from concourse.bass_utils import run_bass_kernel_spmd as _run

    def padded(a, rows, fill=0):
        a = np.asarray(a)
        out = np.full((rows,) + a.shape[1:], fill, a.dtype)
        out[:a.shape[0]] = a
        return out

    def by_tile(a, fill=0):
        return np.ascontiguousarray(padded(a, TILES * P, fill).reshape(TILES, P).T)

    def by_batch_t(a):
        a = padded(a, TILES * P)
        return np.ascontiguousarray(a.reshape(BATCHES, ROWS, a.shape[1]).transpose(0, 2, 1))

    def row(a):
        return np.ascontiguousarray(np.asarray(a).reshape(1, -1))

    def vec(a):
        return np.ascontiguousarray(np.asarray(a).reshape(-1))

    def col(a):
        return np.ascontiguousarray(np.asarray(a).reshape(-1, 1))

    seq = np.full((BATCHES + 1) * ROWS, -2, np.int32)
    seq[0] = -1
    seq[1:1 + BATCHES * ROWS] = padded(dst, TILES * P, N)
    arrays = {
        "x": padded(x, NPAD),
        "src_t": by_tile(src), "dst_t": by_tile(dst, N),
        "src_row": padded(src, TILES * P).reshape(BATCHES, ROWS),
        "src_run": padded(src, TILES * P).reshape(P, TILES),
        "dst_row": padded(dst, TILES * P, N).reshape(BATCHES, ROWS), "dst_seq": seq,
        "w_t": by_tile(edge_weight), "w2_t": by_tile(edge_weight_n2),
        "ea32": by_batch_t(edge_attr_32), "ea64": by_batch_t(edge_attr_64),
        "W0": L0_gnn_W, "b0": row(L0_gnn_b),
        "We": L1_gnn_We, "W1": L1_gnn_W1, "b1": col(L1_gnn_b1),
        "W2": L1_gnn_W2, "b2": row(L1_gnn_b2),
        "nWT": np.asarray(L2_gnn_node_W).T, "nb": row(L2_gnn_node_b),
        "elw": col(L2_gnn_edge_ln_w), "elb": col(L2_gnn_edge_ln_b),
        "eWT": np.asarray(L2_gnn_edge_W).T,
        "rlw": col(L2_gnn_red_ln_w), "rlb": col(L2_gnn_red_ln_b),
        "rWT": np.asarray(L2_gnn_red_W).T, "rb": row(L2_gnn_red_b),
        "Wl": L3_gnn_W_l, "Wr": L3_gnn_W_r,
        "vectors": np.concatenate([vec(v) for v in (
            L0_gnn_deg_coeff, L0_gnn_coeff_param, L0_gnn_scale_param, L1_gnn_eps_gin, L1_gnn_be,
            L2_gnn_edge_b, L1_gnn_gamma, L1_gnn_beta, L2_gnn_node_ln_w, L2_gnn_node_ln_b,
            L2_gnn_red_ln_w, L2_gnn_red_ln_b, L2_gnn_red_b, L3_gnn_bias, L3_gnn_att)]),
    }
    nc = _bacc.Bacc("TRN2", target_bir_lowering=False, num_devices=1)
    arrays = {f"in_{name}": np.ascontiguousarray(a) for name, a in arrays.items()}
    ins = {name[3:]: nc.dram_tensor(name, a.shape, mybir.dt.from_np(a.dtype), kind="ExternalInput").ap()
           for name, a in arrays.items()}
    out = nc.dram_tensor("out", (N, D), F32, kind="ExternalOutput").ap()
    build(nc, ins, out)
    return _run(nc, [arrays], core_ids=[0]).results[0]["out"]
```
